# Optimizing a Trainium2 kernel written in Bass

```python
import numpy as np
import jax
import jax.numpy as jnp

def _softmax(x, axis=-1):
    return jax.nn.softmax(x, axis=axis)

def _gelu(x):
    return jax.nn.gelu(x, approximate=True)

def _silu(x):
    return jax.nn.silu(x)

def _sigmoid(x):
    return jax.nn.sigmoid(x)

def _layernorm(x, axis=-1, eps=1e-05):
    m = jnp.mean(x, axis=axis, keepdims=True)
    v = jnp.var(x, axis=axis, keepdims=True)
    return (x - m) / jnp.sqrt(v + eps)

def _scatter_add(tgt, idx, src, axis=0):
    return tgt.at[idx].add(src)

def _segment_sum(src, seg, n):
    return jax.ops.segment_sum(src, seg, n)
kernel_name = 'mk_seq_postln_d2_jaxref_r8_54e96c'

def setup_inputs(seed: int=0):
    np.random.seed(seed)
    _w = jnp.asarray

    def _L0_attn_setup():
        import jax, jax.numpy as jnp
        import numpy as np
        D_MODEL, N_HEADS, LATENT, ROPE = (512, 128, 64, 64)
        HEAD_DIM = D_MODEL // N_HEADS
        B, S = (2, 128)
        key = jax.random.key(seed)
        ks = jax.random.split(key, 9)

        def w(k, i, o):
            return jax.random.normal(k, (i, o), dtype=jnp.float32) * (1.0 / np.sqrt(i))
        return {'x': jax.random.normal(ks[0], (B, S, D_MODEL), dtype=jnp.float32), 'Wq_down': w(ks[1], D_MODEL, LATENT), 'Wq_up': w(ks[2], LATENT, N_HEADS * HEAD_DIM), 'Wq_rope': w(ks[3], D_MODEL, N_HEADS * ROPE), 'Wkv_down': w(ks[4], D_MODEL, LATENT), 'Wk_up': w(ks[5], LATENT, N_HEADS * HEAD_DIM), 'Wv_up': w(ks[6], LATENT, N_HEADS * HEAD_DIM), 'Wk_rope': w(ks[7], D_MODEL, ROPE), 'Wo': w(ks[8], N_HEADS * HEAD_DIM, D_MODEL)}
    _L0_attn_in = _L0_attn_setup()

    def _L0_ffn_setup():
        import jax, jax.numpy as jnp
        import numpy as np
        DIM = 512
        HID = 1376
        R = 16
        SCALING = 32.0 / 16.0

        def _lora_linear(x, w, a, b):
            base = jnp.einsum('bsd,od->bso', x, w)
            low = jnp.einsum('bsr,or->bso', jnp.einsum('bsd,rd->bsr', x, a), b)
            return base + low * SCALING
        key = jax.random.key(seed)
        ks = jax.random.split(key, 10)
        s_in = 1.0 / np.sqrt(DIM)
        s_hid = 1.0 / np.sqrt(HID)
        return {'x': jax.random.normal(ks[0], (4, 256, DIM), jnp.float32), 'w1': jax.random.normal(ks[1], (HID, DIM), jnp.float32) * s_in, 'w3': jax.random.normal(ks[2], (HID, DIM), jnp.float32) * s_in, 'w2': jax.random.normal(ks[3], (DIM, HID), jnp.float32) * s_hid, 'lora_A1': jax.random.normal(ks[4], (R, DIM), jnp.float32) * s_in, 'lora_B1': jax.random.normal(ks[5], (HID, R), jnp.float32) * 0.02, 'lora_A3': jax.random.normal(ks[6], (R, DIM), jnp.float32) * s_in, 'lora_B3': jax.random.normal(ks[7], (HID, R), jnp.float32) * 0.02, 'lora_A2': jax.random.normal(ks[8], (R, HID), jnp.float32) * s_hid, 'lora_B2': jax.random.normal(ks[9], (DIM, R), jnp.float32) * 0.02}
    _L0_ffn_in = _L0_ffn_setup()

    def _L1_attn_setup():
        import jax, jax.numpy as jnp
        import numpy as np
        NUM_HEADS = 32
        NUM_KV_HEADS = 8
        HEAD_DIM = 128
        ROPE_THETA = 10000.0

        def _rope_cos_sin(seq_len, head_dim, dtype):
            inv_freq = 1.0 / ROPE_THETA ** (jnp.arange(0, head_dim, 2, dtype=jnp.float32) / head_dim)
            t = jnp.arange(seq_len, dtype=jnp.float32)
            freqs = jnp.outer(t, inv_freq)
            emb = jnp.concatenate([freqs, freqs], axis=-1)
            return (jnp.cos(emb).astype(dtype), jnp.sin(emb).astype(dtype))

        def _rotate_half(x):
            h = x.shape[-1] // 2
            return jnp.concatenate([-x[..., h:], x[..., :h]], axis=-1)

        def _apply_rope(x, cos, sin):
            return x * cos[None, None] + _rotate_half(x) * sin[None, None]
        key = jax.random.key(seed)
        ks = jax.random.split(key, 5)
        B, S, H = (1, 256, 512)
        return {'hidden_states': jax.random.normal(ks[0], (B, S, H), dtype=jnp.float32), 'Wq': jax.random.normal(ks[1], (H, NUM_HEADS * HEAD_DIM), dtype=jnp.float32) * 0.02, 'Wk': jax.random.normal(ks[2], (H, NUM_KV_HEADS * HEAD_DIM), dtype=jnp.float32) * 0.02, 'Wv': jax.random.normal(ks[3], (H, NUM_KV_HEADS * HEAD_DIM), dtype=jnp.float32) * 0.02, 'Wo': jax.random.normal(ks[4], (NUM_HEADS * HEAD_DIM, H), dtype=jnp.float32) * 0.02}
    _L1_attn_in = _L1_attn_setup()

    def _L1_ffn_setup():
        import jax, jax.numpy as jnp
        import numpy as np
        IN_F = 512
        OUT_F = 512
        N_CLUSTERS = 64
        THRESHOLD = 0.01
        TEMPERATURE = 0.1
        BATCH, SEQ = (4, 256)
        key = jax.random.key(seed)
        k1, k2, k3, k4, k5 = jax.random.split(key, 5)
        s = 1.0 / np.sqrt(IN_F)
        return {'input': jax.random.normal(k1, (BATCH, SEQ, IN_F), dtype=jnp.float32), 'weight': jax.random.normal(k2, (OUT_F, IN_F), dtype=jnp.float32) * s, 'bias': jax.random.uniform(k3, (OUT_F,), dtype=jnp.float32, minval=-s, maxval=s), 'centroids': jax.random.normal(k4, (N_CLUSTERS, IN_F), dtype=jnp.float32) * s, 'assignments': jax.random.randint(k5, (OUT_F,), 0, N_CLUSTERS, dtype=jnp.int32)}
    _L1_ffn_in = _L1_ffn_setup()
    _d = {'L0_attn_x': _L0_attn_in['x'], 'L0_attn_Wq_down': _L0_attn_in['Wq_down'], 'L0_attn_Wq_up': _L0_attn_in['Wq_up'], 'L0_attn_Wq_rope': _L0_attn_in['Wq_rope'], 'L0_attn_Wkv_down': _L0_attn_in['Wkv_down'], 'L0_attn_Wk_up': _L0_attn_in['Wk_up'], 'L0_attn_Wv_up': _L0_attn_in['Wv_up'], 'L0_attn_Wk_rope': _L0_attn_in['Wk_rope'], 'L0_attn_Wo': _L0_attn_in['Wo'], 'L0_ffn_w1': _L0_ffn_in['w1'], 'L0_ffn_w3': _L0_ffn_in['w3'], 'L0_ffn_w2': _L0_ffn_in['w2'], 'L0_ffn_lora_A1': _L0_ffn_in['lora_A1'], 'L0_ffn_lora_B1': _L0_ffn_in['lora_B1'], 'L0_ffn_lora_A3': _L0_ffn_in['lora_A3'], 'L0_ffn_lora_B3': _L0_ffn_in['lora_B3'], 'L0_ffn_lora_A2': _L0_ffn_in['lora_A2'], 'L0_ffn_lora_B2': _L0_ffn_in['lora_B2'], 'L1_attn_Wq': _L1_attn_in['Wq'], 'L1_attn_Wk': _L1_attn_in['Wk'], 'L1_attn_Wv': _L1_attn_in['Wv'], 'L1_attn_Wo': _L1_attn_in['Wo'], 'L1_ffn_weight': _L1_ffn_in['weight'], 'L1_ffn_bias': _L1_ffn_in['bias'], 'L1_ffn_centroids': _L1_ffn_in['centroids'], 'L1_ffn_assignments': _L1_ffn_in['assignments']}
    _x0 = _d['L0_attn_x']
    _d['L0_attn_x'] = jax.random.normal(jax.random.fold_in(jax.random.key(seed), 1), (2, 512, 512), dtype=_x0.dtype)
    del _x0
    return _d

def reference(L0_attn_x, L0_attn_Wq_down, L0_attn_Wq_up, L0_attn_Wq_rope, L0_attn_Wkv_down, L0_attn_Wk_up, L0_attn_Wv_up, L0_attn_Wk_rope, L0_attn_Wo, L0_ffn_w1, L0_ffn_w3, L0_ffn_w2, L0_ffn_lora_A1, L0_ffn_lora_B1, L0_ffn_lora_A3, L0_ffn_lora_B3, L0_ffn_lora_A2, L0_ffn_lora_B2, L1_attn_Wq, L1_attn_Wk, L1_attn_Wv, L1_attn_Wo, L1_ffn_weight, L1_ffn_bias, L1_ffn_centroids, L1_ffn_assignments):

    def _L0_attn_ref(x, Wq_down, Wq_up, Wq_rope, Wkv_down, Wk_up, Wv_up, Wk_rope, Wo):
        import jax, jax.numpy as jnp
        import numpy as np
        D_MODEL, N_HEADS, LATENT, ROPE = (512, 128, 64, 64)
        HEAD_DIM = D_MODEL // N_HEADS
        B, S = (2, 128)
        b, s, _ = x.shape
        c_q = x @ Wq_down
        c_kv = x @ Wkv_down
        q_c = (c_q @ Wq_up).reshape(b, s, N_HEADS, HEAD_DIM)
        q_r = (x @ Wq_rope).reshape(b, s, N_HEADS, ROPE)
        k_c = (c_kv @ Wk_up).reshape(b, s, N_HEADS, HEAD_DIM)
        v_c = (c_kv @ Wv_up).reshape(b, s, N_HEADS, HEAD_DIM)
        k_r = x @ Wk_rope
        scale = jnp.asarray((HEAD_DIM + ROPE) ** 0.5, x.dtype)
        scores = (jnp.einsum('bqhd,bkhd->bhqk', q_c, k_c) + jnp.einsum('bqhd,bkd->bhqk', q_r, k_r)) / scale
        attn = jax.nn.softmax(scores, axis=-1)
        out = jnp.einsum('bhqk,bkhd->bqhd', attn, v_c)
        out = out.reshape(b, s, N_HEADS * HEAD_DIM)
        return out @ Wo

    def _L0_ffn_ref(x, w1, w3, w2, lora_A1, lora_B1, lora_A3, lora_B3, lora_A2, lora_B2):
        import jax, jax.numpy as jnp
        import numpy as np
        DIM = 512
        HID = 1376
        R = 16
        SCALING = 32.0 / 16.0

        def _lora_linear(x, w, a, b):
            base = jnp.einsum('bsd,od->bso', x, w)
            low = jnp.einsum('bsr,or->bso', jnp.einsum('bsd,rd->bsr', x, a), b)
            return base + low * SCALING
        h1 = _lora_linear(x, w1, lora_A1, lora_B1)
        h3 = _lora_linear(x, w3, lora_A3, lora_B3)
        g = jax.nn.silu(h1) * h3
        return _lora_linear(g, w2, lora_A2, lora_B2)

    def _L1_attn_ref(hidden_states, Wq, Wk, Wv, Wo):
        import jax, jax.numpy as jnp
        import numpy as np
        NUM_HEADS = 32
        NUM_KV_HEADS = 8
        HEAD_DIM = 128
        ROPE_THETA = 10000.0

        def _rope_cos_sin(seq_len, head_dim, dtype):
            inv_freq = 1.0 / ROPE_THETA ** (jnp.arange(0, head_dim, 2, dtype=jnp.float32) / head_dim)
            t = jnp.arange(seq_len, dtype=jnp.float32)
            freqs = jnp.outer(t, inv_freq)
            emb = jnp.concatenate([freqs, freqs], axis=-1)
            return (jnp.cos(emb).astype(dtype), jnp.sin(emb).astype(dtype))

        def _rotate_half(x):
            h = x.shape[-1] // 2
            return jnp.concatenate([-x[..., h:], x[..., :h]], axis=-1)

        def _apply_rope(x, cos, sin):
            return x * cos[None, None] + _rotate_half(x) * sin[None, None]
        B, S, H = hidden_states.shape
        nh, nkv, hd = (NUM_HEADS, NUM_KV_HEADS, HEAD_DIM)
        groups = nh // nkv
        q = (hidden_states @ Wq).reshape(B, S, nh, hd).transpose(0, 2, 1, 3)
        k = (hidden_states @ Wk).reshape(B, S, nkv, hd).transpose(0, 2, 1, 3)
        v = (hidden_states @ Wv).reshape(B, S, nkv, hd).transpose(0, 2, 1, 3)
        cos, sin = _rope_cos_sin(S, hd, q.dtype)
        q = _apply_rope(q, cos, sin)
        k = _apply_rope(k, cos, sin)
        k = jnp.repeat(k, groups, axis=1)
        v = jnp.repeat(v, groups, axis=1)
        scale = 1.0 / jnp.sqrt(jnp.asarray(hd, dtype=q.dtype))
        logits = jnp.einsum('bhqd,bhkd->bhqk', q, k) * scale
        causal = jnp.tril(jnp.ones((S, S), dtype=bool))
        neg = jnp.asarray(jnp.finfo(logits.dtype).min, dtype=logits.dtype)
        logits = jnp.where(causal[None, None], logits, neg)
        attn = jax.nn.softmax(logits.astype(jnp.float32), axis=-1).astype(q.dtype)
        out = jnp.einsum('bhqk,bhkd->bhqd', attn, v)
        out = out.transpose(0, 2, 1, 3).reshape(B, S, nh * hd)
        return out @ Wo

    def _L1_ffn_ref(input, weight, bias, centroids, assignments):
        import jax, jax.numpy as jnp
        import numpy as np
        IN_F = 512
        OUT_F = 512
        N_CLUSTERS = 64
        THRESHOLD = 0.01
        TEMPERATURE = 0.1
        BATCH, SEQ = (4, 256)
        shape = input.shape
        x = input.reshape(-1, shape[-1])
        dots = jax.nn.softmax(x @ centroids.T / TEMPERATURE, axis=-1)
        hits = dots > THRESHOLD
        query_sel = jnp.any(hits, axis=1)
        cluster_sel = jnp.any(hits, axis=0)
        row_sel = cluster_sel[assignments]
        dense = x @ weight.T + bias
        out = jnp.where(query_sel[:, None] & row_sel[None, :], dense, jnp.zeros((), dense.dtype))
        return out.reshape(*shape[:-1], -1)
    x = L0_attn_x
    x = _layernorm(x + _L0_attn_ref(x, L0_attn_Wq_down, L0_attn_Wq_up, L0_attn_Wq_rope, L0_attn_Wkv_down, L0_attn_Wk_up, L0_attn_Wv_up, L0_attn_Wk_rope, L0_attn_Wo), axis=-1)
    x = _layernorm(x + _L0_ffn_ref(x, L0_ffn_w1, L0_ffn_w3, L0_ffn_w2, L0_ffn_lora_A1, L0_ffn_lora_B1, L0_ffn_lora_A3, L0_ffn_lora_B3, L0_ffn_lora_A2, L0_ffn_lora_B2), axis=-1)
    x = _layernorm(x + _L1_attn_ref(x, L1_attn_Wq, L1_attn_Wk, L1_attn_Wv, L1_attn_Wo), axis=-1)
    x = _layernorm(x + _L1_ffn_ref(x, L1_ffn_weight, L1_ffn_bias, L1_ffn_centroids, L1_ffn_assignments), axis=-1)
    return x

_drawn_inputs = setup_inputs


def setup_inputs(seed=0):
    import zlib

    import numpy as np

    out = dict(_drawn_inputs(seed))
    spreads = {}
    factors = {'L1_attn_Wq': 4.867, 'L1_attn_Wk': 4.824, 'L1_ffn_bias': 3.352}
    for name, (base, spread) in spreads.items():
        noise = np.random.default_rng([zlib.crc32(name.encode()), seed]).standard_normal(out[name].shape)
        drawn = base * np.exp(spread * noise) if base else spread * noise
        out[name] = jnp.asarray(drawn.astype(out[name].dtype))
    for name, factor in factors.items():
        out[name] = (out[name] * factor).astype(out[name].dtype)
    return out
```

```python
from contextlib import ExitStack

import concourse.bass as bass
from concourse import mybir

F32 = mybir.dt.float32
F32R = mybir.dt.float32r
ACT = mybir.ActivationFunctionType
ALU = mybir.AluOpType
AXX = mybir.AxisListType.X

P = 128
T = 1024
NB = 2
S = T // NB
D = 512
DC = D // P
TT = T // P
ST = S // P

NH0 = 128
HD0 = D // NH0
LAT = 64
ROPE = 64
GH = 4
NG = NH0 // GH
CROWS = 3 * HD0
MROW = 96
KC0 = ROPE + CROWS


def latent_stage(nc, ctx, dram, sb):
    own = ExitStack()
    with own:
        def buf(name, shape, dt=F32):
            return own.enter_context(nc.sbuf_tensor(name, shape, dt))

        xT = buf("xT_sb", [P, DC, T])
        w_down = buf("w_down_sb", [P, DC, P])
        w_krope = buf("w_krope_sb", [P, DC, P])
        w_up = buf("w_up", [P, 2 * D])
        cT = buf("cT", [P, T])
        hi = {"q": sb["X"][:, :, :].bitcast(F32R).rearrange("p t n -> p (t n)").rearrange("p (m t) -> p m t", m=DC),
              "k": buf("content_hi_k", [P, DC, T], F32R)[:, :, :]}
        lo = {"q": sb["Q1"][:, :, :, :].rearrange("p b j s -> p (b j s)").rearrange("p (m t) -> p m t", m=DC),
              "k": buf("content_lo_k", [P, DC, T], F32R)[:, :, :]}
        zeros = buf("zeros", [P, 1, S])
        ones = buf("ones0", [P, S])
        bank = [own.enter_context(nc.psum_tensor(f"latent_ps{i}", [P, S], F32)) for i in range(8)]

        def sem(name):
            return ctx.enter_context(nc.semaphore(name))

        x_in = sem("x_in")
        w_in = sem("w_in")
        x_split = sem("x_split")
        ps_full = sem("latent_ps_full")
        act_done = sem("latent_act_done")
        dve_done = sem("latent_dve_done")
        rows_set = sem("rows_set")
        rope_set = sem("rope_set")
        zeros_set = sem("zeros_set")
        parts_out = sem("parts_out")
        jobs = [("c", 0, b) for b in range(NB)] + [("r", 0, b) for b in range(NB)]
        jobs += [(k, m, b) for k in "qk" for m in range(DC) for b in range(NB)]
        jobs += [("v", t, 0) for t in range(TT)]
        block = own.enter_context(nc.Block())

        @block.sync
        def _(sp):
            sp.dma_start(w_down[:, :, :], dram["w_down"].rearrange("(c p) n -> p c n", p=P)).then_inc(w_in, 16)
            sp.dma_start(xT[:, :, :], dram["xT"].rearrange("(c p) t -> p c t", p=P)).then_inc(x_in, 16)
            sp.dma_start(w_krope[:, :, :], dram["w_krope"].rearrange("(c p) n -> p c n", p=P)).then_inc(w_in, 16)
            sp.dma_start(w_up[0:LAT, 0:D], dram["w_qup"]).then_inc(w_in, 16)
            sp.dma_start(w_up[LAT:P, :], dram["w_kvup"]).then_inc(w_in, 16)
            for i, k in enumerate("qk"):
                planes = (hi[k], hi[k], lo[k]) if k == "q" else (hi[k], lo[k], hi[k])
                for m in range(DC):
                    n = 4 + (i * DC + m) * NB + NB
                    sp.wait_ge(act_done, n)
                    sp.wait_ge(dve_done, n)
                    for r, part in enumerate(planes):
                        heads = dram["content_" + k][m * 32:(m + 1) * 32, r * HD0:(r + 1) * HD0, :]
                        sp.dma_start(heads, part[:, m, :].bitcast(F32)).then_inc(parts_out, 16)
            sp.wait_ge(parts_out, 2 * DC * 3 * 16)

        @block.gpsimd
        def _(pool):
            pool.memset(zeros[:, :, :], 0.0).then_inc(rows_set, 1)
            pool.wait_ge(rows_set, 1)
            pool.memset(ones[MROW:MROW + 1, :], 1.0).then_inc(rows_set, 1)
            pool.wait_ge(rows_set, 2)
            pool.memset(sb["V_slot"][:, :, :, :, :], 0.0).then_inc(rows_set, 1)
            pool.wait_ge(rows_set, 3)
            pool.memset(sb["V_slot"][:, :, :, :, HD0:HD0 + 1], 1.0).then_inc(rows_set, 1)
            pool.memset(sb["ident"][:, :], 0.0).then_inc(rows_set, 1)
            pool.wait_ge(rows_set, 5)
            pool.affine_select(out=sb["ident"][:, :], in_=sb["ident"][:, :], compare_op=ALU.not_equal, fill=1.0,
                               base=0, pattern=[[-1, P]], channel_multiplier=1).then_inc(rows_set, 1)
            pool.wait_ge(rows_set, 6)

        @block.scalar
        def _(act):
            for n, (kind, m, b) in enumerate(jobs):
                act.wait_ge(ps_full, n + 1)
                src = bank[n % 8][:, :]
                if kind == "c":
                    out = cT[:, b * S:(b + 1) * S]
                elif kind == "r":
                    out = sb["K1"][:, b, :]
                elif kind == "v":
                    out = sb["V"][:, m, :]
                else:
                    out = hi[kind][:, m, b * S:(b + 1) * S]
                act.activation(out, src, ACT.Copy).then_inc(act_done, 1)
                if kind == "r":
                    for j in range(GH):
                        act.activation(sb["KX"][0:ROPE, b, j, :], bank[n % 8][0:ROPE, :], ACT.Copy).then_inc(rope_set, 1)
            act.wait_ge(act_done, len(jobs))
            act.wait_ge(rope_set, NB * GH)

        @block.vector
        def _(dve):
            dve.wait_ge(rows_set, 2)
            for b in range(NB):
                for tile in (sb["Q2"], sb["K2"]):
                    dve.tensor_copy(tile[ROPE:P, b, :, :], zeros[ROPE:P, :, :].broadcast_to([ROPE, GH, S]))\
                       .then_inc(zeros_set, 1)
            dve.wait_ge(zeros_set, 2 * NB)
            for b in range(NB):
                for j in range(GH):
                    dve.tensor_copy(sb["K2"][MROW:MROW + 1, b, j, :], ones[MROW:MROW + 1, :]).then_inc(zeros_set, 1)
            dve.wait_ge(x_in, 16)
            for c in range(DC):
                dve.tensor_copy(sb["xh"][:, c, :], xT[:, c, :]).then_inc(x_split, 1)
                dve.wait_ge(x_split, 2 * c + 1)
                dve.tensor_tensor(sb["xl"][:, c, :], xT[:, c, :], sb["xh"][:, c, :], ALU.subtract).then_inc(x_split, 1)
            dve.wait_ge(x_split, 2 * DC)
            for n, (kind, m, b) in enumerate(jobs):
                if kind == "v":
                    break
                dve.wait_ge(act_done, n + 1)
                src = bank[n % 8]
                if kind == "c":
                    continue
                if kind == "r":
                    dve.wait_ge(rope_set, GH * (b + 1))
                    for j in range(GH):
                        ins = dve.tensor_tensor(sb["K2"][0:ROPE, b, j, :], src[0:ROPE, :], sb["K1"][0:ROPE, b, :],
                                                ALU.subtract)
                    ins.then_inc(dve_done, 3 if b == 0 else 1)
                else:
                    dve.tensor_tensor(lo[kind][:, m, b * S:(b + 1) * S], src[:, :], hi[kind][:, m, b * S:(b + 1) * S],
                                      ALU.subtract).then_inc(dve_done, 1)
            dve.wait_ge(dve_done, 4 + 4 * DC)
            dve.wait_ge(zeros_set, (2 + GH) * NB)

        @block.tensor
        def _(pe):
            pe.wait_ge(w_in, 64)
            pe.wait_ge(x_in, 16)
            for n, (kind, m, b) in enumerate(jobs):
                if n >= 8:
                    pe.wait_ge(act_done, n - 7)
                    if n - 8 >= 2 and jobs[n - 8][0] != "v":
                        pe.wait_ge(dve_done, n - 7)
                out = bank[n % 8][:, :]
                if kind in "cr":
                    w = w_down if kind == "c" else w_krope
                    for c in range(DC):
                        last = pe.matmul(out, w[:, c, :], xT[:, c, b * S:(b + 1) * S], start=c == 0, stop=c == DC - 1)
                else:
                    if n == 4:
                        pe.wait_ge(act_done, 2)
                    if kind == "q":
                        last = pe.matmul(out, w_up[0:LAT, m * P:(m + 1) * P], cT[0:LAT, b * S:(b + 1) * S],
                                         start=True, stop=True)
                    elif kind == "k":
                        last = pe.matmul(out, w_up[LAT:P, m * P:(m + 1) * P], cT[LAT:P, b * S:(b + 1) * S],
                                         start=True, stop=True)
                    else:
                        last = pe.matmul(out, cT[LAT:P, m * P:(m + 1) * P], w_up[LAT:P, D:2 * D],
                                         start=True, stop=True)
                last.then_inc(ps_full, 1)


def mla_stage(nc, ctx, dram, sb, groups=NG):
    SCALE = float((HD0 + ROPE) ** -0.5)
    own = ExitStack()
    with own:
        def buf(name, shape, dt=F32):
            return own.enter_context(nc.sbuf_tensor(name, shape, dt))

        def sem(name):
            return ctx.enter_context(nc.semaphore(name))

        w_raw = buf("w_raw", [P, DC, 2, P])
        w_hi = buf("w_hi", [P, DC, 2, P], F32R)
        w_lo = buf("w_lo", [P, DC, 2, P], F32R)
        Q1 = sb["Q1"]
        Q2 = sb["Q2"]
        K1 = sb["K1"]
        K2 = sb["K2"]
        KX = sb["KX"]
        probs = buf("probs", [P, GH, ST, S])
        row_max = buf("row_max", [P, ST, GH])
        mrow = sb["mrow"]
        oT = buf("oT", [P, S])
        recip = buf("recip", [P, ST, GH, 1])
        V_slot, V, O, ident = sb["V_slot"], sb["V"], sb["X"], sb["ident"]
        ps_score = [own.enter_context(nc.psum_tensor(f"ps_score{i}", [P, 2, S], F32)) for i in range(2)]
        ps_max = [own.enter_context(nc.psum_tensor(f"ps_max{i}", [P, S], F32)) for i in range(2)]
        ps_x = own.enter_context(nc.psum_tensor("ps_x", [P, S], F32))
        ps_o = own.enter_context(nc.psum_tensor("ps_o", [P, S], F32))

        w_in = sem("wq_in")
        w_step = sem("wq_step")
        w_split = sem("wq_split")
        q_made = sem("q_made")
        q_high = sem("q_high")
        q_low = sem("q_low")
        q_copied = sem("q_copied")
        content_in = [sem(f"content_in{b}") for b in range(NB)]
        max_made = sem("max_made")
        max_taken = sem("max_taken")
        max_turned = sem("max_turned")
        row_made = sem("row_made")
        row_in = sem("row_in")
        scored = sem("scored")
        exped = sem("exped")
        v_in = sem("v_in")
        pv_made = sem("pv_made")
        o_taken = sem("o_taken")
        o_turned = sem("o_turned")
        r_made = sem("r_made")
        o_made = sem("o_made")
        gate_sp, gate_pool = sem("gate_sp"), sem("gate_pool")
        ORDER = [("m", 0, 0), ("m", 0, 1), ("s", 0, 0), ("m", 0, 2), ("o", 0, 0), ("s", 0, 1), ("m", 0, 3),
                 ("s", 1, 0), ("m", 1, 0), ("q", 0, 0), ("m", 1, 1), ("q", 1, 0), ("m", 1, 2), ("q", 2, 0),
                 ("m", 1, 3), ("s", 1, 1), ("s", 2, 0), ("m", 2, 0), ("s", 2, 1), ("m", 2, 1), ("m", 2, 2),
                 ("s", 3, 0), ("m", 2, 3), ("m", 3, 0), ("s", 3, 1), ("m", 3, 1), ("m", 3, 2), ("m", 3, 3)]
        w_view = dram["w_qrope"].rearrange("(c p) n -> p c n", p=P)
        block = own.enter_context(nc.Block())

        def run(engine, body):
            body(0, True, groups == 1)
            if groups > 2:
                with engine.Fori(1, groups - 1) as g:
                    body(g, False, False)
            if groups > 1:
                body(groups - 1, False, True)

        @block.sync
        def _(sp):
            def load_w(g):
                sp.dma_start(w_raw[:, :, :, :].rearrange("p c a n -> p c (a n)"),
                             w_view[:, :, bass.ds(g * 2 * P, 2 * P)]).then_inc(w_in, 16)

            def content(g, b):
                for tile, src in ((Q2, "content_q"), (K2, "content_k"), (KX, "content_k")):
                    rows = dram[src][bass.ds(g * GH, GH), :, b * S:(b + 1) * S].rearrange("h r t -> r h t")
                    sp.dma_start(tile[ROPE:KC0, b, :, :].bitcast(F32), rows).then_inc(content_in[b], 16)

            def copy_q(n, b):
                sp.wait_ge(q_high, 2 * n + 2)
                sp.dma_start(Q1[0:ROPE, b, :, :].bitcast(F32), Q2[0:ROPE, b, :, :].bitcast(F32)).then_inc(q_copied, 16)

            load_w(0)
            content(0, 0)
            content(0, 1)
            copy_q(0, 0)

            def body(g, first, last):
                for b in range(NB):
                    n = 2 * g + b
                    sp.wait_ge(row_made, n + 1)
                    sp.dma_start(Q2[MROW:MROW + 1, b, :, :].bitcast(F32), mrow[0:GH, :].bitcast(F32)).then_inc(row_in, 16)
                    if b == 0 and not last:
                        sp.wait_ge(w_split, 2 * g + 2)
                        sp.sem_inc(gate_sp, 1)
                        load_w(g + 1)
                    if not (last and b == 1):
                        copy_q(n + 1, 1 - b)
                    if not last:
                        sp.wait_ge(scored, 8 * (n + 1))
                        sp.sem_inc(gate_sp, 1)
                        content(g + 1, b)

            run(sp, body)

        @block.gpsimd
        def _(pool):
            def split_w(g, pair, first):
                if pair == 0:
                    pool.wait_ge(w_in, 16 * (g + 1))
                if not first:
                    pool.wait_ge(q_made, 4 * g - 1 + pair)
                    pool.sem_inc(gate_pool, 1)
                pool.tensor_copy(w_hi[:, :, pair, :], w_raw[:, :, pair, :]).then_inc(w_step, 1)
                pool.wait_ge(w_step, 2 * g + pair + 1)
                pool.tensor_tensor(w_lo[:, :, pair, :], w_raw[:, :, pair, :], w_hi[:, :, pair, :],
                                   ALU.subtract).then_inc(w_split, 1)

            def values(g, b, n, first):
                if not first:
                    pool.wait_ge(pv_made, n - 1)
                    pool.sem_inc(gate_pool, 1)
                pool.tensor_copy(V_slot[:, b, :, :, 0:HD0],
                                 V[:, b * ST:(b + 1) * ST, bass.ds(g * GH * HD0, GH * HD0)].rearrange(
                                     "p t (h d) -> p t h d", h=GH)).then_inc(v_in, 1)

            split_w(0, 0, True)
            split_w(0, 1, True)

            def body(g, first, last):
                values(g, 0, 2 * g, first)
                if not last:
                    split_w(g + 1, 0, False)
                values(g, 1, 2 * g + 1, first)
                if not last:
                    split_w(g + 1, 1, False)

            run(pool, body)

        @block.scalar
        def _(act):
            def high(n, b, pair):
                act.wait_ge(q_made, 2 * n + pair + 1)
                for k in range(2):
                    ins = act.activation(Q2[0:ROPE, b, 2 * pair + k, :], ps_x[k * ROPE:(k + 1) * ROPE, :], ACT.Copy)
                ins.then_inc(q_high, 1)

            def exp(n, j, half):
                act.wait_ge(scored, 8 * n + 2 * j + half + 1)
                act.activation(probs[:, j, 2 * half:2 * half + 2, :], ps_score[half][:, :, :], ACT.Exp,
                               scale=SCALE).then_inc(exped, 1)

            def take_o(n):
                act.wait_ge(pv_made, n + 1)
                act.activation(oT[:, :], ps_o[:, :], ACT.Copy).then_inc(o_taken, 1)

            for pair in range(2):
                high(0, 0, pair)

            def body(g, first, last):
                for b in range(NB):
                    n = 2 * g + b
                    more = not (last and b == 1)
                    if more:
                        high(n + 1, 1 - b, 0)
                    act.wait_ge(max_turned, n + 1)
                    if not (first and b == 0):
                        act.wait_ge(row_in, 16 * n)
                    act.activation(mrow[0:GH, :], ps_max[0][0:GH, :], ACT.Copy, scale=-1.0).then_inc(row_made, 1)
                    if not (first and b == 0):
                        take_o(n - 1)
                    for kind, j, k in ORDER:
                        if kind == "s":
                            exp(n, j, k)
                        if kind == "q" and j == 2 and more:
                            high(n + 1, 1 - b, 1)

            run(act, body)
            take_o(2 * groups - 1)

        @block.vector
        def _(dve):
            def low(n, b, pair):
                dve.wait_ge(q_high, 2 * n + pair + 1)
                for k in range(2):
                    ins = dve.tensor_tensor(Q1[ROPE:P, b, 2 * pair + k, :], ps_x[k * ROPE:(k + 1) * ROPE, :],
                                            Q2[0:ROPE, b, 2 * pair + k, :], ALU.subtract)
                ins.then_inc(q_low, 1)

            def take_max(n, j, t):
                dve.wait_ge(max_made, 16 * n + 4 * j + t + 1)
                dve.tensor_reduce(row_max[:, t, j:j + 1], ps_max[t % 2][:, :], axis=AXX, op=ALU.max)\
                   .then_inc(max_taken, 1)

            def normalise(g, b, n):
                dve.wait_ge(o_turned, n + 1)
                outs = ps_x[:, :].rearrange("p (t h m) -> p t h m", t=ST, h=GH)
                dve.reciprocal(recip[:, :, :, :], outs[:, :, :, HD0:HD0 + 1]).then_inc(r_made, 1)
                dve.wait_ge(r_made, n + 1)
                for t in range(ST):
                    ins = dve.tensor_tensor(O[:, b * ST + t, bass.ds(g * GH * HD0, GH * HD0)].rearrange(
                        "p (h d) -> p h d", h=GH), outs[:, t, :, 0:HD0],
                        recip[:, t, :, :].broadcast_to([P, GH, HD0]), ALU.mult)
                ins.then_inc(o_made, 1)

            for pair in range(2):
                low(0, 0, pair)
                for j in range(2 * pair, 2 * pair + 2):
                    for t in range(ST):
                        take_max(0, j, t)

            def body(g, first, last):
                for b in range(NB):
                    n = 2 * g + b
                    more = not (last and b == 1)
                    if more:
                        low(n + 1, 1 - b, 0)
                    for kind, j, t in ORDER:
                        if kind == "m" and more:
                            take_max(n + 1, j, t)
                            if (j, t) == (1, 3):
                                low(n + 1, 1 - b, 1)
                        if kind == "o" and not (first and b == 0):
                            normalise(g - 1 + b, 1 - b, n - 1)

            run(dve, body)
            normalise(groups - 1, 1, 2 * groups - 1)
            dve.wait_ge(o_made, 2 * groups)

        @block.tensor
        def _(pe):
            def queries(g, b, n, pair, third):
                if b == 0 and third == 0:
                    pe.wait_ge(w_split, 2 * g + pair + 1)
                w, x = ((w_hi, "xh"), (w_lo, "xh"), (w_hi, "xl"))[third]
                for c in range(DC):
                    last = pe.matmul(ps_x[:, :], w[:, c, pair, :], sb[x][:, c, b * S:(b + 1) * S],
                                     start=third == c == 0, stop=third == 2 and c == DC - 1)
                if third == 2:
                    last.then_inc(q_made, 1)

            def max_scores(g, b, n, j, t, wait_free=True):
                if j % 2 == 0 and t == 0:
                    pe.wait_ge(q_high, 2 * n + j // 2 + 1)
                if j == 0 and t == 0:
                    pe.wait_ge(content_in[b], 48 * (g + 1))
                    if wait_free:
                        pe.wait_ge(row_made, n)
                if wait_free:
                    pe.wait_ge(max_taken, 16 * n + 4 * j + t - 1)
                pe.matmul(ps_max[t % 2][:, :], Q2[0:KC0, b, j, t * P:(t + 1) * P], KX[0:KC0, b, j, :],
                          start=True, stop=True).then_inc(max_made, 1)

            def scores(n, b, j, half, wait_free=True):
                if j == half == 0:
                    pe.wait_ge(q_low, 2 * n + 2)
                    pe.wait_ge(q_copied, 16 * (n + 1))
                    pe.wait_ge(row_in, 16 * (n + 1))
                if wait_free:
                    pe.wait_ge(exped, 8 * n + 2 * j + half - 1)
                for k in range(2):
                    t = 2 * half + k
                    pe.matmul(ps_score[half][:, k, :], K1[:, b, t * P:(t + 1) * P], Q1[:, b, j, :],
                              start=True, stop=False)
                    last = pe.matmul(ps_score[half][:, k, :], K2[0:MROW + 1, b, j, t * P:(t + 1) * P],
                                     Q2[0:MROW + 1, b, j, :], start=False, stop=True)
                last.then_inc(scored, 1)

            def outputs(n, b):
                pe.wait_ge(exped, 8 * (n + 1))
                pe.wait_ge(v_in, n + 1)
                for t in range(ST):
                    for j in range(GH):
                        last = pe.matmul(ps_o[32 * j:32 * (j + 1), :], V_slot[:, b, t, j, :], probs[:, j, t, :],
                                         start=t == 0, stop=t == ST - 1)
                last.then_inc(pv_made, 1)

            def turn_o(n):
                pe.wait_ge(o_taken, n + 1)
                for t in range(ST):
                    last = pe.transpose(ps_x[:, t * P:(t + 1) * P], oT[:, t * P:(t + 1) * P], ident[:, :])
                last.then_inc(o_turned, 1)

            for pair in range(2):
                if pair:
                    pe.wait_ge(q_low, 1)
                for third in range(3):
                    queries(0, 0, 0, pair, third)
            for j in range(GH):
                for t in range(ST):
                    max_scores(0, 0, 0, j, t, wait_free=4 * j + t >= 2)

            def body(g, first, last):
                for b in range(NB):
                    n = 2 * g + b
                    more = not (last and b == 1)
                    before = not (first and b == 0)
                    if more:
                        pe.wait_ge(q_low, 2 * n + 2)
                        for third in range(3):
                            queries(g + b, 1 - b, n + 1, 0, third)
                    pe.wait_ge(max_taken, 16 * (n + 1))
                    for t in range(ST):
                        ins = pe.transpose(ps_max[0][0:GH, t * P:(t + 1) * P], row_max[:, t, :], ident[:, :])
                    ins.then_inc(max_turned, 1)
                    if before:
                        outputs(n - 1, 1 - b)
                    for kind, j, k in ORDER:
                        if kind == "s":
                            scores(n, b, j, k, wait_free=before or j > 0)
                        if kind == "m" and more:
                            max_scores(g + b, 1 - b, n + 1, j, k)
                        if kind == "o" and before:
                            if more:
                                pe.wait_ge(q_low, 2 * n + 3)
                            turn_o(n - 1)
                        if kind == "q" and more:
                            if j == 0 and before:
                                pe.wait_ge(o_made, n)
                            elif j == 0:
                                pe.wait_ge(q_low, 2 * n + 3)
                            queries(g + b, 1 - b, n + 1, 1, j)

            run(pe, body)
            outputs(2 * groups - 1, 1)
            pe.wait_ge(o_made, 2 * groups - 1)
            turn_o(2 * groups - 1)

EPS = 1e-5
HID = 1376
HT = 11
HP = HT * P
RANK = 16
LORA_SCALE = 2.0

NKV = 8
GQ = 4
NCL = 64
THRESHOLD = 0.01
TEMPERATURE = 0.1


def merge_heads_stage(nc, ctx, dram, sb):
    own = ExitStack()
    with own:
        def sem(name):
            return ctx.enter_context(nc.semaphore(name))

        X, ident = sb["X"], sb["ident"]
        x = own.enter_context(nc.sbuf_tensor("x_sb", [P, TT, D], F32))
        wo = own.enter_context(nc.sbuf_tensor("wo0_sb", [P, DC, D], F32))
        oT = own.enter_context(nc.sbuf_tensor("oT0", [P, 2, DC, P], F32))
        turned = [own.enter_context(nc.psum_tensor(f"turned{i}", [P, DC, P], F32)) for i in range(2)]
        made = [own.enter_context(nc.psum_tensor(f"made{i}", [P, D], F32)) for i in range(2)]
        loaded = sem("wo0_in")
        o_turned = sem("o0_turned")
        o_taken = sem("o0_taken")
        y_made = sem("y0_made")
        y_taken = sem("y0_taken")
        block = own.enter_context(nc.Block())

        @block.sync
        def _(sp):
            sp.dma_start(wo[:, :, :], dram["wo0"].rearrange("(c p) n -> p c n", p=P)).then_inc(loaded, 16)
            sp.dma_start(x[:, :, :], dram["x"].rearrange("(t p) n -> p t n", p=P)).then_inc(loaded, 16)

        @block.tensor
        def _(pe):
            def turn(t):
                if t >= 2:
                    pe.wait_ge(o_taken, t - 1)
                for c in range(DC):
                    last = pe.transpose(turned[t % 2][:, c, :], X[:, t, c * P:(c + 1) * P], ident[:, :])
                last.then_inc(o_turned, 1)

            turn(0)
            pe.wait_ge(loaded, 32)
            for t in range(TT):
                if t + 1 < TT:
                    turn(t + 1)
                pe.wait_ge(o_taken, t + 1)
                if t >= 2:
                    pe.wait_ge(y_taken, t - 1)
                for c in range(DC):
                    last = pe.matmul(made[t % 2][:, :], oT[:, t % 2, c, :], wo[:, c, :], start=c == 0, stop=c == DC - 1)
                last.then_inc(y_made, 1)

        @block.scalar
        def _(act):
            for t in range(TT):
                act.wait_ge(o_turned, t + 1)
                if t >= 2:
                    act.wait_ge(y_made, t - 1)
                act.activation(oT[:, t % 2, :, :], turned[t % 2][:, :, :], ACT.Copy).then_inc(o_taken, 1)

        @block.vector
        def _(dve):
            dve.wait_ge(loaded, 32)
            for t in range(TT):
                dve.wait_ge(y_made, t + 1)
                dve.tensor_tensor(X[:, t, :], made[t % 2][:, :], x[:, t, :], ALU.add).then_inc(y_taken, 1)
            dve.wait_ge(y_taken, TT)


def norm_stage(nc, ctx, name, sb, out=None):
    own = ExitStack()
    with own:
        def sem(s):
            return ctx.enter_context(nc.semaphore(name + s))

        X, ident = sb["X"], sb["ident"]
        stats = own.enter_context(nc.sbuf_tensor(name + "stats", [P, TT, 6], F32))
        moments = own.enter_context(nc.sbuf_tensor(name + "moments", [P, TT, 2], F32))
        dev = own.enter_context(nc.sbuf_tensor(name + "dev", [P, TT], F32))
        eps = own.enter_context(nc.sbuf_tensor(name + "eps", [P, 1], F32))
        turned = [own.enter_context(nc.psum_tensor(f"{name}turned{i}", [P, DC, P], F32)) for i in range(4)]
        eps_set = sem("eps_set")
        counted = sem("counted")
        mean_var = sem("mean_var")
        rooted = sem("rooted")
        inverse = sem("inverse")
        normed = sem("normed")
        x_turned = sem("x_turned")
        high = sem("high")
        low = sem("low")
        stored = sem("stored")
        block = own.enter_context(nc.Block())

        @block.vector
        def _(dve):
            dve.memset(eps[:, :], EPS).then_inc(eps_set, 1)
            for t in range(TT):
                dve.bn_stats(stats[:, t, :], X[:, t, :]).then_inc(counted, 1)
            for t in range(TT):
                dve.wait_ge(counted, t + 1)
                dve.bn_aggr(moments[:, t, :], stats[:, t, :]).then_inc(mean_var, 1)
            dve.wait_ge(rooted, 1)
            dve.reciprocal(dev[:, :], dev[:, :]).then_inc(inverse, 1)
            dve.wait_ge(inverse, 1)
            for t in range(TT):
                dve.tensor_scalar(X[:, t, :], X[:, t, :], moments[:, t, 0:1], dev[:, t:t + 1],
                                  ALU.subtract, ALU.mult).then_inc(normed, 1)
            if out is None:
                for t in range(TT):
                    dve.wait_ge(high, t + 1)
                    dve.tensor_tensor(sb["xl"][:, :, t * P:(t + 1) * P], turned[t % 4][:, :, :],
                                      sb["xh"][:, :, t * P:(t + 1) * P], ALU.subtract).then_inc(low, 1)
                dve.wait_ge(low, TT)

        @block.scalar
        def _(act):
            act.wait_ge(eps_set, 1)
            act.wait_ge(mean_var, TT)
            act.activation(dev[:, :], moments[:, :, 1], ACT.Sqrt, bias=eps[:, 0:1]).then_inc(rooted, 1)
            if out is None:
                for t in range(TT):
                    act.wait_ge(x_turned, t + 1)
                    act.activation(sb["xh"][:, :, t * P:(t + 1) * P], turned[t % 4][:, :, :], ACT.Copy)\
                       .then_inc(high, 1)

        @block.tensor
        def _(pe):
            if out is None:
                for t in range(TT):
                    pe.wait_ge(normed, t + 1)
                    if t >= 4:
                        pe.wait_ge(low, t - 3)
                    for c in range(DC):
                        last = pe.transpose(turned[t % 4][:, c, :], X[:, t, c * P:(c + 1) * P], ident[:, :])
                    last.then_inc(x_turned, 1)

        @block.sync
        def _(sp):
            if out is not None:
                rows = out.rearrange("(t p) n -> p t n", p=P)
                for t in range(TT):
                    sp.wait_ge(normed, t + 1)
                    sp.dma_start(rows[:, t, :], X[:, t, :]).then_inc(stored, 16)
                sp.wait_ge(stored, 16 * TT)


def swiglu_stage(nc, ctx, dram, sb):
    own = ExitStack()
    with own:
        def buf(name, shape, dt=F32):
            return own.enter_context(nc.sbuf_tensor(name, shape, dt))

        def sem(name):
            return ctx.enter_context(nc.semaphore("ffn_" + name))

        X, xh, xl = sb["X"], sb["xh"], sb["xl"]
        w_hi = buf("w13_hi", [P, 2, DC, HP], F32R)
        w_lo = buf("w13_lo", [P, 2, DC, HP], F32R)
        w2 = buf("w2_sb", [P, HT, D])
        raw = buf("w13_raw", [P, 2, HP])
        lora_a = buf("lora_a", [RANK, 2, D])
        lora_b = buf("lora_b", [RANK, 2, HP])
        a2 = buf("lora_a2", [RANK, HP])
        b2 = buf("lora_b2", [RANK, D])
        gate = buf("gate", [P, 2, S])
        g = buf("gated", [P, 2, S])
        banks = [own.enter_context(nc.psum_tensor(f"ffn_ps{i}", [P, S], F32)) for i in range(8)]
        lora_in = sem("lora_in")
        w2_in = sem("w2_in")
        raw_in = [sem(f"raw_in{i}") for i in range(2)]
        delta = sem("delta")
        folded = sem("folded")
        w_high = sem("w_high")
        w_low = sem("w_low")
        hidden = sem("hidden")
        gated = sem("gated")
        g_made = sem("g_made")
        down = sem("down")
        taken = sem("taken")
        CUTS = [(0, 512), (512, 512), (1024, HP - 1024)]
        NC = len(CUTS)
        ONE = 1
        block = own.enter_context(nc.Block())
        steps = [(i, c) for i in range(2) for c in range(DC)]

        @block.sync
        def _(sp):
            sp.dma_start(lora_a[:, :, :], dram["lora_a13"].rearrange("i r d -> r i d")).then_inc(lora_in, 16)
            sp.dma_start(lora_b[:, :, :], dram["lora_b13"].rearrange("i r h -> r i h")).then_inc(lora_in, 16)
            sp.dma_start(a2[:, :], dram["lora_a2"]).then_inc(lora_in, 16)
            sp.dma_start(b2[:, :], dram["lora_b2"]).then_inc(lora_in, 16)
            for s, (i, c) in enumerate(steps):
                if s >= 2:
                    sp.wait_ge(w_low, s - 1)
                sp.dma_start(raw[:, s % 2, :], dram["w13"][i, c * P:(c + 1) * P, :]).then_inc(raw_in[s % 2], 16)
                if s == 1:
                    sp.dma_start(w2[:, :, :], dram["w2"].rearrange("(m p) n -> p m n", p=P)).then_inc(w2_in, 16)

        @block.scalar
        def _(act):
            for s, (i, c) in enumerate(steps):
                act.wait_ge(folded, NC * (s + 1))
                act.activation(w_hi[:, i, c, :], raw[:, s % 2, :], ACT.Copy).then_inc(w_high, 1)
            with act.Fori(0, NB) as half:
                for m in range(HT):
                    act.wait_ge(hidden, half * HT + m + 1)
                    if m >= 2:
                        act.wait_ge(g_made, ONE + half * HT + m - 1)
                    else:
                        act.wait_ge(g_made, ONE + half * HT)
                    act.activation(gate[:, m % 2, :], banks[4 + m % 2][:, :], ACT.Silu).then_inc(gated, 1)

        @block.vector
        def _(dve):
            dve.sem_inc(g_made, ONE)
            dve.sem_inc(taken, ONE)
            for s, (i, c) in enumerate(steps):
                dve.wait_ge(raw_in[s % 2], 16 * (s // 2 + 1))
                for k, (at, n) in enumerate(CUTS):
                    j = NC * s + k
                    dve.wait_ge(delta, j + 1)
                    dve.scalar_tensor_tensor(out=raw[:, s % 2, at:at + n], in0=banks[j % 8][:, 0:n], scalar=LORA_SCALE,
                                             in1=raw[:, s % 2, at:at + n], op0=ALU.mult, op1=ALU.add)\
                       .then_inc(folded, 1)
                dve.wait_ge(w_high, s + 1)
                dve.tensor_tensor(w_lo[:, i, c, :], raw[:, s % 2, :], w_hi[:, i, c, :], ALU.subtract).then_inc(w_low, 1)
            dve.wait_ge(w2_in, 16)
            for m in range(HT):
                j = NC * len(steps) + m
                dve.wait_ge(delta, j + 1)
                dve.scalar_tensor_tensor(out=w2[:, m, :], in0=banks[j % 8][:, :], scalar=LORA_SCALE,
                                         in1=w2[:, m, :], op0=ALU.mult, op1=ALU.add).then_inc(folded, 1)
            with dve.Fori(0, NB) as half:
                for m in range(HT):
                    dve.wait_ge(gated, half * HT + m + 1)
                    if m >= 2:
                        dve.wait_ge(down, ONE + half * HT + m - 1)
                    else:
                        dve.wait_ge(down, ONE + half * HT)
                    dve.tensor_tensor(g[:, m % 2, :], banks[6 + m % 2][:, :], gate[:, m % 2, :], ALU.mult)\
                       .then_inc(g_made, 1)
                dve.wait_ge(down, ONE + (half + 1) * HT)
                for t in range(ST):
                    row = X[:, bass.ds(half * ST + t, 1), :].rearrange("p a n -> p (a n)")
                    dve.tensor_tensor(row, banks[t][:, :], row, ALU.add).then_inc(taken, 1)
            dve.wait_ge(taken, ONE + TT)

        @block.tensor
        def _(pe):
            pe.sem_inc(down, ONE)
            pe.wait_ge(lora_in, 64)
            j = 0
            for i, c in steps:
                for at, n in CUTS:
                    if j >= 8:
                        pe.wait_ge(folded, j - 7)
                    pe.matmul(banks[j % 8][:, 0:n], lora_a[:, i, c * P:(c + 1) * P], lora_b[:, i, at:at + n],
                              start=True, stop=True).then_inc(delta, 1)
                    j += 1
            for m in range(HT):
                pe.wait_ge(folded, j - 7)
                pe.matmul(banks[j % 8][:, :], a2[:, m * P:(m + 1) * P], b2[:, :], start=True, stop=True)\
                  .then_inc(delta, 1)
                j += 1
            pe.wait_ge(w_low, len(steps))
            pe.wait_ge(folded, j)

            def project(half, m):
                if m >= 2:
                    pe.wait_ge(g_made, ONE + half * HT + m - 1)
                else:
                    pe.wait_ge(g_made, ONE + half * HT)
                for i in range(2):
                    k = 0
                    for w, x in ((w_hi, xh), (w_lo, xh), (w_hi, xl)):
                        for c in range(DC):
                            last = pe.matmul(banks[4 + 2 * i + m % 2][:, :], w[:, i, c, m * P:(m + 1) * P],
                                             x[:, c, bass.ds(half * S, S)], start=k == 0, stop=k == 3 * DC - 1)
                            k += 1
                last.then_inc(hidden, 1)

            with pe.Fori(0, NB) as half:
                project(half, 0)
                pe.wait_ge(taken, ONE + half * ST)
                for m in range(HT):
                    if m + 1 < HT:
                        project(half, m + 1)
                    pe.wait_ge(g_made, ONE + half * HT + m + 1)
                    for t in range(ST):
                        last = pe.matmul(banks[t][:, :], g[:, m % 2, t * P:(t + 1) * P], w2[:, m, :],
                                         start=m == 0, stop=m == HT - 1)
                    last.then_inc(down, 1)


def gqa_stage(nc, ctx, dram, sb):
    own = ExitStack()
    with own:
        def buf(name, shape, dt=F32):
            return own.enter_context(nc.sbuf_tensor(name, shape, dt))

        def psum(name, shape):
            return own.enter_context(nc.psum_tensor(name, shape, F32))

        def sem(name):
            return ctx.enter_context(nc.semaphore("gqa_" + name))

        X, xh, xl, ident = sb["X"], sb["xh"], sb["xl"], sb["ident"]
        NU = GQ * NB
        wq_raw = buf("wq_raw", [P, GQ, DC, P])
        wkv_raw = buf("wkv_raw", [P, 2, DC, P])
        wo_raw = buf("wo_raw", [P, GQ, D])
        wq = [buf(f"wq_{k}", [P, GQ, DC, P], F32R) for k in ("hi", "lo")]
        wkv = [buf(f"wkv_{k}", [P, 2, DC, P], F32R) for k in ("hi", "lo")]
        wo = [buf(f"wo_{k}", [P, GQ, D], F32R) for k in ("hi", "lo")]
        K = [buf(f"k_{k}", [P, NB, S], F32R) for k in ("hi", "lo")]
        Q = [buf(f"q_{k}", [P, 2, S], F32R) for k in ("hi", "lo")]
        V = buf("v1", [P, NB, ST, P])
        tables = buf("tables", [P, 4, S])
        by_cos = buf("by_cos", [P, S])
        by_sin = buf("by_sin", [P, S])
        roped = buf("roped", [P, S])
        probs = buf("probs1", [P, 2, ST, S])
        probsT = buf("probsT", [P, 3, S])
        O = [buf(f"o_{k}", [P, NB, GQ, S], F32R) for k in ("hi", "lo")]
        minus_max = buf("minus_max", [P, ST])
        sums = buf("sums", [P, 2, ST])
        inverse = buf("inverse", [P, ST])
        mask = buf("mask_sb", [P, 2, P], F32R)
        mask_raw = buf("mask_raw", [P, 2, P])
        ps_s = [psum(f"ps_s{i}", [P, S]) for i in range(3)]
        place = {3: (0, 0), 2: (1, 0), 0: (1, 3 * P), 1: (2, 0)}
        ps_t = [psum(f"ps_t{i}", [P, S]) for i in range(2)]
        ps_r = [psum(f"ps_r{i}", [P, S]) for i in range(2)]
        ps_o = psum("ps_o1", [P, S])
        pieces = [[(0, 0)], [(1, 0), (3, 3 * P)], [(2, 0)]]

        tables_in = sem("tables_in")
        mask_set = sem("mask_set")
        wqkv_in = sem("wqkv_in")
        wo_in = sem("wo_in")
        step = sem("step")
        wkv_split = sem("wkv_split")
        wq_split = sem("wq_split")
        wo_split = sem("wo_split")
        made = sem("made")
        taken = sem("taken")
        v_taken = sem("v_taken")
        summed = sem("summed")
        r_high = sem("r_high")
        r_low = sem("r_low")
        scored = sem("scored")
        maxed = sem("maxed")
        exped = sem("exped")
        inverted = sem("inverted")
        normed = sem("normed")
        turned = sem("turned")
        t_taken = sem("t_taken")
        pv_made = sem("pv_made")
        o_high = sem("o_high")
        o_low = sem("o_low")
        gate_sp, gate_pool = sem("gate_sp"), sem("gate_pool")
        START, PER, TAKEN = 4, 3 * NU - 4, 3 * NU - 6

        def ring_query(u): return u
        def ring_next(k): return NU + k
        def ring_out(last, j): return (NU if last else NU + 4) + j
        def take_query(u): return u - 2
        def take_next(k): return NU - 2 + k
        def take_out(last, j): return (NU - 2 if last else NU + 2) + j
        ONE = 1
        RP = NU + 2

        block = own.enter_context(nc.Block())

        def run(engine, body):
            with engine.Fori(0, NKV - 1) as kv:
                body(kv, False)
            body(NKV - 1, True)

        @block.sync
        def _(sp):
            def load_qkv(kv):
                sp.dma_start(wkv_raw[:, :, :, :], dram["wkv1"][bass.ds(kv, 1), :, :, :, :].rearrange(
                    "a p i c n -> (a p) i c n")).then_inc(wqkv_in, 16)
                sp.dma_start(wq_raw[:, :, :, :], dram["wq1"][bass.ds(kv, 1), :, :, :, :].rearrange(
                    "a p h c n -> (a p) h c n")).then_inc(wqkv_in, 16)

            def load_wo(kv):
                sp.dma_start(wo_raw[:, :, :], dram["wo1"][bass.ds(kv, 1), :, :, :].rearrange(
                    "a p h n -> (a p) h n")).then_inc(wo_in, 16)

            load_qkv(0)
            sp.dma_start(tables[:, :, :], dram["tables"].rearrange("i p s -> p i s")).then_inc(tables_in, 16)
            load_wo(0)

            def body(kv, last):
                if not last:
                    sp.wait_ge(wkv_split, 2 * (kv + 1))
                    sp.sem_inc(gate_sp, 1)
                    sp.wait_ge(wq_split, GQ * (kv + 1))
                    sp.sem_inc(gate_sp, 1)
                    load_qkv(kv + 1)
                    sp.wait_ge(wo_split, GQ * (kv + 1))
                    sp.sem_inc(gate_sp, 1)
                    load_wo(kv + 1)

            run(sp, body)

        @block.gpsimd
        def _(pool):
            pool.memset(mask_raw[:, :, :], 0.0).then_inc(mask_set, 1)
            pool.wait_ge(mask_set, 1)
            pool.affine_select(out=mask_raw[:, 0, :], in_=mask_raw[:, 0, :], compare_op=ALU.not_equal, fill=1.0,
                               base=0, pattern=[[-1, P]], channel_multiplier=1).then_inc(mask_set, 1)
            pool.affine_select(out=mask_raw[:, 1, :], in_=mask_raw[:, 1, :], compare_op=ALU.is_ge, fill=-1e30,
                               base=0, pattern=[[-1, P]], channel_multiplier=1).then_inc(mask_set, 1)
            pool.wait_ge(mask_set, 3)
            pool.tensor_copy(mask[:, :, :], mask_raw[:, :, :]).then_inc(mask_set, 1)

            def split(parts, raw, count, at_step):
                pool.sem_inc(gate_pool, 1)
                hi, lo = parts
                pool.tensor_copy(hi, raw).then_inc(step, 1)
                pool.wait_ge(step, at_step)
                pool.tensor_tensor(lo, raw, hi, ALU.subtract).then_inc(count, 1)

            EACH = 2 + 2 * GQ

            def split_kv(i, at_step):
                split([w[:, i, :, :] for w in wkv], wkv_raw[:, i, :, :], wkv_split, at_step)

            def split_q(h, at_step):
                split([w[:, h, :, :] for w in wq], wq_raw[:, h, :, :], wq_split, at_step)

            def split_o(h, at_step):
                split([w[:, h, :] for w in wo], wo_raw[:, h, :], wo_split, at_step)

            def rope(n, place, out, hi):
                pool.wait_ge(taken, place + 1)
                pool.wait_ge(r_low, n)
                pool.tensor_tensor(roped[:, :], by_cos[:, :], by_sin[:, :], ALU.add).then_inc(summed, 1)
                pool.wait_ge(r_high, n + 1)
                pool.tensor_tensor(out, roped[:, :], hi, ALU.subtract).then_inc(r_low, 1)

            def rope_key(n, place, b):
                rope(n, place, K[1][:, b, :], K[0][:, b, :])

            def rope_query(n, place, u):
                rope(n, place, Q[1][:, u % 2, :], Q[0][:, u % 2, :])

            pool.wait_ge(wqkv_in, 32)
            split_kv(0, 1)
            split_q(0, 2)
            for b in range(NB):
                rope_key(2 * b, 2 * b, b)
                rope_query(2 * b + 1, 2 * b + 1, b)
            split_kv(1, 3)
            for h in range(1, GQ):
                split_q(h, 3 + h)

            def body(kv, last):
                r = START + RP * kv
                tk = START + TAKEN * kv
                s = 2 + GQ + EACH * kv
                n = 0
                after = {2: [("o", 0)], 3: [("o", 1), ("kv", 0)], 4: [("o", 2), ("q", 0)],
                         5: [("o", 3), ("q", 1)], 6: [("kv", 1)], 7: [("q", 2)]}
                for u in range(2, NU):
                    rope_query(r + u - 2, tk + take_query(u), u)
                    if u == 2:
                        pool.wait_ge(wo_in, 16 * (kv + 1))
                        pool.sem_inc(gate_pool, 1)
                        pool.wait_ge(made, START + PER * kv)
                    if u == 3 and not last:
                        pool.wait_ge(wqkv_in, 32 * (kv + 2))
                    for kind, h in after[u]:
                        if last and kind != "o":
                            continue
                        n += 1
                        {"o": split_o, "kv": split_kv, "q": split_q}[kind](h, s + n)
                if not last:
                    for b in range(NB):
                        rope_key(r + NU - 2 + 2 * b, tk + take_next(2 * b), b)
                        rope_query(r + NU - 1 + 2 * b, tk + take_next(2 * b + 1), b)
                    split_q(3, s + n + 1)

            run(pool, body)

        @block.scalar
        def _(act):
            def rope_high(n, out):
                act.wait_ge(summed, n + 1)
                act.activation(out, roped[:, :], ACT.Copy).then_inc(r_high, 1)

            def values(kv, b):
                act.wait_ge(made, START + PER * kv + b + 1)
                act.activation(V[:, b, :, :], ps_r[(START + b) % 2][:, :].rearrange("p (t n) -> p t n", t=ST), ACT.Copy)\
                   .then_inc(v_taken, 1)

            def softmax(i, u):
                for k, t in enumerate((3, 2, 0, 1)):
                    act.wait_ge(maxed, ST * i + (3 if k == 1 else k + 1))
                    bank, at = place[t]
                    n = (t + 1) * P
                    act.activation(probs[:, u % 2, t, 0:n], ps_s[bank][:, at:at + n], ACT.Exp,
                                   bias=minus_max[:, t:t + 1], accum_out=sums[:, u % 2, t:t + 1]).then_inc(exped, 1)

            def take_turned(kv, u, k):
                act.wait_ge(turned, 3 * (NU * kv + u) + k + 1)
                n = S if k < 2 else 2 * P
                act.activation(probsT[:, k, 0:n], ps_t[(u + k) % 2][:, 0:n], ACT.Copy).then_inc(t_taken, 1)

            def take_outputs(kv, u):
                i = NU * kv + u
                act.wait_ge(pv_made, i + 1)
                act.activation(O[0][:, u % 2, u // 2, :], ps_o[:, :], ACT.Copy).then_inc(o_high, 1)

            act.sem_inc(exped, ONE)
            for b in range(NB):
                rope_high(2 * b, K[0][:, b, :])
                rope_high(2 * b + 1, Q[0][:, b, :])

            def body(kv, last):
                r = START + RP * kv
                i = NU * kv
                softmax(i, 0)
                values(kv, 0)
                values(kv, 1)
                rope_high(r, Q[0][:, 0, :])
                for u in range(1, NU):
                    take_turned(kv, u - 1, 0)
                    take_turned(kv, u - 1, 1)
                    softmax(i + u, u)
                    take_turned(kv, u - 1, 2)
                    if u < NU - 2:
                        rope_high(r + u, Q[0][:, u % 2, :])
                    elif not last:
                        rope_high(r + NU - 2 + 2 * (u % 2), K[0][:, u % 2, :])
                    take_outputs(kv, u - 1)
                    if u >= NU - 2 and not last:
                        rope_high(r + NU - 1 + 2 * (u % 2), Q[0][:, u % 2, :])
                for k in range(3):
                    take_turned(kv, NU - 1, k)
                take_outputs(kv, NU - 1)

            run(act, body)

        @block.vector
        def _(dve):
            def rope(n, ring, bank, keys, first=False):
                dve.wait_ge(made, ring + 1)
                if not first:
                    dve.wait_ge(summed, n)
                cos, sin = tables[:, 2 * keys, :], 2 * keys + 1
                ps = ps_r[bank]
                h = P // 2
                dve.tensor_tensor(by_sin[0:h, :], ps[h:P, :], tables[0:h, sin, :], ALU.mult)
                dve.tensor_tensor(by_sin[h:P, :], ps[0:h, :], tables[h:P, sin, :], ALU.mult)
                dve.tensor_tensor(by_cos[:, :], ps[:, :], cos, ALU.mult).then_inc(taken, 1)

            def maxima(i, u):
                for k, t in enumerate((3, 2, 0, 1)):
                    if k == 0:
                        dve.wait_ge(scored, i + 1)
                    bank, at = place[t]
                    dve.tensor_reduce(minus_max[:, t:t + 1], ps_s[bank][:, at:at + (t + 1) * P], axis=AXX, op=ALU.max,
                                      negate=True).then_inc(maxed, 1)

            def normalise(i, u):
                dve.wait_ge(exped, ONE + ST * (i + 1))
                dve.reciprocal(inverse[:, :], sums[:, u % 2, :]).then_inc(inverted, 1)
                dve.wait_ge(inverted, i + 1)
                for t in range(ST):
                    n = (t + 1) * P
                    ins = dve.tensor_scalar(probs[:, u % 2, t, 0:n], probs[:, u % 2, t, 0:n], inverse[:, t:t + 1],
                                            None, ALU.mult)
                ins.then_inc(normed, 1)

            def low_o(i, u):
                dve.wait_ge(o_high, i + 1)
                dve.tensor_tensor(O[1][:, u % 2, u // 2, :], ps_o[:, :], O[0][:, u % 2, u // 2, :], ALU.subtract)\
                   .then_inc(o_low, 1)

            dve.sem_inc(o_low, ONE)
            dve.wait_ge(tables_in, 16)
            for n in range(START):
                rope(n, n, n % 2, 1 - n % 2, n == 0)

            def body(kv, last):
                r = START + RP * kv
                ring = START + PER * kv
                i = NU * kv

                def add_out(j):
                    at = ring_out(last, j)
                    dve.wait_ge(made, ring + at + 1)
                    dve.tensor_tensor(X[:, j, :], ps_r[(START + at) % 2][:, :], X[:, j, :], ALU.add).then_inc(taken, 1)

                maxima(i, 0)
                normalise(i, 0)
                rope(r, ring + ring_query(2), (START + ring_query(2)) % 2, 0)
                for u in range(1, NU):
                    maxima(i + u, u)
                    normalise(i + u, u)
                    if u < NU - 2:
                        rope(r + u, ring + ring_query(u + 2), (START + ring_query(u + 2)) % 2, 0)
                        low_o(i + u - 1, u - 1)
                    else:
                        for k in range(2) if not last else ():
                            at = 2 * (u % 2) + k
                            rope(r + NU - 2 + at, ring + ring_next(at), (START + ring_next(at)) % 2, 1 - k)
                        low_o(i + u - 1, u - 1)
                add_out(0)
                add_out(1)
                low_o(i + NU - 1, NU - 1)
                for j in range(2, TT):
                    add_out(j)

            run(dve, body)
            dve.wait_ge(taken, TAKEN * NKV)

        @block.tensor
        def _(pe):
            TERMS = ((0, 0), (1, 0), (0, 1))
            x = (xh, xl)

            def project(w, sl, b, bank):
                k = 0
                for i, j in TERMS:
                    for c in range(DC):
                        last = pe.matmul(ps_r[bank][:, :], w[i][:, sl, c, :], x[j][:, c, b * S:(b + 1) * S],
                                         start=k == 0, stop=k == 3 * DC - 1)
                        k += 1
                last.then_inc(made, 1)

            def values(b, bank):
                for t in range(ST):
                    k = 0
                    at = b * S + t * P
                    for i, j in TERMS:
                        for c in range(DC):
                            last = pe.matmul(ps_r[bank][:, t * P:(t + 1) * P], x[j][:, c, at:at + P], wkv[i][:, 1, c, :],
                                             start=k == 0, stop=k == 3 * DC - 1)
                            k += 1
                last.then_inc(made, 1)

            def scores(i, u, rope):
                b = u % 2
                pe.wait_ge(r_low, rope + 1)
                pe.wait_ge(exped, ONE + ST * i)
                for t in (3, 2, 0, 1):
                    bank, at = place[t]
                    n = (t + 1) * P
                    out = ps_s[bank][:, at:at + n]
                    for k, (q, kk) in enumerate(TERMS):
                        pe.matmul(out, Q[q][:, b, t * P:(t + 1) * P], K[kk][:, b, 0:n], start=k == 0, stop=False)
                    last = pe.matmul(ps_s[bank][:, at + n - P:at + n], mask[:, 0, :], mask[:, 1, :],
                                     start=False, stop=True)
                last.then_inc(scored, 1)

            def turn(i, u, k):
                if k == 0:
                    pe.wait_ge(normed, i + 1)
                if k == 2:
                    pe.wait_ge(t_taken, 3 * i + 1)
                for tile, at in pieces[k]:
                    for t in range(tile, ST):
                        last = pe.transpose(ps_t[(u + k) % 2][:, at + (t - tile) * P:at + (t - tile + 1) * P],
                                            probs[:, u % 2, t, tile * P:(tile + 1) * P], ident[:, :])
                last.then_inc(turned, 1)

            def outputs(i, u):
                b = u % 2
                pe.wait_ge(o_low, ONE + i)
                for k, piece in enumerate(pieces):
                    pe.wait_ge(t_taken, 3 * i + k + 1)
                    for tile, at in piece:
                        last = pe.matmul(ps_o[:, tile * P:S], V[:, b, tile, :], probsT[:, k, at:at + S - tile * P],
                                         start=tile == 0, stop=k == 2)
                last.then_inc(pv_made, 1)

            def merge(last, tk, j):
                at = ring_out(last, j)
                pe.wait_ge(taken, tk + take_out(last, j) - 1)
                k = 0
                for o, w in TERMS:
                    for h in range(GQ):
                        ins = pe.matmul(ps_r[(START + at) % 2][:, :],
                                        O[o][:, j // ST, h, (j % ST) * P:(j % ST + 1) * P], wo[w][:, h, :],
                                        start=k == 0, stop=k == 3 * GQ - 1)
                        k += 1
                ins.then_inc(made, 1)

            pe.wait_ge(mask_set, 4)
            pe.wait_ge(wkv_split, 1)
            project(wkv, 0, 0, 0)
            pe.wait_ge(wq_split, 1)
            project(wq, 0, 0, 1)
            pe.wait_ge(taken, 1)
            project(wkv, 0, 1, 0)
            pe.wait_ge(taken, 2)
            project(wq, 0, 1, 1)

            def body(kv, last):
                tk = START + TAKEN * kv
                r = START + RP * kv
                i = NU * kv

                def query(u):
                    pe.wait_ge(wq_split, GQ * kv + u // 2 + 1)
                    if u < 4:
                        pe.wait_ge(v_taken, 2 * kv + u - 1)
                    else:
                        pe.wait_ge(taken, tk + take_query(u) - 1)
                    project(wq, u // 2, u % 2, (START + ring_query(u)) % 2)

                scores(i, 0, r - 3)
                pe.wait_ge(wkv_split, 2 * kv + 2)
                for b in range(NB):
                    pe.wait_ge(taken, tk + b - 1)
                    values(b, (START + b) % 2)
                query(2)
                for u in range(1, NU):
                    scores(i + u, u, r + u - 2)
                    turn(i + u - 1, u - 1, 0)
                    turn(i + u - 1, u - 1, 1)
                    if u < NU - 2:
                        query(u + 2)
                    elif not last:
                        b = u % 2
                        pe.wait_ge(wkv_split, 2 * kv + 3)
                        pe.wait_ge(taken, tk + take_next(2 * b) - 1)
                        project(wkv, 0, b, (START + ring_next(2 * b)) % 2)
                        pe.wait_ge(wq_split, GQ * (kv + 1) + 1)
                        pe.wait_ge(taken, tk + take_next(2 * b + 1) - 1)
                        project(wq, 0, b, (START + ring_next(2 * b + 1)) % 2)
                    if u == 1:
                        pe.wait_ge(v_taken, 2 * kv + 2)
                    turn(i + u - 1, u - 1, 2)
                    outputs(i + u - 1, u - 1)
                for k in range(3):
                    turn(i + NU - 1, NU - 1, k)
                pe.wait_ge(wo_split, GQ * (kv + 1))
                pe.wait_ge(o_low, ONE + i + NU - 1)
                merge(last, tk, 0)
                merge(last, tk, 1)
                outputs(i + NU - 1, NU - 1)
                merge(last, tk, 2)
                merge(last, tk, 3)
                pe.wait_ge(o_low, ONE + i + NU)
                for j in range(ST, TT):
                    merge(last, tk, j)

            run(pe, body)


def cluster_stage(nc, ctx, dram, sb):
    own = ExitStack()
    with own:
        def buf(name, shape, dt=F32):
            return own.enter_context(nc.sbuf_tensor(name, shape, dt))

        def sem(name):
            return ctx.enter_context(nc.semaphore("cl_" + name))

        X, xh, xl = sb["X"], sb["xh"], sb["xl"]
        w = buf("w_dense", [P, DC, D])
        wh = buf("w_dense_hi", [P, DC, D], F32R)
        wl = buf("w_dense_lo", [P, DC, D], F32R)
        cent = buf("cent", [P, DC, NCL])
        ch = buf("cent_hi", [P, DC, NCL], F32R)
        cl = buf("cent_lo", [P, DC, NCL], F32R)
        bias = buf("bias_sb", [1, D])
        ones = buf("ones_sb", [P, P])
        assign_i = buf("assign_i", [NCL, D], mybir.dt.int32)
        assign = buf("assign", [NCL, D])
        which = buf("which", [NCL, 1])
        onehot = buf("onehot", [NCL, D])
        chosen = buf("chosen", [NCL, 1])
        soft = buf("soft", [P, TT, NCL])
        top = buf("top", [P, TT, 1])
        total = buf("total", [P, TT, 1])
        query = buf("query", [P, TT])
        any_hit = buf("any_hit", [P, NCL])
        column = buf("column", [P, D])
        dense = buf("dense", [P, 2, D])
        ps_l = own.enter_context(nc.psum_tensor("ps_l", [P, TT, NCL], F32))
        ps_c = own.enter_context(nc.psum_tensor("ps_c", [P, D], F32))
        ps_h = own.enter_context(nc.psum_tensor("ps_h", [P, D], F32))
        ps_d = [own.enter_context(nc.psum_tensor(f"ps_d{i}", [P, D], F32)) for i in range(4)]
        cent_in, w_in, small_in = sem("cent_in"), sem("w_in"), sem("small_in")
        ones_set = sem("ones_set")
        which_set = sem("which_set")
        step = sem("step")
        logits = sem("logits")
        shifted = sem("shifted")
        exped = sem("exped")
        hits_done = sem("hits_done")
        cent_done = sem("cent_done")
        w_done = sem("w_done")
        counted = sem("counted")
        onehot_done = sem("onehot_done")
        column_made = sem("column_made")
        made = sem("made")
        taken = sem("taken")
        added = sem("added")
        block = own.enter_context(nc.Block())

        @block.sync
        def _(sp):
            sp.dma_start(cent[:, :, :], dram["centroids"].rearrange("(c p) n -> p c n", p=P)).then_inc(cent_in, 16)
            sp.dma_start(w[:, :, :], dram["w_dense"].rearrange("(c p) n -> p c n", p=P)).then_inc(w_in, 16)
            sp.dma_start(assign_i[:, :], dram["assignments"].partition_broadcast(NCL)).then_inc(small_in, 16)
            sp.dma_start(bias[:, :], dram["bias"].rearrange("(a n) -> a n", a=1)).then_inc(small_in, 16)

        @block.gpsimd
        def _(pool):
            pool.memset(ones[:, :], 1.0).then_inc(ones_set, 1)
            pool.iota(which[:, :], pattern=[[0, 1]], base=0, channel_multiplier=1,
                      allow_small_or_imprecise_dtypes=True).then_inc(which_set, 1)

        @block.scalar
        def _(act):
            act.wait_ge(w_in, 16)
            act.activation(wh[:, :, :], w[:, :, :], ACT.Copy).then_inc(w_done, 1)
            act.wait_ge(shifted, 1)
            act.activation(soft[:, :, :], soft[:, :, :], ACT.Exp, scale=1.0 / TEMPERATURE).then_inc(exped, 1)

        @block.vector
        def _(dve):
            n = [0]

            def after(ins):
                n[0] += 1
                ins.then_inc(step, 1)
                dve.wait_ge(step, n[0])

            dve.wait_ge(cent_in, 16)
            after(dve.tensor_copy(ch[:, :, :], cent[:, :, :]))
            dve.tensor_tensor(cl[:, :, :], cent[:, :, :], ch[:, :, :], ALU.subtract).then_inc(cent_done, 1)
            dve.wait_ge(w_done, 1)
            dve.tensor_tensor(wl[:, :, :], w[:, :, :], wh[:, :, :], ALU.subtract).then_inc(w_done, 1)
            dve.wait_ge(small_in, 32)
            after(dve.tensor_copy(assign[:, :], assign_i[:, :]))
            dve.wait_ge(logits, 1)
            after(dve.tensor_reduce(top[:, :, 0], ps_l[:, :, :], axis=AXX, op=ALU.max))
            dve.tensor_tensor(soft[:, :, :], ps_l[:, :, :], top[:, :, :].broadcast_to([P, TT, NCL]),
                              ALU.subtract).then_inc(shifted, 1)
            dve.wait_ge(exped, 1)
            after(dve.tensor_reduce(total[:, :, 0], soft[:, :, :], axis=AXX, op=ALU.add))
            after(dve.reciprocal(total[:, :, 0], total[:, :, 0]))
            after(dve.tensor_tensor(soft[:, :, :], soft[:, :, :], total[:, :, :].broadcast_to([P, TT, NCL]), ALU.mult))
            after(dve.tensor_scalar(soft[:, :, :], soft[:, :, :], THRESHOLD, None, ALU.is_gt))
            dve.tensor_reduce(query[:, :], soft[:, :, :], axis=AXX, op=ALU.max)
            dve.tensor_reduce(any_hit[:, :], soft[:, :, :].rearrange("p t n -> p n t"), axis=AXX, op=ALU.max)\
               .then_inc(hits_done, 1)
            dve.wait_ge(counted, 1)
            after(dve.tensor_scalar(chosen[:, :], ps_c[0:NCL, 0:1], 0.5, None, ALU.is_gt))
            dve.wait_ge(which_set, 1)
            dve.tensor_scalar(onehot[:, :], assign[:, :], which[:, 0:1], chosen[:, 0:1], ALU.is_equal, ALU.mult)\
               .then_inc(onehot_done, 1)
            dve.wait_ge(column_made, 1)
            after(dve.tensor_copy(column[:, :], ps_h[:, :]))
            for t in range(TT):
                dve.wait_ge(made, t + 1)
                dve.scalar_tensor_tensor(out=dense[:, t % 2, :], in0=ps_d[t % 4][:, :], scalar=query[:, t:t + 1],
                                         in1=column[:, :], op0=ALU.mult, op1=ALU.mult).then_inc(taken, 1)
                dve.wait_ge(taken, t + 1)
                dve.tensor_tensor(X[:, t, :], X[:, t, :], dense[:, t % 2, :], ALU.add).then_inc(added, 1)
            dve.wait_ge(added, TT)

        @block.tensor
        def _(pe):
            TERMS = ((0, 0), (1, 0), (0, 1))
            x = (xh, xl)

            def product(out, t, w):
                k = 0
                for i, j in TERMS:
                    for c in range(DC):
                        last = pe.matmul(out, x[i][:, c, t * P:(t + 1) * P], w[j][:, c, :], start=k == 0,
                                         stop=k == 3 * DC - 1)
                        k += 1
                return last

            pe.wait_ge(cent_done, 1)
            for t in range(TT):
                last = product(ps_l[:, t, :], t, (ch, cl))
            last.then_inc(logits, 1)
            pe.wait_ge(w_done, 2)
            pe.wait_ge(small_in, 32)
            pe.wait_ge(ones_set, 1)

            def dense_tile(t):
                if t >= 4:
                    pe.wait_ge(taken, t - 3)
                pe.matmul(ps_d[t % 4][:, :], ones[0:1, :], bias[:, :], start=True, stop=False)
                k = 0
                for i, j in TERMS:
                    for c in range(DC):
                        last = pe.matmul(ps_d[t % 4][:, :], x[i][:, c, t * P:(t + 1) * P], (wh, wl)[j][:, c, :],
                                         start=False, stop=k == 3 * DC - 1)
                        k += 1
                last.then_inc(made, 1)

            for t in range(4):
                dense_tile(t)
            pe.wait_ge(hits_done, 1)
            pe.matmul(ps_c[0:NCL, 0:1], any_hit[:, :], ones[:, 0:1], start=True, stop=True).then_inc(counted, 1)
            pe.wait_ge(onehot_done, 1)
            pe.matmul(ps_h[:, :], ones[0:NCL, :], onehot[:, :], start=True, stop=True).then_inc(column_made, 1)
            for t in range(4, TT):
                dense_tile(t)


def program(nc, dram, out):
    for name in ("content_q", "content_k"):
        dram[name] = nc.dram_tensor(name, (NH0, CROWS, T), F32, kind="Internal").ap()
    with ExitStack() as ctx:
        def keep(stack, name, shape, dt=F32):
            sb[name] = stack.enter_context(nc.sbuf_tensor(name, shape, dt))

        sb = {}
        keep(ctx, "ident", [P, P])
        keep(ctx, "X", [P, TT, D])
        keep(ctx, "xh", [P, DC, T], F32R)
        keep(ctx, "xl", [P, DC, T], F32R)
        with ExitStack() as layer:
            for name in ("Q1", "Q2", "K2", "KX"):
                keep(layer, name, [P, NB, GH, S], F32R)
            keep(layer, "K1", [P, NB, S], F32R)
            keep(layer, "V", [P, TT, D])
            keep(layer, "V_slot", [P, NB, ST, GH, 32])
            keep(layer, "mrow", [GH, S], F32R)
            latent_stage(nc, ctx, dram, sb)
            mla_stage(nc, ctx, dram, sb)
        merge_heads_stage(nc, ctx, dram, sb)
        norm_stage(nc, ctx, "n1_", sb)
        swiglu_stage(nc, ctx, dram, sb)
        norm_stage(nc, ctx, "n2_", sb)
        gqa_stage(nc, ctx, dram, sb)
        norm_stage(nc, ctx, "n3_", sb)
        cluster_stage(nc, ctx, dram, sb)
        norm_stage(nc, ctx, "n4_", sb, out)


def layouts(i):
    import numpy as np

    def cat(names, axis):
        return np.concatenate([i[n] for n in names], axis)

    def pad(a, axis):
        width = [(0, 0)] * a.ndim
        width[axis] = (0, HP - HID)
        return np.pad(a, width)

    def by_key_head(w, heads):
        return w.reshape(DC, P, NKV, heads, P).transpose(2, 1, 3, 0, 4)

    x = i["L0_attn_x"].reshape(T, D)
    half = P // 2
    inv_freq = (1.0 / 10000.0 ** (np.arange(0, P, 2, dtype=np.float32) / np.float32(P))).astype(np.float32)
    angle = np.outer(inv_freq, np.arange(S, dtype=np.float32)).astype(np.float32)
    cos = np.concatenate([np.cos(angle)] * 2, 0).astype(np.float32)
    sin = np.concatenate([-np.sin(angle), np.sin(angle)], 0).astype(np.float32)
    scale = np.float32(P) ** np.float32(-0.5)
    return {
        "x": x,
        "xT": x.T,
        "w_down": cat(["L0_attn_Wq_down", "L0_attn_Wkv_down"], 1),
        "w_krope": cat(["L0_attn_Wk_rope", "L0_attn_Wk_rope"], 1),
        "w_qup": i["L0_attn_Wq_up"],
        "w_kvup": cat(["L0_attn_Wk_up", "L0_attn_Wv_up"], 1),
        "w_qrope": i["L0_attn_Wq_rope"],
        "wo0": i["L0_attn_Wo"],
        "w13": pad(np.stack([i["L0_ffn_w1"].T, i["L0_ffn_w3"].T]), 2),
        "w2": pad(i["L0_ffn_w2"].T, 0),
        "lora_a13": np.stack([i["L0_ffn_lora_A1"], i["L0_ffn_lora_A3"]]),
        "lora_b13": pad(np.stack([i["L0_ffn_lora_B1"].T, i["L0_ffn_lora_B3"].T]), 2),
        "lora_a2": pad(i["L0_ffn_lora_A2"], 1),
        "lora_b2": i["L0_ffn_lora_B2"].T,
        "wq1": by_key_head(i["L1_attn_Wq"], GQ),
        "wkv1": np.concatenate([by_key_head(i["L1_attn_Wk"], 1), by_key_head(i["L1_attn_Wv"], 1)], 2),
        "wo1": i["L1_attn_Wo"].reshape(NKV, GQ, P, D).transpose(0, 2, 1, 3),
        "tables": np.stack([cos * scale, sin * scale, cos, sin]).astype(np.float32),
        "w_dense": i["L1_ffn_weight"].T,
        "bias": i["L1_ffn_bias"],
        "centroids": i["L1_ffn_centroids"].T,
        "assignments": i["L1_ffn_assignments"],
    }


def kernel(**inputs):
    import numpy as np
    import concourse.bacc as bacc
    from concourse.bass_utils import run_bass_kernel_spmd

    arrays = {"in_" + n: np.ascontiguousarray(a) for n, a in layouts({n: np.asarray(a) for n, a in inputs.items()}).items()}
    nc = bacc.Bacc("TRN2", target_bir_lowering=False, num_devices=1)
    dram = {n[3:]: nc.dram_tensor(n, a.shape, mybir.dt.from_np(a.dtype), kind="ExternalInput").ap()
            for n, a in arrays.items()}
    out = nc.dram_tensor("out", (T, D), F32, kind="ExternalOutput").ap()
    program(nc, dram, out)
    r = run_bass_kernel_spmd(nc, [arrays], core_ids=[0])
    return r.results[0]["out"].reshape(NB, S, D)
```

```python
from contextlib import ExitStack

import concourse.bass as bass
from concourse import mybir

F32 = mybir.dt.float32
F32R = mybir.dt.float32r
ACT = mybir.ActivationFunctionType
ALU = mybir.AluOpType
AXX = mybir.AxisListType.X

P = 128
T = 1024
NB = 2
S = T // NB
D = 512
DC = D // P
TT = T // P
ST = S // P

NH0 = 128
HD0 = D // NH0
LAT = 64
ROPE = 64
GH = 4
NG = NH0 // GH
CROWS = 3 * HD0
MROW = 96
KC0 = ROPE + CROWS


def latent_stage(nc, ctx, dram, sb):
    own = ExitStack()
    with own:
        def buf(name, shape, dt=F32):
            return own.enter_context(nc.sbuf_tensor(name, shape, dt))

        xT = buf("xT_sb", [P, DC, T])
        w_down = buf("w_down_sb", [P, DC, P])
        w_krope = buf("w_krope_sb", [P, DC, P])
        w_up = buf("w_up", [P, 2 * D])
        cT = buf("cT", [P, T])
        hi = {"q": sb["X"][:, :, :].bitcast(F32R).rearrange("p t n -> p (t n)").rearrange("p (m t) -> p m t", m=DC),
              "k": buf("content_hi_k", [P, DC, T], F32R)[:, :, :]}
        lo = {"q": sb["Q1"][:, :, :, :].rearrange("p b j s -> p (b j s)").rearrange("p (m t) -> p m t", m=DC),
              "k": buf("content_lo_k", [P, DC, T], F32R)[:, :, :]}
        zeros = buf("zeros", [P, 1, S])
        ones = buf("ones0", [P, S])
        bank = [own.enter_context(nc.psum_tensor(f"latent_ps{i}", [P, S], F32)) for i in range(8)]

        def sem(name):
            return ctx.enter_context(nc.semaphore(name))

        x_in = sem("x_in")
        w_in = sem("w_in")
        x_split = sem("x_split")
        ps_full = sem("latent_ps_full")
        act_done = sem("latent_act_done")
        dve_done = sem("latent_dve_done")
        rows_set = sem("rows_set")
        rope_set = sem("rope_set")
        zeros_set = sem("zeros_set")
        parts_out = sem("parts_out")
        jobs = [("c", 0, b) for b in range(NB)] + [("r", 0, b) for b in range(NB)]
        jobs += [(k, m, b) for k in "qk" for m in range(DC) for b in range(NB)]
        jobs += [("v", t, 0) for t in range(TT)]
        block = own.enter_context(nc.Block())

        @block.sync
        def _(sp):
            sp.dma_start(w_down[:, :, :], dram["w_down"].rearrange("(c p) n -> p c n", p=P)).then_inc(w_in, 16)
            sp.dma_start(xT[:, :, :], dram["xT"].rearrange("(c p) t -> p c t", p=P)).then_inc(x_in, 16)
            sp.dma_start(w_krope[:, :, :], dram["w_krope"].rearrange("(c p) n -> p c n", p=P)).then_inc(w_in, 16)
            sp.dma_start(w_up[0:LAT, 0:D], dram["w_qup"]).then_inc(w_in, 16)
            sp.dma_start(w_up[LAT:P, :], dram["w_kvup"]).then_inc(w_in, 16)
            for i, k in enumerate("qk"):
                planes = (hi[k], hi[k], lo[k]) if k == "q" else (hi[k], lo[k], hi[k])
                for m in range(DC):
                    n = 4 + (i * DC + m) * NB + NB
                    sp.wait_ge(act_done, n)
                    sp.wait_ge(dve_done, n)
                    for r, part in enumerate(planes):
                        heads = dram["content_" + k][m * 32:(m + 1) * 32, r * HD0:(r + 1) * HD0, :]
                        sp.dma_start(heads, part[:, m, :].bitcast(F32)).then_inc(parts_out, 16)
            sp.wait_ge(parts_out, 2 * DC * 3 * 16)

        @block.gpsimd
        def _(pool):
            pool.memset(zeros[:, :, :], 0.0).then_inc(rows_set, 1)
            pool.wait_ge(rows_set, 1)
            pool.memset(ones[MROW:MROW + 1, :], 1.0).then_inc(rows_set, 1)
            pool.wait_ge(rows_set, 2)
            pool.memset(sb["V_slot"][:, :, :, :, :], 0.0).then_inc(rows_set, 1)
            pool.wait_ge(rows_set, 3)
            pool.memset(sb["V_slot"][:, :, :, :, HD0:HD0 + 1], 1.0).then_inc(rows_set, 1)
            pool.memset(sb["ident"][:, :], 0.0).then_inc(rows_set, 1)
            pool.wait_ge(rows_set, 5)
            pool.affine_select(out=sb["ident"][:, :], in_=sb["ident"][:, :], compare_op=ALU.not_equal, fill=1.0,
                               base=0, pattern=[[-1, P]], channel_multiplier=1).then_inc(rows_set, 1)
            pool.wait_ge(rows_set, 6)

        @block.scalar
        def _(act):
            for n, (kind, m, b) in enumerate(jobs):
                act.wait_ge(ps_full, n + 1)
                src = bank[n % 8][:, :]
                if kind == "c":
                    out = cT[:, b * S:(b + 1) * S]
                elif kind == "r":
                    out = sb["K1"][:, b, :]
                elif kind == "v":
                    out = sb["V"][:, m, :]
                else:
                    out = hi[kind][:, m, b * S:(b + 1) * S]
                act.activation(out, src, ACT.Copy).then_inc(act_done, 1)
                if kind == "r":
                    for j in range(GH):
                        act.activation(sb["KX"][0:ROPE, b, j, :], bank[n % 8][0:ROPE, :], ACT.Copy).then_inc(rope_set, 1)
            act.wait_ge(act_done, len(jobs))
            act.wait_ge(rope_set, NB * GH)

        @block.vector
        def _(dve):
            dve.wait_ge(rows_set, 2)
            for b in range(NB):
                for tile in (sb["Q2"], sb["K2"]):
                    dve.tensor_copy(tile[ROPE:P, b, :, :], zeros[ROPE:P, :, :].broadcast_to([ROPE, GH, S]))\
                       .then_inc(zeros_set, 1)
            dve.wait_ge(zeros_set, 2 * NB)
            for b in range(NB):
                for j in range(GH):
                    dve.tensor_copy(sb["K2"][MROW:MROW + 1, b, j, :], ones[MROW:MROW + 1, :]).then_inc(zeros_set, 1)
            dve.wait_ge(x_in, 16)
            for c in range(DC):
                dve.tensor_copy(sb["xh"][:, c, :], xT[:, c, :]).then_inc(x_split, 1)
                dve.wait_ge(x_split, 2 * c + 1)
                dve.tensor_tensor(sb["xl"][:, c, :], xT[:, c, :], sb["xh"][:, c, :], ALU.subtract).then_inc(x_split, 1)
            dve.wait_ge(x_split, 2 * DC)
            for n, (kind, m, b) in enumerate(jobs):
                if kind == "v":
                    break
                dve.wait_ge(act_done, n + 1)
                src = bank[n % 8]
                if kind == "c":
                    continue
                if kind == "r":
                    dve.wait_ge(rope_set, GH * (b + 1))
                    for j in range(GH):
                        ins = dve.tensor_tensor(sb["K2"][0:ROPE, b, j, :], src[0:ROPE, :], sb["K1"][0:ROPE, b, :],
                                                ALU.subtract)
                    ins.then_inc(dve_done, 3 if b == 0 else 1)
                else:
                    dve.tensor_tensor(lo[kind][:, m, b * S:(b + 1) * S], src[:, :], hi[kind][:, m, b * S:(b + 1) * S],
                                      ALU.subtract).then_inc(dve_done, 1)
            dve.wait_ge(dve_done, 4 + 4 * DC)
            dve.wait_ge(zeros_set, (2 + GH) * NB)

        @block.tensor
        def _(pe):
            pe.wait_ge(w_in, 64)
            pe.wait_ge(x_in, 16)
            for n, (kind, m, b) in enumerate(jobs):
                if n >= 8:
                    pe.wait_ge(act_done, n - 7)
                    if n - 8 >= 2 and jobs[n - 8][0] != "v":
                        pe.wait_ge(dve_done, n - 7)
                out = bank[n % 8][:, :]
                if kind in "cr":
                    w = w_down if kind == "c" else w_krope
                    for c in range(DC):
                        last = pe.matmul(out, w[:, c, :], xT[:, c, b * S:(b + 1) * S], start=c == 0, stop=c == DC - 1)
                else:
                    if n == 4:
                        pe.wait_ge(act_done, 2)
                    if kind == "q":
                        last = pe.matmul(out, w_up[0:LAT, m * P:(m + 1) * P], cT[0:LAT, b * S:(b + 1) * S],
                                         start=True, stop=True)
                    elif kind == "k":
                        last = pe.matmul(out, w_up[LAT:P, m * P:(m + 1) * P], cT[LAT:P, b * S:(b + 1) * S],
                                         start=True, stop=True)
                    else:
                        last = pe.matmul(out, cT[LAT:P, m * P:(m + 1) * P], w_up[LAT:P, D:2 * D],
                                         start=True, stop=True)
                last.then_inc(ps_full, 1)


def mla_stage(nc, ctx, dram, sb, groups=NG):
    SCALE = float((HD0 + ROPE) ** -0.5)
    own = ExitStack()
    with own:
        def buf(name, shape, dt=F32):
            return own.enter_context(nc.sbuf_tensor(name, shape, dt))

        def sem(name):
            return ctx.enter_context(nc.semaphore(name))

        w_raw = buf("w_raw", [P, DC, 2, P])
        w_hi = buf("w_hi", [P, DC, 2, P], F32R)
        w_lo = buf("w_lo", [P, DC, 2, P], F32R)
        Q1 = sb["Q1"]
        Q2 = sb["Q2"]
        K1 = sb["K1"]
        K2 = sb["K2"]
        KX = sb["KX"]
        probs = buf("probs", [P, GH, ST, S])
        row_max = buf("row_max", [P, ST, GH])
        mrow = sb["mrow"]
        oT = buf("oT", [P, S])
        recip = buf("recip", [P, ST, GH, 1])
        V_slot, V, O, ident = sb["V_slot"], sb["V"], sb["X"], sb["ident"]
        ps_score = [own.enter_context(nc.psum_tensor(f"ps_score{i}", [P, 2, S], F32)) for i in range(2)]
        ps_max = [own.enter_context(nc.psum_tensor(f"ps_max{i}", [P, S], F32)) for i in range(2)]
        ps_x = own.enter_context(nc.psum_tensor("ps_x", [P, S], F32))
        ps_o = own.enter_context(nc.psum_tensor("ps_o", [P, S], F32))

        w_in = sem("wq_in")
        w_step = sem("wq_step")
        w_split = sem("wq_split")
        q_made = sem("q_made")
        q_high = sem("q_high")
        q_low = sem("q_low")
        q_copied = [sem(f"q_copied{b}") for b in range(NB)]
        content_in = [sem(f"content_in{b}") for b in range(NB)]
        max_made = sem("max_made")
        max_taken = sem("max_taken")
        max_turned = sem("max_turned")
        row_made = sem("row_made")
        row_in = sem("row_in")
        scored = sem("scored")
        exped = sem("exped")
        v_in = sem("v_in")
        pv_made = sem("pv_made")
        o_taken = sem("o_taken")
        o_turned = sem("o_turned")
        r_made = sem("r_made")
        o_made = sem("o_made")
        gate_sp, gate_pool = sem("gate_sp"), sem("gate_pool")
        ORDER = [(step[0], int(step[1]), int(step[2])) for step in (
            "v00 v10 m00 v20 v30 m01 q00 m02 q10 m03 m10 q20 m11 s00 l00 m12 s01 m13 "
            "s10 o00 m20 s11 m21 s20 m22 m23 s21 m30 s30 m31 m32 s31 m33").split()]
        w_view = dram["w_qrope"].rearrange("(c p) n -> p c n", p=P)
        block = own.enter_context(nc.Block())

        def run(engine, body):
            body(0, True, groups == 1)
            if groups > 2:
                with engine.Fori(1, groups - 1) as g:
                    body(g, False, False)
            if groups > 1:
                body(groups - 1, False, True)

        @block.sync
        def _(sp):
            def load_w(g):
                sp.dma_start(w_raw[:, :, :, :].rearrange("p c a n -> p c (a n)"),
                             w_view[:, :, bass.ds(g * 2 * P, 2 * P)]).then_inc(w_in, 16)

            def content(g, b):
                for tile, src in ((Q2, "content_q"), (K2, "content_k"), (KX, "content_k")):
                    rows = dram[src][bass.ds(g * GH, GH), :, b * S:(b + 1) * S].rearrange("h r t -> r h t")
                    sp.dma_start(tile[ROPE:KC0, b, :, :].bitcast(F32), rows).then_inc(content_in[b], 16)

            def copy_q(n, b):
                sp.wait_ge(q_high, 2 * n + 2)
                sp.dma_start(Q1[0:ROPE, b, :, :].bitcast(F32), Q2[0:ROPE, b, :, :].bitcast(F32)).then_inc(q_copied[b], 16)

            load_w(0)
            content(0, 0)
            content(0, 1)
            copy_q(0, 0)

            def body(g, first, last):
                for b in range(NB):
                    n = 2 * g + b
                    sp.wait_ge(row_made, n + 1)
                    sp.dma_start(Q2[MROW:MROW + 1, b, :, :].bitcast(F32), mrow[0:GH, :].bitcast(F32)).then_inc(row_in, 16)
                    if b == 0 and not last:
                        sp.wait_ge(w_split, 2 * g + 2)
                        sp.sem_inc(gate_sp, 1)
                        load_w(g + 1)
                    if not (last and b == 1):
                        copy_q(n + 1, 1 - b)
                    if not last:
                        sp.wait_ge(scored, 8 * (n + 1))
                        sp.sem_inc(gate_sp, 1)
                        content(g + 1, b)

            run(sp, body)

        @block.gpsimd
        def _(pool):
            def split_w(g, pair, first):
                if pair == 0:
                    pool.wait_ge(w_in, 16 * (g + 1))
                if not first:
                    pool.wait_ge(q_made, 4 * g - 1 + pair)
                    pool.sem_inc(gate_pool, 1)
                pool.tensor_copy(w_hi[:, :, pair, :], w_raw[:, :, pair, :]).then_inc(w_step, 1)
                pool.wait_ge(w_step, 2 * g + pair + 1)
                pool.tensor_tensor(w_lo[:, :, pair, :], w_raw[:, :, pair, :], w_hi[:, :, pair, :],
                                   ALU.subtract).then_inc(w_split, 1)

            def values(g, b, n, first):
                if not first:
                    pool.wait_ge(pv_made, n - 1)
                    pool.sem_inc(gate_pool, 1)
                pool.tensor_copy(V_slot[:, b, :, :, 0:HD0],
                                 V[:, b * ST:(b + 1) * ST, bass.ds(g * GH * HD0, GH * HD0)].rearrange(
                                     "p t (h d) -> p t h d", h=GH)).then_inc(v_in, 1)

            split_w(0, 0, True)
            split_w(0, 1, True)

            def body(g, first, last):
                values(g, 0, 2 * g, first)
                if not last:
                    split_w(g + 1, 0, False)
                values(g, 1, 2 * g + 1, first)
                if not last:
                    split_w(g + 1, 1, False)

            run(pool, body)

        @block.scalar
        def _(act):
            def high(n, b, pair):
                act.wait_ge(q_made, 2 * n + pair + 1)
                for k in range(2):
                    ins = act.activation(Q2[0:ROPE, b, 2 * pair + k, :], ps_x[k * ROPE:(k + 1) * ROPE, :], ACT.Copy)
                ins.then_inc(q_high, 1)

            def exp(n, j, half):
                act.wait_ge(scored, 8 * n + 2 * j + half + 1)
                act.activation(probs[:, j, 2 * half:2 * half + 2, :], ps_score[half][:, :, :], ACT.Exp,
                               scale=SCALE).then_inc(exped, 1)

            def take_o(n):
                act.wait_ge(pv_made, n + 1)
                act.activation(oT[:, :], ps_o[:, :], ACT.Copy).then_inc(o_taken, 1)

            for pair in range(2):
                high(0, 0, pair)

            def body(g, first, last):
                for b in range(NB):
                    n = 2 * g + b
                    more = not (last and b == 1)
                    if more:
                        high(n + 1, 1 - b, 0)
                    act.wait_ge(max_turned, n + 1)
                    if not (first and b == 0):
                        act.wait_ge(row_in, 16 * n)
                    act.activation(mrow[0:GH, :], ps_max[0][0:GH, :], ACT.Copy, scale=-1.0).then_inc(row_made, 1)
                    if not (first and b == 0):
                        take_o(n - 1)
                    for kind, j, k in ORDER:
                        if kind == "s":
                            exp(n, j, k)
                        if kind == "q" and j == 2 and more:
                            high(n + 1, 1 - b, 1)

            run(act, body)
            take_o(2 * groups - 1)

        @block.vector
        def _(dve):
            def low(n, b, pair):
                dve.wait_ge(q_high, 2 * n + pair + 1)
                for k in range(2):
                    ins = dve.tensor_tensor(Q1[ROPE:P, b, 2 * pair + k, :], ps_x[k * ROPE:(k + 1) * ROPE, :],
                                            Q2[0:ROPE, b, 2 * pair + k, :], ALU.subtract)
                ins.then_inc(q_low, 1)

            def take_max(n, j, t):
                dve.wait_ge(max_made, 16 * n + 4 * j + t + 1)
                dve.tensor_reduce(row_max[:, t, j:j + 1], ps_max[t % 2][:, :], axis=AXX, op=ALU.max)\
                   .then_inc(max_taken, 1)

            def normalise(g, b, n):
                dve.wait_ge(o_turned, n + 1)
                outs = ps_x[:, :].rearrange("p (t h m) -> p t h m", t=ST, h=GH)
                dve.reciprocal(recip[:, :, :, :], outs[:, :, :, HD0:HD0 + 1]).then_inc(r_made, 1)
                dve.wait_ge(r_made, n + 1)
                for t in range(ST):
                    ins = dve.tensor_tensor(O[:, b * ST + t, bass.ds(g * GH * HD0, GH * HD0)].rearrange(
                        "p (h d) -> p h d", h=GH), outs[:, t, :, 0:HD0],
                        recip[:, t, :, :].broadcast_to([P, GH, HD0]), ALU.mult)
                ins.then_inc(o_made, 1)

            for pair in range(2):
                low(0, 0, pair)
                for j in range(2 * pair, 2 * pair + 2):
                    for t in range(ST):
                        take_max(0, j, t)

            def body(g, first, last):
                for b in range(NB):
                    n = 2 * g + b
                    more = not (last and b == 1)
                    if more:
                        low(n + 1, 1 - b, 0)
                    for kind, j, t in ORDER:
                        if kind == "m" and more:
                            take_max(n + 1, j, t)
                        if kind == "l" and more:
                            low(n + 1, 1 - b, 1)
                        if kind == "o" and not (first and b == 0):
                            normalise(g - 1 + b, 1 - b, n - 1)

            run(dve, body)
            normalise(groups - 1, 1, 2 * groups - 1)
            dve.wait_ge(o_made, 2 * groups)

        @block.tensor
        def _(pe):
            def queries(g, b, n, pair, third):
                if b == 0 and third == 0:
                    pe.wait_ge(w_split, 2 * g + pair + 1)
                w, x = ((w_hi, "xh"), (w_lo, "xh"), (w_hi, "xl"))[third]
                for c in range(DC):
                    last = pe.matmul(ps_x[:, :], w[:, c, pair, :], sb[x][:, c, b * S:(b + 1) * S],
                                     start=third == c == 0, stop=third == 2 and c == DC - 1)
                if third == 2:
                    last.then_inc(q_made, 1)

            def max_scores(g, b, n, j, t, wait_free=True):
                if j % 2 == 0 and t == 0:
                    pe.wait_ge(q_high, 2 * n + j // 2 + 1)
                if j == 0 and t == 0:
                    pe.wait_ge(content_in[b], 48 * (g + 1))
                    if wait_free:
                        pe.wait_ge(row_made, n)
                if wait_free:
                    pe.wait_ge(max_taken, 16 * n + 4 * j + t - 1)
                pe.matmul(ps_max[t % 2][:, :], Q2[0:KC0, b, j, t * P:(t + 1) * P], KX[0:KC0, b, j, :],
                          start=True, stop=True).then_inc(max_made, 1)

            def scores(g, n, b, j, half, wait_free=True):
                if j == half == 0:
                    pe.wait_ge(q_low, 2 * n + 2)
                    pe.wait_ge(q_copied[b], 16 * (g + 1))
                    pe.wait_ge(row_in, 16 * (n + 1))
                if wait_free:
                    pe.wait_ge(exped, 8 * n + 2 * j + half - 1)
                for k in range(2):
                    t = 2 * half + k
                    pe.matmul(ps_score[half][:, k, :], K1[:, b, t * P:(t + 1) * P], Q1[:, b, j, :],
                              start=True, stop=False)
                    last = pe.matmul(ps_score[half][:, k, :], K2[0:MROW + 1, b, j, t * P:(t + 1) * P],
                                     Q2[0:MROW + 1, b, j, :], start=False, stop=True)
                last.then_inc(scored, 1)

            def outputs(n, b, t):
                if t == 0:
                    pe.wait_ge(exped, 8 * (n + 1))
                    pe.wait_ge(v_in, n + 1)
                for j in range(GH):
                    last = pe.matmul(ps_o[32 * j:32 * (j + 1), :], V_slot[:, b, t, j, :], probs[:, j, t, :],
                                     start=t == 0, stop=t == ST - 1)
                if t == ST - 1:
                    last.then_inc(pv_made, 1)

            def turn_o(n):
                pe.wait_ge(o_taken, n + 1)
                for t in range(ST):
                    last = pe.transpose(ps_x[:, t * P:(t + 1) * P], oT[:, t * P:(t + 1) * P], ident[:, :])
                last.then_inc(o_turned, 1)

            for pair in range(2):
                if pair:
                    pe.wait_ge(q_low, 1)
                for third in range(3):
                    queries(0, 0, 0, pair, third)
            for j in range(GH):
                for t in range(ST):
                    max_scores(0, 0, 0, j, t, wait_free=4 * j + t >= 2)

            def body(g, first, last):
                for b in range(NB):
                    n = 2 * g + b
                    more = not (last and b == 1)
                    before = not (first and b == 0)
                    if more:
                        if first:
                            pe.wait_ge(q_low, 2 * n + 2)
                        if not first:
                            pe.wait_ge(o_made, n - 1)
                        for third in range(3):
                            queries(g + b, 1 - b, n + 1, 0, third)
                    pe.wait_ge(max_taken, 16 * (n + 1))
                    for t in range(ST):
                        ins = pe.transpose(ps_max[0][0:GH, t * P:(t + 1) * P], row_max[:, t, :], ident[:, :])
                    ins.then_inc(max_turned, 1)
                    for kind, j, k in ORDER:
                        if kind == "v" and before:
                            outputs(n - 1, 1 - b, j)
                        if kind == "s":
                            scores(g, n, b, j, k, wait_free=before or j > 0)
                        if kind == "m" and more:
                            max_scores(g + b, 1 - b, n + 1, j, k)
                        if kind == "o" and before:
                            if more:
                                pe.wait_ge(q_low, 2 * n + 4)
                            else:
                                pe.wait_ge(o_made, n - 1)
                            turn_o(n - 1)
                        if kind == "q" and more:
                            if j == 0:
                                pe.wait_ge(q_low, 2 * n + 3)
                            queries(g + b, 1 - b, n + 1, 1, j)

            run(pe, body)
            for t in range(ST):
                outputs(2 * groups - 1, 1, t)
            pe.wait_ge(o_made, 2 * groups - 1)
            turn_o(2 * groups - 1)

EPS = 1e-5
HID = 1376
HT = 11
HP = HT * P
RANK = 16
LORA_SCALE = 2.0

NKV = 8
GQ = 4
NCL = 64
THRESHOLD = 0.01
TEMPERATURE = 0.1


def merge_heads_stage(nc, ctx, dram, sb):
    own = ExitStack()
    with own:
        def sem(name):
            return ctx.enter_context(nc.semaphore(name))

        X, ident = sb["X"], sb["ident"]
        x = own.enter_context(nc.sbuf_tensor("x_sb", [P, TT, D], F32))
        wo = own.enter_context(nc.sbuf_tensor("wo0_sb", [P, DC, D], F32))
        oT = own.enter_context(nc.sbuf_tensor("oT0", [P, 2, DC, P], F32))
        turned = [own.enter_context(nc.psum_tensor(f"turned{i}", [P, DC, P], F32)) for i in range(2)]
        made = [own.enter_context(nc.psum_tensor(f"made{i}", [P, D], F32)) for i in range(2)]
        loaded = sem("wo0_in")
        o_turned = sem("o0_turned")
        o_taken = sem("o0_taken")
        y_made = sem("y0_made")
        y_taken = sem("y0_taken")
        block = own.enter_context(nc.Block())

        @block.sync
        def _(sp):
            sp.dma_start(wo[:, :, :], dram["wo0"].rearrange("(c p) n -> p c n", p=P)).then_inc(loaded, 16)
            sp.dma_start(x[:, :, :], dram["x"].rearrange("(t p) n -> p t n", p=P)).then_inc(loaded, 16)

        @block.tensor
        def _(pe):
            def turn(t):
                if t >= 2:
                    pe.wait_ge(o_taken, t - 1)
                for c in range(DC):
                    last = pe.transpose(turned[t % 2][:, c, :], X[:, t, c * P:(c + 1) * P], ident[:, :])
                last.then_inc(o_turned, 1)

            turn(0)
            pe.wait_ge(loaded, 32)
            for t in range(TT):
                if t + 1 < TT:
                    turn(t + 1)
                pe.wait_ge(o_taken, t + 1)
                if t >= 2:
                    pe.wait_ge(y_taken, t - 1)
                for c in range(DC):
                    last = pe.matmul(made[t % 2][:, :], oT[:, t % 2, c, :], wo[:, c, :], start=c == 0, stop=c == DC - 1)
                last.then_inc(y_made, 1)

        @block.scalar
        def _(act):
            for t in range(TT):
                act.wait_ge(o_turned, t + 1)
                if t >= 2:
                    act.wait_ge(y_made, t - 1)
                act.activation(oT[:, t % 2, :, :], turned[t % 2][:, :, :], ACT.Copy).then_inc(o_taken, 1)

        @block.vector
        def _(dve):
            dve.wait_ge(loaded, 32)
            for t in range(TT):
                dve.wait_ge(y_made, t + 1)
                dve.tensor_tensor(X[:, t, :], made[t % 2][:, :], x[:, t, :], ALU.add).then_inc(y_taken, 1)
            dve.wait_ge(y_taken, TT)


def norm_stage(nc, ctx, name, sb, out=None, ahead=None):
    own = ExitStack()
    with own:
        def sem(s):
            return ctx.enter_context(nc.semaphore(name + s))

        X, ident = sb["X"], sb["ident"]
        stats = own.enter_context(nc.sbuf_tensor(name + "stats", [P, TT, 6], F32))
        moments = own.enter_context(nc.sbuf_tensor(name + "moments", [P, TT, 2], F32))
        dev = own.enter_context(nc.sbuf_tensor(name + "dev", [P, TT], F32))
        eps = own.enter_context(nc.sbuf_tensor(name + "eps", [P, 1], F32))
        turned = [own.enter_context(nc.psum_tensor(f"{name}turned{i}", [P, DC, P], F32)) for i in range(4)]
        eps_set = sem("eps_set")
        counted = sem("counted")
        mean_var = sem("mean_var")
        rooted = sem("rooted")
        inverse = sem("inverse")
        normed = sem("normed")
        x_turned = sem("x_turned")
        high = sem("high")
        low = sem("low")
        stored = sem("stored")
        block = own.enter_context(nc.Block())

        @block.vector
        def _(dve):
            dve.memset(eps[:, :], EPS).then_inc(eps_set, 1)
            for t in range(TT):
                dve.bn_stats(stats[:, t, :], X[:, t, :]).then_inc(counted, 1)
            for t in range(TT):
                dve.wait_ge(counted, t + 1)
                dve.bn_aggr(moments[:, t, :], stats[:, t, :]).then_inc(mean_var, 1)
            dve.wait_ge(rooted, 1)
            dve.reciprocal(dev[:, :], dev[:, :]).then_inc(inverse, 1)
            dve.wait_ge(inverse, 1)
            for t in range(TT):
                dve.tensor_scalar(X[:, t, :], X[:, t, :], moments[:, t, 0:1], dev[:, t:t + 1],
                                  ALU.subtract, ALU.mult).then_inc(normed, 1)
            if out is None:
                for t in range(TT):
                    dve.wait_ge(high, t + 1)
                    dve.tensor_tensor(sb["xl"][:, :, t * P:(t + 1) * P], turned[t % 4][:, :, :],
                                      sb["xh"][:, :, t * P:(t + 1) * P], ALU.subtract).then_inc(low, 1)
                dve.wait_ge(low, TT)

        @block.scalar
        def _(act):
            act.wait_ge(eps_set, 1)
            act.wait_ge(mean_var, TT)
            act.activation(dev[:, :], moments[:, :, 1], ACT.Sqrt, bias=eps[:, 0:1]).then_inc(rooted, 1)
            if out is None:
                for t in range(TT):
                    act.wait_ge(x_turned, t + 1)
                    act.activation(sb["xh"][:, :, t * P:(t + 1) * P], turned[t % 4][:, :, :], ACT.Copy)\
                       .then_inc(high, 1)

        @block.tensor
        def _(pe):
            if out is None:
                for t in range(TT):
                    pe.wait_ge(normed, t + 1)
                    if t >= 4:
                        pe.wait_ge(low, t - 3)
                    for c in range(DC):
                        last = pe.transpose(turned[t % 4][:, c, :], X[:, t, c * P:(c + 1) * P], ident[:, :])
                    last.then_inc(x_turned, 1)

        @block.sync
        def _(sp):
            if ahead is not None:
                ahead(sp)
            if out is not None:
                rows = out.rearrange("(t p) n -> p t n", p=P)
                for t in range(TT):
                    sp.wait_ge(normed, t + 1)
                    sp.dma_start(rows[:, t, :], X[:, t, :]).then_inc(stored, 16)
                sp.wait_ge(stored, 16 * TT)


RAW = 3
LR = 3 * 32


def swiglu_memory(nc, own, ctx):
    m = {}

    def buf(name, shape, dt=F32):
        m[name] = own.enter_context(nc.sbuf_tensor(name, shape, dt))

    buf("w13_hi", [P, 2, DC, HP], F32R)
    buf("w13_lo", [P, 2, DC, HP], F32R)
    buf("w2_sb", [P, HT, D])
    buf("w13_raw", [P, 2, HP])
    buf("lora_a", [LR, 2, D], F32R)
    buf("lora_b", [LR, 2, HP], F32R)
    buf("lora_a2", [LR, HP], F32R)
    buf("lora_b2", [LR, D], F32R)
    buf("gates", [P, 2, 2, S])
    late = m["w2_sb"][0:LR, :, :].rearrange("p m n -> p (m n)")
    m["raw_a"] = late[:, 0:2 * D].rearrange("p (i d) -> p i d", i=2)
    m["raw_b"] = late[:, 2 * D:2 * D + 2 * HP].rearrange("p (i h) -> p i h", i=2)
    m["raw_a2"] = late[:, 2 * D + 2 * HP:2 * D + 3 * HP]
    early = m["gates"][:, :, :, :].rearrange("p i k s -> p (i k s)")
    m["raw_b2"] = early[0:LR, HP:HP + D]
    m["raw"] = [m["w13_raw"][:, 0, :], m["w13_raw"][:, 1, :], early[:, 0:HP]]
    m["lora_in"] = ctx.enter_context(nc.semaphore("ffn_lora_in"))
    m["raw_in"] = [ctx.enter_context(nc.semaphore(f"ffn_raw_in{i}")) for i in range(RAW)]
    return m


def swiglu_load_step(sp, dram, m, s):
    i, c = s // DC, s % DC
    sp.dma_start(m["raw"][s % RAW], dram["w13"][i, c * P:(c + 1) * P, :]).then_inc(m["raw_in"][s % RAW], 16)


def swiglu_first_loads(sp, dram, m):
    sp.dma_start(m["raw_a"], dram["lora_a13"].rearrange("i r d -> r i d")).then_inc(m["lora_in"], 16)
    sp.dma_start(m["raw_b"], dram["lora_b13"].rearrange("i r h -> r i h")).then_inc(m["lora_in"], 16)
    sp.dma_start(m["raw_a2"], dram["lora_a2"]).then_inc(m["lora_in"], 16)
    sp.dma_start(m["raw_b2"], dram["lora_b2"]).then_inc(m["lora_in"], 16)
    for s in range(RAW):
        swiglu_load_step(sp, dram, m, s)


def swiglu_stage(nc, ctx, dram, sb, mem):
    own = ExitStack()
    with own:
        def sem(name):
            return ctx.enter_context(nc.semaphore("ffn_" + name))

        X, xh, xl = sb["X"], sb["xh"], sb["xl"]
        w_hi, w_lo, w2, raw = mem["w13_hi"], mem["w13_lo"], mem["w2_sb"], mem["raw"]
        lora_a, lora_b, a2, b2 = mem["lora_a"], mem["lora_b"], mem["lora_a2"], mem["lora_b2"]
        gate, g = mem["gates"][:, 0, :, :], mem["gates"][:, 1, :, :]
        lora_in, raw_in = mem["lora_in"], mem["raw_in"]
        w2_in = sem("w2_in")
        banks = [own.enter_context(nc.psum_tensor(f"ffn_ps{i}", [P, S], F32)) for i in range(8)]
        factors = [(mem["raw_a"], lora_a[:, :, :], 2),
                   (mem["raw_b"][:, 0, :], lora_b[:, 0, :], 1), (mem["raw_b"][:, 1, :], lora_b[:, 1, :], 1),
                   (mem["raw_a2"], a2[:, :], 2), (mem["raw_b2"], b2[:, :], 1)]
        factor_high = sem("factor_high")
        factor_low = sem("factor_low")
        delta = sem("delta")
        folded = sem("folded")
        w_high = sem("w_high")
        w_low = [sem(f"w_low{i}") for i in range(RAW)]
        hidden = sem("hidden")
        gated = sem("gated")
        g_made = sem("g_made")
        down = sem("down")
        taken = sem("taken")
        CUTS = [(0, 512), (512, 512), (1024, HP - 1024)]
        NC = len(CUTS)
        ONE = 1
        block = own.enter_context(nc.Block())
        steps = [(i, c) for i in range(2) for c in range(DC)]

        @block.sync
        def _(sp):
            for s in range(RAW, len(steps)):
                sp.wait_ge(w_low[s % RAW], s // RAW)
                swiglu_load_step(sp, dram, mem, s)
            sp.wait_ge(factor_low, 5)
            sp.dma_start(w2[:, :, :], dram["w2"].rearrange("(m p) n -> p m n", p=P)).then_inc(w2_in, 16)

        def low_part(engine, s):
            i, c = steps[s]
            engine.wait_ge(w_high, s + 1)
            engine.tensor_tensor(w_lo[:, i, c, :], raw[s % RAW], w_hi[:, i, c, :], ALU.subtract)\
                  .then_inc(w_low[s % RAW], 1)

        @block.gpsimd
        def _(pool):
            for s in range(1, len(steps), 2):
                low_part(pool, s)

        @block.scalar
        def _(act):
            def factor(k):
                act.activation(factors[k][1], factors[k][0], ACT.Copy).then_inc(factor_high, 1)

            act.wait_ge(lora_in, 64)
            for k in range(3):
                factor(k)
            for s, (i, c) in enumerate(steps):
                if s == 2:
                    factor(3)
                    factor(4)
                act.wait_ge(folded, NC * (s + 1))
                act.activation(w_hi[:, i, c, :], raw[s % RAW], ACT.Copy).then_inc(w_high, 1)
            with act.Fori(0, NB) as half:
                for m in range(HT):
                    act.wait_ge(hidden, half * HT + m + 1)
                    if m >= 2:
                        act.wait_ge(g_made, ONE + half * HT + m - 1)
                    else:
                        act.wait_ge(g_made, ONE + half * HT)
                    act.activation(gate[:, m % 2, :], banks[4 + m % 2][:, :], ACT.Silu).then_inc(gated, 1)

        @block.vector
        def _(dve):
            dve.sem_inc(g_made, ONE)
            dve.sem_inc(taken, ONE)

            def factor(k):
                source, parts, slot = factors[k]
                rows = slice(32 * slot, 32 * (slot + 1))
                dve.wait_ge(factor_high, k + 1)
                dve.tensor_tensor(parts[rows], source[rows], parts[rows], ALU.subtract).then_inc(factor_low, 1)

            factor(0)
            factor(1)
            for s, (i, c) in enumerate(steps):
                if s == 1:
                    factor(2)
                if s == 3:
                    factor(3)
                    factor(4)
                dve.wait_ge(raw_in[s % RAW], 16 * (s // RAW + 1))
                for k, (at, n) in enumerate(CUTS):
                    j = NC * s + k
                    dve.wait_ge(delta, j + 1)
                    dve.scalar_tensor_tensor(out=raw[s % RAW][:, at:at + n], in0=banks[j % 8][:, 0:n], scalar=LORA_SCALE,
                                             in1=raw[s % RAW][:, at:at + n], op0=ALU.mult, op1=ALU.add)\
                       .then_inc(folded, 1)
                if s % 2:
                    low_part(dve, s - 1)
            dve.wait_ge(w2_in, 16)
            for m in range(HT):
                j = NC * len(steps) + m
                dve.wait_ge(delta, j + 1)
                dve.scalar_tensor_tensor(out=w2[:, m, :], in0=banks[m % 4][:, :], scalar=LORA_SCALE,
                                         in1=w2[:, m, :], op0=ALU.mult, op1=ALU.add).then_inc(folded, 1)
            with dve.Fori(0, NB) as half:
                for m in range(HT):
                    dve.wait_ge(gated, half * HT + m + 1)
                    if m >= 2:
                        dve.wait_ge(down, ONE + half * HT + m - 1)
                    else:
                        dve.wait_ge(down, ONE + half * HT)
                    dve.tensor_tensor(g[:, m % 2, :], banks[6 + m % 2][:, :], gate[:, m % 2, :], ALU.mult)\
                       .then_inc(g_made, 1)
                dve.wait_ge(down, ONE + (half + 1) * HT)
                for t in range(ST):
                    row = X[:, bass.ds(half * ST + t, 1), :].rearrange("p a n -> p (a n)")
                    dve.tensor_tensor(row, banks[t][:, :], row, ALU.add).then_inc(taken, 1)
            dve.wait_ge(taken, ONE + TT)

        @block.tensor
        def _(pe):
            pe.sem_inc(down, ONE)
            j = 0
            for i, c in steps:
                if c == 0:
                    pe.wait_ge(factor_low, i + 2)
                for at, n in CUTS:
                    if j >= 8:
                        pe.wait_ge(folded, j - 7)
                    pe.matmul(banks[j % 8][:, 0:n], lora_a[:, i, c * P:(c + 1) * P], lora_b[:, i, at:at + n],
                              start=True, stop=True).then_inc(delta, 1)
                    j += 1
            pe.wait_ge(factor_low, 5)
            for m in range(HT):
                pe.wait_ge(folded, NC * len(steps) if m < 4 else j - 3)
                pe.matmul(banks[m % 4][:, :], a2[:, m * P:(m + 1) * P], b2[:, :], start=True, stop=True)\
                  .then_inc(delta, 1)
                j += 1
            for k in range(RAW):
                pe.wait_ge(w_low[k], len(steps[k::RAW]))

            def project(half, m):
                if m >= 2:
                    pe.wait_ge(g_made, ONE + half * HT + m - 1)
                else:
                    pe.wait_ge(g_made, ONE + half * HT)
                for i in range(2):
                    k = 0
                    for w, x in ((w_hi, xh), (w_lo, xh), (w_hi, xl)):
                        for c in range(DC):
                            last = pe.matmul(banks[4 + 2 * i + m % 2][:, :], w[:, i, c, m * P:(m + 1) * P],
                                             x[:, c, bass.ds(half * S, S)], start=k == 0, stop=k == 3 * DC - 1)
                            k += 1
                last.then_inc(hidden, 1)

            with pe.Fori(0, NB) as half:
                project(half, 0)
                pe.wait_ge(taken, ONE + half * ST)
                for m in range(HT):
                    if m + 1 < HT:
                        project(half, m + 1)
                    pe.wait_ge(g_made, ONE + half * HT + m + 1)
                    if m == 0:
                        pe.wait_ge(folded, NC * len(steps) + HT)
                    for t in range(ST):
                        last = pe.matmul(banks[t][:, :], g[:, m % 2, t * P:(t + 1) * P], w2[:, m, :],
                                         start=m == 0, stop=m == HT - 1)
                    last.then_inc(down, 1)


def gqa_stage(nc, ctx, dram, sb):
    own = ExitStack()
    with own:
        def buf(name, shape, dt=F32):
            return own.enter_context(nc.sbuf_tensor(name, shape, dt))

        def psum(name, shape):
            return own.enter_context(nc.psum_tensor(name, shape, F32))

        def sem(name):
            return ctx.enter_context(nc.semaphore("gqa_" + name))

        X, xh, xl, ident = sb["X"], sb["xh"], sb["xl"], sb["ident"]
        NU = GQ * NB
        wq_raw = buf("wq_raw", [P, GQ, DC, P])
        wkv_raw = buf("wkv_raw", [P, 2, DC, P])
        wo_raw = buf("wo_raw", [P, GQ, D])
        wq = [buf(f"wq_{k}", [P, GQ, DC, P], F32R) for k in ("hi", "lo")]
        wkv = [buf(f"wkv_{k}", [P, 2, DC, P], F32R) for k in ("hi", "lo")]
        wo = [buf(f"wo_{k}", [P, GQ, D], F32R) for k in ("hi", "lo")]
        K = [buf(f"k_{k}", [P, NB, S], F32R) for k in ("hi", "lo")]
        Q = [buf(f"q_{k}", [P, 2, S], F32R) for k in ("hi", "lo")]
        V = buf("v1", [P, NB, ST, P])
        tables = buf("tables", [P, 4, S])
        by_sin = buf("by_sin", [P, S])
        roped = buf("roped", [P, 2, S])
        probs = buf("probs1", [P, 2, ST, S])
        probsT = buf("probsT", [P, 3, S])
        O = [buf(f"o_{k}", [P, NB, GQ, S], F32R) for k in ("hi", "lo")]
        minus_max = buf("minus_max", [P, ST])
        sums = buf("sums", [P, 2, ST])
        inverse = buf("inverse", [P, ST])
        mask = buf("mask_sb", [P, 2, P], F32R)
        mask_raw = buf("mask_raw", [P, 2, P])
        ps_s = [psum(f"ps_s{i}", [P, S]) for i in range(3)]
        place = {3: (0, 0), 2: (1, 0), 0: (1, 3 * P), 1: (2, 0)}
        ps_t = [psum(f"ps_t{i}", [P, S]) for i in range(2)]
        ps_r = [psum(f"ps_r{i}", [P, S]) for i in range(2)]
        ps_o = psum("ps_o1", [P, S])
        pieces = [[(0, 0)], [(1, 0), (3, 3 * P)], [(2, 0)]]

        tables_in = sem("tables_in")
        mask_set = sem("mask_set")
        wqkv_in = sem("wqkv_in")
        wo_in = sem("wo_in")
        step = sem("step")
        wkv_split = sem("wkv_split")
        wq_split = sem("wq_split")
        wo_split = sem("wo_split")
        made = sem("made")
        taken = sem("taken")
        v_taken = sem("v_taken")
        v_turned = sem("v_turned")
        v_ready = sem("v_ready")
        summed = sem("summed")
        r_high = sem("r_high")
        r_low = sem("r_low")
        scored = sem("scored")
        maxed = sem("maxed")
        exped = sem("exped")
        inverted = sem("inverted")
        normed = sem("normed")
        turned = sem("turned")
        t_taken = sem("t_taken")
        pv_made = sem("pv_made")
        o_high = sem("o_high")
        o_low = sem("o_low")
        gate_sp, gate_pool = sem("gate_sp"), sem("gate_pool")
        START, PER, TAKEN = 4, 3 * NU - 4, 3 * NU - 6

        def ring_query(u): return u
        def ring_next(k): return NU + k
        def ring_out(last, j): return (NU if last else NU + 4) + j
        def take_query(u): return u - 2
        def take_next(k): return NU - 2 + k
        def take_out(last, j): return (NU - 2 if last else NU + 2) + j
        ONE = 1
        RP = NU + 2

        block = own.enter_context(nc.Block())

        def run(engine, body):
            with engine.Fori(0, NKV - 1) as kv:
                body(kv, False)
            body(NKV - 1, True)

        @block.sync
        def _(sp):
            def load_qkv(kv):
                sp.dma_start(wkv_raw[:, :, :, :], dram["wkv1"][bass.ds(kv, 1), :, :, :, :].rearrange(
                    "a p i c n -> (a p) i c n")).then_inc(wqkv_in, 16)
                sp.dma_start(wq_raw[:, :, :, :], dram["wq1"][bass.ds(kv, 1), :, :, :, :].rearrange(
                    "a p h c n -> (a p) h c n")).then_inc(wqkv_in, 16)

            def load_wo(kv):
                sp.dma_start(wo_raw[:, :, :], dram["wo1"][bass.ds(kv, 1), :, :, :].rearrange(
                    "a p h n -> (a p) h n")).then_inc(wo_in, 16)

            load_qkv(0)
            sp.dma_start(tables[:, :, :], dram["tables"].rearrange("i p s -> p i s")).then_inc(tables_in, 16)
            load_wo(0)

            def body(kv, last):
                if not last:
                    sp.wait_ge(wkv_split, 2 * (kv + 1))
                    sp.sem_inc(gate_sp, 1)
                    sp.wait_ge(wq_split, GQ * (kv + 1))
                    sp.sem_inc(gate_sp, 1)
                    load_qkv(kv + 1)
                    sp.wait_ge(wo_split, GQ * (kv + 1))
                    sp.sem_inc(gate_sp, 1)
                    load_wo(kv + 1)

            run(sp, body)

        @block.gpsimd
        def _(pool):
            pool.memset(mask_raw[:, :, :], 0.0).then_inc(mask_set, 1)
            pool.wait_ge(mask_set, 1)
            pool.affine_select(out=mask_raw[:, 0, :], in_=mask_raw[:, 0, :], compare_op=ALU.not_equal, fill=1.0,
                               base=0, pattern=[[-1, P]], channel_multiplier=1).then_inc(mask_set, 1)
            pool.affine_select(out=mask_raw[:, 1, :], in_=mask_raw[:, 1, :], compare_op=ALU.is_ge, fill=-1e30,
                               base=0, pattern=[[-1, P]], channel_multiplier=1).then_inc(mask_set, 1)
            pool.wait_ge(mask_set, 3)
            pool.tensor_copy(mask[:, :, :], mask_raw[:, :, :]).then_inc(mask_set, 1)

            def split(parts, raw, count, at_step):
                pool.sem_inc(gate_pool, 1)
                hi, lo = parts
                pool.tensor_copy(hi, raw).then_inc(step, 1)
                pool.wait_ge(step, at_step)
                pool.tensor_tensor(lo, raw, hi, ALU.subtract).then_inc(count, 1)

            EACH = 2 + 2 * GQ

            def split_kv(i, at_step):
                split([w[:, i, :, :] for w in wkv], wkv_raw[:, i, :, :], wkv_split, at_step)

            def split_q(h, at_step):
                split([w[:, h, :, :] for w in wq], wq_raw[:, h, :, :], wq_split, at_step)

            def split_o(h, at_step):
                split([w[:, h, :] for w in wo], wo_raw[:, h, :], wo_split, at_step)

            def rope(n, at, parts):
                pool.wait_ge(summed, n + 1)
                pool.sem_inc(gate_pool, 1)
                pool.tensor_copy(parts[0], roped[:, at, :]).then_inc(r_high, 1)
                pool.wait_ge(r_high, n + 1)
                pool.tensor_tensor(parts[1], roped[:, at, :], parts[0], ALU.subtract).then_inc(r_low, 1)

            def rope_key(n, b):
                rope(n, 0, [k[:, b, :] for k in K])

            def rope_query(n, u, at):
                rope(n, at, [q[:, u % 2, :] for q in Q])

            pool.wait_ge(wqkv_in, 32)
            split_kv(0, 1)
            split_q(0, 2)
            for b in range(NB):
                rope_key(2 * b, b)
                rope_query(2 * b + 1, b, 1)
            split_kv(1, 3)
            for h in range(1, GQ):
                split_q(h, 3 + h)

            def body(kv, last):
                r = START + RP * kv
                s = 2 + GQ + EACH * kv
                n = 0
                after = {2: ("o", 0), 3: ("kv", 0), 4: ("q", 0), 5: ("o", 1), 6: ("o", 2), 7: ("o", 3)}
                for u in range(2, NU):
                    pool.wait_ge(scored, NU * kv + u - 1)
                    rope_query(r + u - 2, u, u % 2)
                    if u == 2:
                        pool.wait_ge(wo_in, 16 * (kv + 1))
                        pool.sem_inc(gate_pool, 1)
                        pool.wait_ge(made, START + PER * kv)
                    if u == 3 and not last:
                        pool.wait_ge(wqkv_in, 32 * (kv + 2))
                    kind, h = after[u]
                    if kind == "o" or not last:
                        n += 1
                        {"o": split_o, "kv": split_kv, "q": split_q}[kind](h, s + n)
                if not last:
                    for b in range(NB):
                        pool.wait_ge(scored, NU * kv + NU - 1 + b)
                        rope_key(r + NU - 2 + 2 * b, b)
                        rope_query(r + NU - 1 + 2 * b, b, 1)
                        if b == 0:
                            split_kv(1, s + n + 1)
                    for h in range(1, GQ):
                        split_q(h, s + n + 1 + h)

            run(pool, body)

        @block.scalar
        def _(act):
            def values(kv, b):
                act.wait_ge(made, START + PER * kv + b + 1)
                act.activation(probsT[:, b, :], ps_r[(START + b) % 2][:, :], ACT.Copy).then_inc(v_taken, 1)

            def turned_values(kv, b):
                act.wait_ge(v_turned, NB * kv + b + 1)
                act.activation(V[:, b, :, :], ps_t[b][:, :].rearrange("p (t n) -> p t n", t=ST), ACT.Copy)\
                   .then_inc(v_ready, 1)

            def softmax(i, u):
                for k, t in enumerate((3, 2, 0, 1)):
                    act.wait_ge(maxed, ST * i + (3 if k == 1 else k + 1))
                    bank, at = place[t]
                    n = (t + 1) * P
                    act.activation(probs[:, u % 2, t, 0:n], ps_s[bank][:, at:at + n], ACT.Exp,
                                   bias=minus_max[:, t:t + 1], accum_out=sums[:, u % 2, t:t + 1]).then_inc(exped, 1)

            def take_turned(kv, u, k):
                act.wait_ge(turned, 3 * (NU * kv + u) + k + 1)
                n = S if k < 2 else 2 * P
                act.activation(probsT[:, k, 0:n], ps_t[(u + k) % 2][:, 0:n], ACT.Copy).then_inc(t_taken, 1)

            def take_outputs(kv, u):
                i = NU * kv + u
                act.wait_ge(pv_made, i + 1)
                act.activation(O[0][:, u % 2, u // 2, :], ps_o[:, :], ACT.Copy).then_inc(o_high, 1)

            act.sem_inc(exped, ONE)
            def body(kv, last):
                i = NU * kv
                softmax(i, 0)
                values(kv, 0)
                values(kv, 1)
                turned_values(kv, 0)
                turned_values(kv, 1)
                for u in range(1, NU):
                    take_turned(kv, u - 1, 0)
                    take_turned(kv, u - 1, 1)
                    softmax(i + u, u)
                    take_turned(kv, u - 1, 2)
                    take_outputs(kv, u - 1)
                for k in range(3):
                    take_turned(kv, NU - 1, k)
                take_outputs(kv, NU - 1)

            run(act, body)

        @block.vector
        def _(dve):
            def rope(n, ring, bank, keys, take, at, first=False, second=False):
                dve.wait_ge(made, ring + 1)
                if not first:
                    dve.wait_ge(summed, n)
                if not first and not second:
                    dve.wait_ge(r_low, n - 1)
                cos, sin = tables[:, 2 * keys, :], 2 * keys + 1
                ps = ps_r[bank]
                h = P // 2
                dve.tensor_tensor(by_sin[0:h, :], ps[h:P, :], tables[0:h, sin, :], ALU.mult)
                dve.tensor_tensor(by_sin[h:P, :], ps[0:h, :], tables[h:P, sin, :], ALU.mult)
                dve.tensor_tensor(roped[:, at, :], ps[:, :], cos, ALU.mult).then_inc(taken, 1)
                dve.wait_ge(taken, take + 1)
                dve.tensor_tensor(roped[:, at, :], roped[:, at, :], by_sin[:, :], ALU.add).then_inc(summed, 1)

            def maxima(i, u):
                for k, t in enumerate((3, 2, 0, 1)):
                    if k == 0:
                        dve.wait_ge(scored, i + 1)
                    bank, at = place[t]
                    dve.tensor_reduce(minus_max[:, t:t + 1], ps_s[bank][:, at:at + (t + 1) * P], axis=AXX, op=ALU.max,
                                      negate=True).then_inc(maxed, 1)

            def normalise(i, u):
                dve.wait_ge(exped, ONE + ST * (i + 1))
                dve.reciprocal(inverse[:, :], sums[:, u % 2, :]).then_inc(inverted, 1)
                dve.wait_ge(inverted, i + 1)
                for t in range(ST):
                    n = (t + 1) * P
                    ins = dve.tensor_scalar(probs[:, u % 2, t, 0:n], probs[:, u % 2, t, 0:n], inverse[:, t:t + 1],
                                            None, ALU.mult)
                ins.then_inc(normed, 1)

            def low_o(i, u):
                dve.wait_ge(o_high, i + 1)
                dve.tensor_tensor(O[1][:, u % 2, u // 2, :], ps_o[:, :], O[0][:, u % 2, u // 2, :], ALU.subtract)\
                   .then_inc(o_low, 1)

            dve.sem_inc(o_low, ONE)
            dve.wait_ge(tables_in, 16)
            for n in range(START):
                rope(n, n, n % 2, 1 - n % 2, n, n % 2, n == 0, n == 1)

            def body(kv, last):
                r = START + RP * kv
                ring = START + PER * kv
                tk = START + TAKEN * kv
                i = NU * kv

                def add_out(j):
                    at = ring_out(last, j)
                    dve.wait_ge(made, ring + at + 1)
                    dve.tensor_tensor(X[:, j, :], ps_r[(START + at) % 2][:, :], X[:, j, :], ALU.add).then_inc(taken, 1)

                maxima(i, 0)
                normalise(i, 0)
                rope(r, ring + ring_query(2), (START + ring_query(2)) % 2, 0, tk, 0)
                for u in range(1, NU):
                    maxima(i + u, u)
                    normalise(i + u, u)
                    if u < NU - 2:
                        rope(r + u, ring + ring_query(u + 2), (START + ring_query(u + 2)) % 2, 0, tk + u, u % 2)
                        low_o(i + u - 1, u - 1)
                    else:
                        for k in range(2) if not last else ():
                            at = 2 * (u % 2) + k
                            rope(r + NU - 2 + at, ring + ring_next(at), (START + ring_next(at)) % 2, 1 - k, tk + take_next(at), k)
                        low_o(i + u - 1, u - 1)
                add_out(0)
                add_out(1)
                low_o(i + NU - 1, NU - 1)
                for j in range(2, TT):
                    add_out(j)

            run(dve, body)
            dve.wait_ge(taken, TAKEN * NKV)

        @block.tensor
        def _(pe):
            TERMS = ((0, 0), (1, 0), (0, 1))
            x = (xh, xl)

            def project(w, sl, b, bank):
                k = 0
                for i, j in TERMS:
                    for c in range(DC):
                        last = pe.matmul(ps_r[bank][:, :], w[i][:, sl, c, :], x[j][:, c, b * S:(b + 1) * S],
                                         start=k == 0, stop=k == 3 * DC - 1)
                        k += 1
                last.then_inc(made, 1)

            def turn_values(kv, b):
                pe.wait_ge(v_taken, NB * kv + b + 1)
                for t in range(ST):
                    last = pe.transpose(ps_t[b][:, t * P:(t + 1) * P], probsT[:, b, t * P:(t + 1) * P], ident[:, :])
                last.then_inc(v_turned, 1)

            def scores(i, u, rope):
                b = u % 2
                pe.wait_ge(r_low, rope + 1)
                pe.wait_ge(exped, ONE + ST * i)
                for t in (3, 2, 0, 1):
                    bank, at = place[t]
                    n = (t + 1) * P
                    out = ps_s[bank][:, at:at + n]
                    for k, (q, kk) in enumerate(TERMS):
                        pe.matmul(out, Q[q][:, b, t * P:(t + 1) * P], K[kk][:, b, 0:n], start=k == 0, stop=False)
                    last = pe.matmul(ps_s[bank][:, at + n - P:at + n], mask[:, 0, :], mask[:, 1, :],
                                     start=False, stop=True)
                last.then_inc(scored, 1)

            def turn(i, u, k):
                if k == 0:
                    pe.wait_ge(normed, i + 1)
                if k == 2:
                    pe.wait_ge(t_taken, 3 * i + 1)
                for tile, at in pieces[k]:
                    for t in range(tile, ST):
                        last = pe.transpose(ps_t[(u + k) % 2][:, at + (t - tile) * P:at + (t - tile + 1) * P],
                                            probs[:, u % 2, t, tile * P:(tile + 1) * P], ident[:, :])
                last.then_inc(turned, 1)

            def outputs(i, u):
                b = u % 2
                pe.wait_ge(o_low, ONE + i)
                for k, piece in enumerate(pieces):
                    pe.wait_ge(t_taken, 3 * i + k + 1)
                    for tile, at in piece:
                        last = pe.matmul(ps_o[:, tile * P:S], V[:, b, tile, :], probsT[:, k, at:at + S - tile * P],
                                         start=tile == 0, stop=k == 2)
                last.then_inc(pv_made, 1)

            def merge(last, tk, j):
                at = ring_out(last, j)
                pe.wait_ge(taken, tk + take_out(last, j) - 1)
                k = 0
                for o, w in TERMS:
                    for h in range(GQ):
                        ins = pe.matmul(ps_r[(START + at) % 2][:, :],
                                        O[o][:, j // ST, h, (j % ST) * P:(j % ST + 1) * P], wo[w][:, h, :],
                                        start=k == 0, stop=k == 3 * GQ - 1)
                        k += 1
                ins.then_inc(made, 1)

            pe.wait_ge(mask_set, 4)
            pe.wait_ge(wkv_split, 1)
            project(wkv, 0, 0, 0)
            pe.wait_ge(wq_split, 1)
            project(wq, 0, 0, 1)
            pe.wait_ge(taken, 1)
            project(wkv, 0, 1, 0)
            pe.wait_ge(taken, 2)
            project(wq, 0, 1, 1)

            def body(kv, last):
                tk = START + TAKEN * kv
                r = START + RP * kv
                i = NU * kv

                def query(u):
                    pe.wait_ge(wq_split, GQ * kv + u // 2 + 1)
                    if u < 4:
                        pe.wait_ge(v_taken, 2 * kv + u - 1)
                    else:
                        pe.wait_ge(taken, tk + take_query(u) - 1)
                    project(wq, u // 2, u % 2, (START + ring_query(u)) % 2)

                scores(i, 0, r - 3)
                pe.wait_ge(wkv_split, 2 * kv + 2)
                for b in range(NB):
                    pe.wait_ge(taken, tk + b - 1)
                    project(wkv, 1, b, (START + b) % 2)
                query(2)
                for b in range(NB):
                    turn_values(kv, b)
                for u in range(1, NU):
                    scores(i + u, u, r + u - 2)
                    if u == 1:
                        pe.wait_ge(v_ready, NB * (kv + 1))
                    turn(i + u - 1, u - 1, 0)
                    turn(i + u - 1, u - 1, 1)
                    if u < NU - 2:
                        query(u + 2)
                    elif not last:
                        b = u % 2
                        pe.wait_ge(wkv_split, 2 * kv + 3)
                        pe.wait_ge(taken, tk + take_next(2 * b) - 1)
                        project(wkv, 0, b, (START + ring_next(2 * b)) % 2)
                        pe.wait_ge(wq_split, GQ * (kv + 1) + 1)
                        pe.wait_ge(taken, tk + take_next(2 * b + 1) - 1)
                        project(wq, 0, b, (START + ring_next(2 * b + 1)) % 2)
                    turn(i + u - 1, u - 1, 2)
                    outputs(i + u - 1, u - 1)
                for k in range(3):
                    turn(i + NU - 1, NU - 1, k)
                pe.wait_ge(wo_split, GQ * (kv + 1))
                pe.wait_ge(o_low, ONE + i + NU - 1)
                merge(last, tk, 0)
                merge(last, tk, 1)
                outputs(i + NU - 1, NU - 1)
                merge(last, tk, 2)
                merge(last, tk, 3)
                pe.wait_ge(o_low, ONE + i + NU)
                for j in range(ST, TT):
                    merge(last, tk, j)

            run(pe, body)


def cluster_stage(nc, ctx, dram, sb):
    own = ExitStack()
    with own:
        def buf(name, shape, dt=F32):
            return own.enter_context(nc.sbuf_tensor(name, shape, dt))

        def sem(name):
            return ctx.enter_context(nc.semaphore("cl_" + name))

        X, xh, xl = sb["X"], sb["xh"], sb["xl"]
        w = buf("w_dense", [P, DC, D])
        wh = buf("w_dense_hi", [P, DC, D], F32R)
        wl = buf("w_dense_lo", [P, DC, D], F32R)
        cent = buf("cent", [P, DC, NCL])
        ch = buf("cent_hi", [P, DC, NCL], F32R)
        cl = buf("cent_lo", [P, DC, NCL], F32R)
        bias = buf("bias_sb", [1, D])
        ones = buf("ones_sb", [P, P])
        assign_i = buf("assign_i", [NCL, D], mybir.dt.int32)
        assign = buf("assign", [NCL, D])
        which = buf("which", [NCL, 1])
        onehot = buf("onehot", [NCL, D])
        chosen = buf("chosen", [NCL, 1])
        soft = buf("soft", [P, TT, NCL])
        top = buf("top", [P, TT, 1])
        total = buf("total", [P, TT, 1])
        query = buf("query", [P, TT])
        any_hit = buf("any_hit", [P, NCL])
        column = buf("column", [P, D])
        dense = buf("dense", [P, 2, D])
        ps_l = own.enter_context(nc.psum_tensor("ps_l", [P, TT, NCL], F32))
        ps_c = own.enter_context(nc.psum_tensor("ps_c", [P, D], F32))
        ps_h = own.enter_context(nc.psum_tensor("ps_h", [P, D], F32))
        ps_d = [own.enter_context(nc.psum_tensor(f"ps_d{i}", [P, D], F32)) for i in range(4)]
        cent_in, w_in, small_in = sem("cent_in"), sem("w_in"), sem("small_in")
        ones_set = sem("ones_set")
        which_set = sem("which_set")
        step = sem("step")
        logits = sem("logits")
        shifted = sem("shifted")
        exped = sem("exped")
        hits_done = sem("hits_done")
        cent_done = sem("cent_done")
        w_done = sem("w_done")
        counted = sem("counted")
        onehot_done = sem("onehot_done")
        column_made = sem("column_made")
        made = sem("made")
        taken = sem("taken")
        added = sem("added")
        block = own.enter_context(nc.Block())

        @block.sync
        def _(sp):
            sp.dma_start(cent[:, :, :], dram["centroids"].rearrange("(c p) n -> p c n", p=P)).then_inc(cent_in, 16)
            sp.dma_start(w[:, :, :], dram["w_dense"].rearrange("(c p) n -> p c n", p=P)).then_inc(w_in, 16)
            sp.dma_start(assign_i[:, :], dram["assignments"].partition_broadcast(NCL)).then_inc(small_in, 16)
            sp.dma_start(bias[:, :], dram["bias"].rearrange("(a n) -> a n", a=1)).then_inc(small_in, 16)

        @block.gpsimd
        def _(pool):
            pool.memset(ones[:, :], 1.0).then_inc(ones_set, 1)
            pool.iota(which[:, :], pattern=[[0, 1]], base=0, channel_multiplier=1,
                      allow_small_or_imprecise_dtypes=True).then_inc(which_set, 1)

        @block.scalar
        def _(act):
            act.wait_ge(w_in, 16)
            act.activation(wh[:, :, :], w[:, :, :], ACT.Copy).then_inc(w_done, 1)
            act.wait_ge(shifted, 1)
            act.activation(soft[:, :, :], soft[:, :, :], ACT.Exp, scale=1.0 / TEMPERATURE).then_inc(exped, 1)

        @block.vector
        def _(dve):
            n = [0]

            def after(ins):
                n[0] += 1
                ins.then_inc(step, 1)
                dve.wait_ge(step, n[0])

            dve.wait_ge(cent_in, 16)
            after(dve.tensor_copy(ch[:, :, :], cent[:, :, :]))
            dve.tensor_tensor(cl[:, :, :], cent[:, :, :], ch[:, :, :], ALU.subtract).then_inc(cent_done, 1)
            dve.wait_ge(w_done, 1)
            dve.tensor_tensor(wl[:, :, :], w[:, :, :], wh[:, :, :], ALU.subtract).then_inc(w_done, 1)
            dve.wait_ge(small_in, 32)
            after(dve.tensor_copy(assign[:, :], assign_i[:, :]))
            dve.wait_ge(logits, 1)
            after(dve.tensor_reduce(top[:, :, 0], ps_l[:, :, :], axis=AXX, op=ALU.max))
            dve.tensor_tensor(soft[:, :, :], ps_l[:, :, :], top[:, :, :].broadcast_to([P, TT, NCL]),
                              ALU.subtract).then_inc(shifted, 1)
            dve.wait_ge(exped, 1)
            after(dve.tensor_reduce(total[:, :, 0], soft[:, :, :], axis=AXX, op=ALU.add))
            after(dve.reciprocal(total[:, :, 0], total[:, :, 0]))
            after(dve.tensor_tensor(soft[:, :, :], soft[:, :, :], total[:, :, :].broadcast_to([P, TT, NCL]), ALU.mult))
            after(dve.tensor_scalar(soft[:, :, :], soft[:, :, :], THRESHOLD, None, ALU.is_gt))
            dve.tensor_reduce(query[:, :], soft[:, :, :], axis=AXX, op=ALU.max)
            dve.tensor_reduce(any_hit[:, :], soft[:, :, :].rearrange("p t n -> p n t"), axis=AXX, op=ALU.max)\
               .then_inc(hits_done, 1)
            dve.wait_ge(counted, 1)
            after(dve.tensor_scalar(chosen[:, :], ps_c[0:NCL, 0:1], 0.5, None, ALU.is_gt))
            dve.wait_ge(which_set, 1)
            dve.tensor_scalar(onehot[:, :], assign[:, :], which[:, 0:1], chosen[:, 0:1], ALU.is_equal, ALU.mult)\
               .then_inc(onehot_done, 1)
            dve.wait_ge(column_made, 1)
            after(dve.tensor_copy(column[:, :], ps_h[:, :]))
            for t in range(TT):
                dve.wait_ge(made, t + 1)
                dve.scalar_tensor_tensor(out=dense[:, t % 2, :], in0=ps_d[t % 4][:, :], scalar=query[:, t:t + 1],
                                         in1=column[:, :], op0=ALU.mult, op1=ALU.mult).then_inc(taken, 1)
                dve.wait_ge(taken, t + 1)
                dve.tensor_tensor(X[:, t, :], X[:, t, :], dense[:, t % 2, :], ALU.add).then_inc(added, 1)
            dve.wait_ge(added, TT)

        @block.tensor
        def _(pe):
            TERMS = ((0, 0), (1, 0), (0, 1))
            x = (xh, xl)

            def product(out, t, w):
                k = 0
                for i, j in TERMS:
                    for c in range(DC):
                        last = pe.matmul(out, x[i][:, c, t * P:(t + 1) * P], w[j][:, c, :], start=k == 0,
                                         stop=k == 3 * DC - 1)
                        k += 1
                return last

            pe.wait_ge(cent_done, 1)
            for t in range(TT):
                last = product(ps_l[:, t, :], t, (ch, cl))
            last.then_inc(logits, 1)
            pe.wait_ge(w_done, 2)
            pe.wait_ge(small_in, 32)
            pe.wait_ge(ones_set, 1)

            def dense_tile(t):
                if t >= 4:
                    pe.wait_ge(taken, t - 3)
                pe.matmul(ps_d[t % 4][:, :], ones[0:1, :], bias[:, :], start=True, stop=False)
                k = 0
                for i, j in TERMS:
                    for c in range(DC):
                        last = pe.matmul(ps_d[t % 4][:, :], x[i][:, c, t * P:(t + 1) * P], (wh, wl)[j][:, c, :],
                                         start=False, stop=k == 3 * DC - 1)
                        k += 1
                last.then_inc(made, 1)

            for t in range(4):
                dense_tile(t)
            pe.wait_ge(hits_done, 1)
            pe.matmul(ps_c[0:NCL, 0:1], any_hit[:, :], ones[:, 0:1], start=True, stop=True).then_inc(counted, 1)
            pe.wait_ge(onehot_done, 1)
            pe.matmul(ps_h[:, :], ones[0:NCL, :], onehot[:, :], start=True, stop=True).then_inc(column_made, 1)
            for t in range(4, TT):
                dense_tile(t)


def program(nc, dram, out):
    for name in ("content_q", "content_k"):
        dram[name] = nc.dram_tensor(name, (NH0, CROWS, T), F32, kind="Internal").ap()
    with ExitStack() as ctx:
        def keep(stack, name, shape, dt=F32):
            sb[name] = stack.enter_context(nc.sbuf_tensor(name, shape, dt))

        sb = {}
        keep(ctx, "ident", [P, P])
        keep(ctx, "X", [P, TT, D])
        keep(ctx, "xh", [P, DC, T], F32R)
        keep(ctx, "xl", [P, DC, T], F32R)
        with ExitStack() as layer:
            for name in ("Q1", "Q2", "K2", "KX"):
                keep(layer, name, [P, NB, GH, S], F32R)
            keep(layer, "K1", [P, NB, S], F32R)
            keep(layer, "V", [P, TT, D])
            keep(layer, "V_slot", [P, NB, ST, GH, 32])
            keep(layer, "mrow", [GH, S], F32R)
            latent_stage(nc, ctx, dram, sb)
            mla_stage(nc, ctx, dram, sb)
        merge_heads_stage(nc, ctx, dram, sb)
        with ExitStack() as own:
            mem = swiglu_memory(nc, own, ctx)
            norm_stage(nc, ctx, "n1_", sb, ahead=lambda sp: swiglu_first_loads(sp, dram, mem))
            swiglu_stage(nc, ctx, dram, sb, mem)
        norm_stage(nc, ctx, "n2_", sb)
        gqa_stage(nc, ctx, dram, sb)
        norm_stage(nc, ctx, "n3_", sb)
        cluster_stage(nc, ctx, dram, sb)
        norm_stage(nc, ctx, "n4_", sb, out)


def layouts(i):
    import numpy as np

    def cat(names, axis):
        return np.concatenate([i[n] for n in names], axis)

    def pad(a, axis):
        width = [(0, 0)] * a.ndim
        width[axis] = (0, HP - HID)
        return np.pad(a, width)

    def slots(a, axis):
        width = [(0, 0)] * a.ndim
        width[axis] = (0, 32 - a.shape[axis])
        return np.concatenate([np.pad(a, width)] * 3, axis)

    def by_key_head(w, heads):
        return w.reshape(DC, P, NKV, heads, P).transpose(2, 1, 3, 0, 4)

    x = i["L0_attn_x"].reshape(T, D)
    half = P // 2
    inv_freq = (1.0 / 10000.0 ** (np.arange(0, P, 2, dtype=np.float32) / np.float32(P))).astype(np.float32)
    angle = np.outer(inv_freq, np.arange(S, dtype=np.float32)).astype(np.float32)
    cos = np.concatenate([np.cos(angle)] * 2, 0).astype(np.float32)
    sin = np.concatenate([-np.sin(angle), np.sin(angle)], 0).astype(np.float32)
    scale = np.float32(P) ** np.float32(-0.5)
    return {
        "x": x,
        "xT": x.T,
        "w_down": cat(["L0_attn_Wq_down", "L0_attn_Wkv_down"], 1),
        "w_krope": cat(["L0_attn_Wk_rope", "L0_attn_Wk_rope"], 1),
        "w_qup": i["L0_attn_Wq_up"],
        "w_kvup": cat(["L0_attn_Wk_up", "L0_attn_Wv_up"], 1),
        "w_qrope": i["L0_attn_Wq_rope"],
        "wo0": i["L0_attn_Wo"],
        "w13": pad(np.stack([i["L0_ffn_w1"].T, i["L0_ffn_w3"].T]), 2),
        "w2": pad(i["L0_ffn_w2"].T, 0),
        "lora_a13": slots(np.stack([i["L0_ffn_lora_A1"], i["L0_ffn_lora_A3"]]), 1),
        "lora_b13": slots(pad(np.stack([i["L0_ffn_lora_B1"].T, i["L0_ffn_lora_B3"].T]), 2), 1),
        "lora_a2": slots(pad(i["L0_ffn_lora_A2"], 1), 0),
        "lora_b2": slots(i["L0_ffn_lora_B2"].T, 0),
        "wq1": by_key_head(i["L1_attn_Wq"], GQ),
        "wkv1": np.concatenate([by_key_head(i["L1_attn_Wk"], 1), by_key_head(i["L1_attn_Wv"], 1)], 2),
        "wo1": i["L1_attn_Wo"].reshape(NKV, GQ, P, D).transpose(0, 2, 1, 3),
        "tables": np.stack([cos * scale, sin * scale, cos, sin]).astype(np.float32),
        "w_dense": i["L1_ffn_weight"].T,
        "bias": i["L1_ffn_bias"],
        "centroids": i["L1_ffn_centroids"].T,
        "assignments": i["L1_ffn_assignments"],
    }


def kernel(**inputs):
    import numpy as np
    import concourse.bacc as bacc
    from concourse.bass_utils import run_bass_kernel_spmd

    arrays = {"in_" + n: np.ascontiguousarray(a) for n, a in layouts({n: np.asarray(a) for n, a in inputs.items()}).items()}
    nc = bacc.Bacc("TRN2", target_bir_lowering=False, num_devices=1)
    dram = {n[3:]: nc.dram_tensor(n, a.shape, mybir.dt.from_np(a.dtype), kind="ExternalInput").ap()
            for n, a in arrays.items()}
    out = nc.dram_tensor("out", (T, D), F32, kind="ExternalOutput").ap()
    program(nc, dram, out)
    r = run_bass_kernel_spmd(nc, [arrays], core_ids=[0])
    return r.results[0]["out"].reshape(NB, S, D)
```

```python
from contextlib import ExitStack

import concourse.bass as bass
from concourse import mybir

F32 = mybir.dt.float32
F32R = mybir.dt.float32r
ACT = mybir.ActivationFunctionType
ALU = mybir.AluOpType
AXX = mybir.AxisListType.X

P = 128
T = 1024
NB = 2
S = T // NB
D = 512
DC = D // P
TT = T // P
ST = S // P

NH0 = 128
HD0 = D // NH0
LAT = 64
ROPE = 64
GH = 4
NG = NH0 // GH
PARTS = 2
CROWS = 3 * HD0
MROW = 96
KC0 = ROPE + HD0


def latent_stage(nc, ctx, dram, sb):
    own = ExitStack()
    with own:
        def buf(name, shape, dt=F32):
            return own.enter_context(nc.sbuf_tensor(name, shape, dt))

        xT = buf("xT_sb", [P, DC, T])
        w_down = buf("w_down_sb", [P, DC, P])
        w_krope = buf("w_krope_sb", [P, DC, P])
        w_up = buf("w_up", [P, 2 * D])
        cT = buf("cT", [P, T])
        hi = {"q": sb["X"][:, :, :].bitcast(F32R).rearrange("p t n -> p (t n)").rearrange("p (m t) -> p m t", m=DC),
              "k": buf("content_hi_k", [P, DC, T], F32R)[:, :, :]}
        lo = {"q": sb["Q1"][:, :, :, :].rearrange("p b j s -> p (b j s)").rearrange("p (m t) -> p m t", m=DC),
              "k": buf("content_lo_k", [P, DC, T], F32R)[:, :, :]}
        zeros = buf("zeros", [P, 1, S])
        ones = buf("ones0", [P, S])
        bank = [own.enter_context(nc.psum_tensor(f"latent_ps{i}", [P, S], F32)) for i in range(8)]

        def sem(name):
            return ctx.enter_context(nc.semaphore(name))

        x_in = [sem(f"x_in{c}") for c in range(DC)]
        down_in = sem("w_down_in")
        up_in = sem("w_up_in")
        krope_in = sem("w_krope_in")
        x_split = sem("x_split")
        ps_full = sem("latent_ps_full")
        act_done = sem("latent_act_done")
        dve_done = sem("latent_dve_done")
        rows_set = sem("rows_set")
        rope_set = sem("rope_set")
        zeros_set = sem("zeros_set")
        parts_out = sem("parts_out")
        jobs = [("c", 0, b) for b in range(NB)]
        jobs += [(k, m, b) for m in range(DC) for k in "qk" for b in range(NB)]
        jobs += [("r", 0, b) for b in range(NB)] + [("v", t, 0) for t in range(TT)]
        block = own.enter_context(nc.Block())

        @block.sync
        def _(sp):
            sp.dma_start(w_down[:, :, :], dram["w_down"].rearrange("(c p) n -> p c n", p=P)).then_inc(down_in, 16)
            for c in range(DC):
                sp.dma_start(xT[:, c, :], dram["xT"][c * P:(c + 1) * P, :]).then_inc(x_in[c], 16)
            sp.dma_start(w_up[0:LAT, 0:D], dram["w_qup"]).then_inc(up_in, 16)
            sp.dma_start(w_up[LAT:P, :], dram["w_kvup"]).then_inc(up_in, 16)
            sp.dma_start(w_krope[:, :, :], dram["w_krope"].rearrange("(c p) n -> p c n", p=P)).then_inc(krope_in, 16)
            for n, (k, m, b) in enumerate(jobs):
                if k not in "qk" or b != NB - 1:
                    continue
                sp.wait_ge(act_done, n + 1)
                sp.wait_ge(dve_done, n + 1 - NB)
                for r, part in enumerate((hi[k], lo[k])):
                    heads = dram["content_" + k][m * 32:(m + 1) * 32, r * HD0:(r + 1) * HD0, :]
                    sp.dma_start(heads, part[:, m, :].bitcast(F32)).then_inc(parts_out, 16)
            sp.wait_ge(parts_out, 2 * DC * PARTS * 16)

        @block.gpsimd
        def _(pool):
            pool.memset(zeros[:, :, :], 0.0).then_inc(rows_set, 1)
            pool.wait_ge(rows_set, 1)
            pool.memset(ones[MROW:MROW + 1, :], 1.0).then_inc(rows_set, 1)
            pool.wait_ge(rows_set, 2)
            pool.memset(sb["V_slot"][:, :, :, :, :], 0.0).then_inc(rows_set, 1)
            pool.wait_ge(rows_set, 3)
            pool.memset(sb["V_slot"][:, :, :, :, HD0:HD0 + 1], 1.0).then_inc(rows_set, 1)
            pool.memset(sb["ident"][:, :], 0.0).then_inc(rows_set, 1)
            pool.wait_ge(rows_set, 5)
            pool.affine_select(out=sb["ident"][:, :], in_=sb["ident"][:, :], compare_op=ALU.not_equal, fill=1.0,
                               base=0, pattern=[[-1, P]], channel_multiplier=1).then_inc(rows_set, 1)
            pool.wait_ge(rows_set, 6)

        @block.scalar
        def _(act):
            for n, (kind, m, b) in enumerate(jobs):
                act.wait_ge(ps_full, n + 1)
                src = bank[n % 8][:, :]
                if kind == "c":
                    out = cT[:, b * S:(b + 1) * S]
                elif kind == "r":
                    out = sb["K1"][:, b, :]
                elif kind == "v":
                    out = sb["V"][:, m, :]
                else:
                    out = hi[kind][:, m, b * S:(b + 1) * S]
                act.activation(out, src, ACT.Copy).then_inc(act_done, 1)
                if kind == "r":
                    for j in range(GH):
                        act.activation(sb["KX"][0:ROPE, b, j, :], bank[n % 8][0:ROPE, :], ACT.Copy).then_inc(rope_set, 1)
            act.wait_ge(act_done, len(jobs))
            act.wait_ge(rope_set, NB * GH)

        @block.vector
        def _(dve):
            dve.wait_ge(rows_set, 2)
            for b in range(NB):
                for tile in (sb["Q2"], sb["K2"]):
                    dve.tensor_copy(tile[ROPE:P, b, :, :], zeros[ROPE:P, :, :].broadcast_to([ROPE, GH, S]))\
                       .then_inc(zeros_set, 1)
            dve.wait_ge(zeros_set, 2 * NB)
            for b in range(NB):
                for j in range(GH):
                    dve.tensor_copy(sb["K2"][MROW:MROW + 1, b, j, :], ones[MROW:MROW + 1, :]).then_inc(zeros_set, 1)
            for c in range(DC):
                dve.wait_ge(x_in[c], 16)
                dve.tensor_copy(sb["xh"][:, c, :], xT[:, c, :]).then_inc(x_split, 1)
                dve.wait_ge(x_split, 2 * c + 1)
                dve.tensor_tensor(sb["xl"][:, c, :], xT[:, c, :], sb["xh"][:, c, :], ALU.subtract).then_inc(x_split, 1)
            dve.wait_ge(x_split, 2 * DC)
            for n, (kind, m, b) in enumerate(jobs):
                if kind == "v":
                    break
                dve.wait_ge(act_done, n + 1)
                src = bank[n % 8]
                if kind == "c":
                    continue
                if kind == "r":
                    dve.wait_ge(rope_set, GH * (b + 1))
                    for j in range(GH):
                        ins = dve.tensor_tensor(sb["K2"][0:ROPE, b, j, :], src[0:ROPE, :], sb["K1"][0:ROPE, b, :],
                                                ALU.subtract)
                    ins.then_inc(dve_done, 1)
                else:
                    dve.tensor_tensor(lo[kind][:, m, b * S:(b + 1) * S], src[:, :], hi[kind][:, m, b * S:(b + 1) * S],
                                      ALU.subtract).then_inc(dve_done, 1)
            dve.wait_ge(dve_done, NB * (1 + 2 * DC))
            dve.wait_ge(zeros_set, (2 + GH) * NB)

        @block.tensor
        def _(pe):
            pe.wait_ge(down_in, 16)
            for c in range(DC):
                pe.wait_ge(x_in[c], 16)
                for b in range(NB):
                    last = pe.matmul(bank[b][:, :], w_down[:, c, :], xT[:, c, b * S:(b + 1) * S],
                                     start=c == 0, stop=c == DC - 1)
                    if c == DC - 1:
                        last.then_inc(ps_full, 1)
            for n, (kind, m, b) in enumerate(jobs):
                if kind == "c":
                    continue
                if n >= 8:
                    pe.wait_ge(act_done, n - 7)
                    if n - 8 >= NB and jobs[n - 8][0] != "v":
                        pe.wait_ge(dve_done, n - 7 - NB)
                out = bank[n % 8][:, :]
                if kind == "r":
                    if b == 0:
                        pe.wait_ge(krope_in, 16)
                    for c in range(DC):
                        last = pe.matmul(out, w_krope[:, c, :], xT[:, c, b * S:(b + 1) * S], start=c == 0, stop=c == DC - 1)
                else:
                    if n == NB:
                        pe.wait_ge(up_in, 32)
                        pe.wait_ge(act_done, NB)
                    if kind == "q":
                        last = pe.matmul(out, w_up[0:LAT, m * P:(m + 1) * P], cT[0:LAT, b * S:(b + 1) * S],
                                         start=True, stop=True)
                    elif kind == "k":
                        last = pe.matmul(out, w_up[LAT:P, m * P:(m + 1) * P], cT[LAT:P, b * S:(b + 1) * S],
                                         start=True, stop=True)
                    else:
                        last = pe.matmul(out, cT[LAT:P, m * P:(m + 1) * P], w_up[LAT:P, D:2 * D],
                                         start=True, stop=True)
                last.then_inc(ps_full, 1)


def mla_stage(nc, ctx, dram, sb, groups=NG):
    SCALE = float((HD0 + ROPE) ** -0.5)
    own = ExitStack()
    with own:
        def buf(name, shape, dt=F32):
            return own.enter_context(nc.sbuf_tensor(name, shape, dt))

        def sem(name):
            return ctx.enter_context(nc.semaphore(name))

        w_raw = buf("w_raw", [P, DC, 2, P])
        w_hi = buf("w_hi", [P, DC, 2, P], F32R)
        w_lo = buf("w_lo", [P, DC, 2, P], F32R)
        Q1 = sb["Q1"]
        Q2 = sb["Q2"]
        K1 = sb["K1"]
        K2 = sb["K2"]
        KX = sb["KX"]
        probs = buf("probs", [P, GH, ST, S])
        row_max = buf("row_max", [P, ST, GH])
        mrow = sb["mrow"]
        oT = buf("oT", [P, S])
        recip = buf("recip", [P, ST, GH, 1])
        V_slot, V, O, ident = sb["V_slot"], sb["V"], sb["X"], sb["ident"]
        ps_score = [own.enter_context(nc.psum_tensor(f"ps_score{i}", [P, 2, S], F32)) for i in range(2)]
        ps_max = [own.enter_context(nc.psum_tensor(f"ps_max{i}", [P, S], F32)) for i in range(2)]
        ps_x = own.enter_context(nc.psum_tensor("ps_x", [P, S], F32))
        ps_o = own.enter_context(nc.psum_tensor("ps_o", [P, S], F32))

        w_in = sem("wq_in")
        w_step = sem("wq_step")
        w_split = sem("wq_split")
        q_made = sem("q_made")
        q_high = sem("q_high")
        q_low = sem("q_low")
        q_copied = [sem(f"q_copied{b}") for b in range(NB)]
        content_in = [sem(f"content_in{b}") for b in range(NB)]
        max_made = sem("max_made")
        max_taken = sem("max_taken")
        max_turned = sem("max_turned")
        row_made = sem("row_made")
        row_in = sem("row_in")
        scored = sem("scored")
        exped = sem("exped")
        v_in = sem("v_in")
        pv_made = sem("pv_made")
        o_taken = sem("o_taken")
        o_turned = sem("o_turned")
        r_made = sem("r_made")
        o_made = sem("o_made")
        gate_sp, gate_pool = sem("gate_sp"), sem("gate_pool")
        ORDER = [(step[0], int(step[1]), int(step[2])) for step in (
            "v00 v10 m00 v20 v30 m01 q00 m02 q10 m03 m10 q20 m11 s00 l00 m12 s01 m13 "
            "s10 o00 m20 s11 m21 s20 m22 m23 s21 m30 s30 m31 m32 s31 m33").split()]
        w_view = dram["w_qrope"].rearrange("(c p) n -> p c n", p=P)
        block = own.enter_context(nc.Block())

        def run(engine, body):
            body(0, True, groups == 1)
            if groups > 2:
                with engine.Fori(1, groups - 1) as g:
                    body(g, False, False)
            if groups > 1:
                body(groups - 1, False, True)

        @block.sync
        def _(sp):
            def load_w(g):
                sp.dma_start(w_raw[:, :, :, :].rearrange("p c a n -> p c (a n)"),
                             w_view[:, :, bass.ds(g * 2 * P, 2 * P)]).then_inc(w_in, 16)

            def content(g, b):
                for tile, src, row, parts in ((Q2, "content_q", 0, 1), (Q2, "content_q", 1, 2),
                                              (K2, "content_k", 0, 2), (K2, "content_k", 2, 1),
                                              (KX, "content_k", 0, 1)):
                    rows = dram[src][bass.ds(g * GH, GH), 0:parts * HD0, b * S:(b + 1) * S].rearrange("h r t -> r h t")
                    at = ROPE + row * HD0
                    sp.dma_start(tile[at:at + parts * HD0, b, :, :].bitcast(F32), rows).then_inc(content_in[b], 16)

            def copy_q(n, b):
                sp.wait_ge(q_high, 2 * n + 2)
                sp.dma_start(Q1[0:ROPE, b, :, :].bitcast(F32), Q2[0:ROPE, b, :, :].bitcast(F32)).then_inc(q_copied[b], 16)

            load_w(0)
            content(0, 0)
            content(0, 1)
            copy_q(0, 0)

            def body(g, first, last):
                for b in range(NB):
                    n = 2 * g + b
                    sp.wait_ge(row_made, n + 1)
                    sp.dma_start(Q2[MROW:MROW + 1, b, :, :].bitcast(F32), mrow[0:GH, :].bitcast(F32)).then_inc(row_in, 16)
                    if b == 0 and not last:
                        sp.wait_ge(w_split, 2 * g + 2)
                        sp.sem_inc(gate_sp, 1)
                        load_w(g + 1)
                    if not (last and b == 1):
                        copy_q(n + 1, 1 - b)
                    if not last:
                        sp.wait_ge(scored, 8 * (n + 1))
                        sp.sem_inc(gate_sp, 1)
                        content(g + 1, b)

            run(sp, body)

        @block.gpsimd
        def _(pool):
            def split_w(g, pair):
                if pair == 0:
                    pool.wait_ge(w_in, 16 * (g + 1))
                pool.wait_ge(w_split, 2 * g + pair)
                pool.wait_ge(q_made, 4 * g - 1 + pair)
                pool.sem_inc(gate_pool, 1)
                pool.tensor_copy(w_hi[:, :, pair, :], w_raw[:, :, pair, :]).then_inc(w_step, 1)
                pool.wait_ge(w_step, 2 * g + pair + 1)
                pool.tensor_tensor(w_lo[:, :, pair, :], w_raw[:, :, pair, :], w_hi[:, :, pair, :],
                                   ALU.subtract).then_inc(w_split, 1)

            def values(g, b, n, first):
                if not first:
                    pool.wait_ge(pv_made, n - 1)
                    pool.sem_inc(gate_pool, 1)
                pool.tensor_copy(V_slot[:, b, :, :, 0:HD0],
                                 V[:, b * ST:(b + 1) * ST, bass.ds(g * GH * HD0, GH * HD0)].rearrange(
                                     "p t (h d) -> p t h d", h=GH)).then_inc(v_in, 1)

            def body(g, first, last):
                values(g, 0, 2 * g, first)
                if not last:
                    split_w(g + 1, 0)
                values(g, 1, 2 * g + 1, first)
                if not last:
                    split_w(g + 1, 1)

            run(pool, body)

        @block.scalar
        def _(act):
            def high(n, b, pair):
                act.wait_ge(q_made, 2 * n + pair + 1)
                for k in range(2):
                    ins = act.activation(Q2[0:ROPE, b, 2 * pair + k, :], ps_x[k * ROPE:(k + 1) * ROPE, :], ACT.Copy)
                ins.then_inc(q_high, 1)

            def exp(n, j, half):
                act.wait_ge(scored, 8 * n + 2 * j + half + 1)
                act.activation(probs[:, j, 2 * half:2 * half + 2, :], ps_score[half][:, :, :], ACT.Exp,
                               scale=SCALE).then_inc(exped, 1)

            def take_o(n):
                act.wait_ge(pv_made, n + 1)
                act.activation(oT[:, :], ps_o[:, :], ACT.Copy).then_inc(o_taken, 1)

            act.wait_ge(w_in, 16)
            for pair in range(2):
                act.activation(w_hi[:, :, pair, :], w_raw[:, :, pair, :], ACT.Copy).then_inc(w_step, 1)
            for pair in range(2):
                high(0, 0, pair)

            def body(g, first, last):
                for b in range(NB):
                    n = 2 * g + b
                    more = not (last and b == 1)
                    if more:
                        high(n + 1, 1 - b, 0)
                    act.wait_ge(max_turned, n + 1)
                    if not (first and b == 0):
                        act.wait_ge(row_in, 16 * n)
                    act.activation(mrow[0:GH, :], ps_max[0][0:GH, :], ACT.Copy, scale=-1.0).then_inc(row_made, 1)
                    if not (first and b == 0):
                        take_o(n - 1)
                    for kind, j, k in ORDER:
                        if kind == "s":
                            exp(n, j, k)
                        if kind == "q" and j == 2 and more:
                            high(n + 1, 1 - b, 1)

            run(act, body)
            take_o(2 * groups - 1)

        @block.vector
        def _(dve):
            def low(n, b, pair):
                dve.wait_ge(q_high, 2 * n + pair + 1)
                for k in range(2):
                    ins = dve.tensor_tensor(Q1[ROPE:P, b, 2 * pair + k, :], ps_x[k * ROPE:(k + 1) * ROPE, :],
                                            Q2[0:ROPE, b, 2 * pair + k, :], ALU.subtract)
                ins.then_inc(q_low, 1)

            def take_max(n, j, t):
                dve.wait_ge(max_made, 16 * n + 4 * j + t + 1)
                dve.tensor_reduce(row_max[:, t, j:j + 1], ps_max[t % 2][:, :], axis=AXX, op=ALU.max)\
                   .then_inc(max_taken, 1)

            def normalise(g, b, n):
                dve.wait_ge(o_turned, n + 1)
                outs = ps_x[:, :].rearrange("p (t h m) -> p t h m", t=ST, h=GH)
                dve.reciprocal(recip[:, :, :, :], outs[:, :, :, HD0:HD0 + 1]).then_inc(r_made, 1)
                dve.wait_ge(r_made, n + 1)
                for t in range(ST):
                    ins = dve.tensor_tensor(O[:, b * ST + t, bass.ds(g * GH * HD0, GH * HD0)].rearrange(
                        "p (h d) -> p h d", h=GH), outs[:, t, :, 0:HD0],
                        recip[:, t, :, :].broadcast_to([P, GH, HD0]), ALU.mult)
                ins.then_inc(o_made, 1)

            for pair in range(2):
                dve.wait_ge(w_step, pair + 1)
                dve.tensor_tensor(w_lo[:, :, pair, :], w_raw[:, :, pair, :], w_hi[:, :, pair, :],
                                  ALU.subtract).then_inc(w_split, 1)
            for pair in range(2):
                low(0, 0, pair)
                for j in range(2 * pair, 2 * pair + 2):
                    for t in range(ST):
                        take_max(0, j, t)

            def body(g, first, last):
                for b in range(NB):
                    n = 2 * g + b
                    more = not (last and b == 1)
                    if more:
                        low(n + 1, 1 - b, 0)
                    for kind, j, t in ORDER:
                        if kind == "m" and more:
                            take_max(n + 1, j, t)
                        if kind == "l" and more:
                            low(n + 1, 1 - b, 1)
                        if kind == "o" and not (first and b == 0):
                            normalise(g - 1 + b, 1 - b, n - 1)

            run(dve, body)
            normalise(groups - 1, 1, 2 * groups - 1)
            dve.wait_ge(o_made, 2 * groups)

        @block.tensor
        def _(pe):
            def queries(g, b, pair, third):
                if b == 0 and third == 0:
                    pe.wait_ge(w_split, 2 * g + pair + 1)
                w, x = ((w_hi, "xh"), (w_lo, "xh"), (w_hi, "xl"))[third]
                for c in range(DC):
                    last = pe.matmul(ps_x[:, :], w[:, c, pair, :], sb[x][:, c, b * S:(b + 1) * S],
                                     start=third == c == 0, stop=third == 2 and c == DC - 1)
                if third == 2:
                    last.then_inc(q_made, 1)

            def max_scores(g, b, n, j, t, wait_free=True):
                if j % 2 == 0 and t == 0:
                    pe.wait_ge(q_high, 2 * n + j // 2 + 1)
                if j == 0 and t == 0:
                    pe.wait_ge(content_in[b], 80 * (g + 1))
                    if wait_free:
                        pe.wait_ge(row_made, n)
                if wait_free:
                    pe.wait_ge(max_taken, 16 * n + 4 * j + t - 1)
                pe.matmul(ps_max[t % 2][:, :], Q2[0:KC0, b, j, t * P:(t + 1) * P], KX[0:KC0, b, j, :],
                          start=True, stop=True).then_inc(max_made, 1)

            def scores(g, n, b, j, half, wait_free=True):
                if j == half == 0:
                    pe.wait_ge(q_low, 2 * n + 2)
                    pe.wait_ge(q_copied[b], 16 * (g + 1))
                    pe.wait_ge(row_in, 16 * (n + 1))
                if wait_free:
                    pe.wait_ge(exped, 8 * n + 2 * j + half - 1)
                for k in range(2):
                    t = 2 * half + k
                    pe.matmul(ps_score[half][:, k, :], K1[:, b, t * P:(t + 1) * P], Q1[:, b, j, :],
                              start=True, stop=False)
                    last = pe.matmul(ps_score[half][:, k, :], K2[0:MROW + 1, b, j, t * P:(t + 1) * P],
                                     Q2[0:MROW + 1, b, j, :], start=False, stop=True)
                last.then_inc(scored, 1)

            def outputs(n, b, t):
                if t == 0:
                    pe.wait_ge(exped, 8 * (n + 1))
                    pe.wait_ge(v_in, n + 1)
                for j in range(GH):
                    last = pe.matmul(ps_o[32 * j:32 * (j + 1), :], V_slot[:, b, t, j, :], probs[:, j, t, :],
                                     start=t == 0, stop=t == ST - 1)
                if t == ST - 1:
                    last.then_inc(pv_made, 1)

            def turn_o(n):
                pe.wait_ge(o_taken, n + 1)
                for t in range(ST):
                    last = pe.transpose(ps_x[:, t * P:(t + 1) * P], oT[:, t * P:(t + 1) * P], ident[:, :])
                last.then_inc(o_turned, 1)

            for pair in range(2):
                if pair:
                    pe.wait_ge(q_low, 1)
                for third in range(3):
                    queries(0, 0, pair, third)
            for j in range(GH):
                for t in range(ST):
                    max_scores(0, 0, 0, j, t, wait_free=4 * j + t >= 2)

            def body(g, first, last):
                for b in range(NB):
                    n = 2 * g + b
                    more = not (last and b == 1)
                    before = not (first and b == 0)
                    if more:
                        if first:
                            pe.wait_ge(q_low, 2 * n + 2)
                        if not first:
                            pe.wait_ge(o_made, n - 1)
                        for third in range(3):
                            queries(g + b, 1 - b, 0, third)
                    pe.wait_ge(max_taken, 16 * (n + 1))
                    for t in range(ST):
                        ins = pe.transpose(ps_max[0][0:GH, t * P:(t + 1) * P], row_max[:, t, :], ident[:, :])
                    ins.then_inc(max_turned, 1)
                    for kind, j, k in ORDER:
                        if kind == "v" and before:
                            outputs(n - 1, 1 - b, j)
                        if kind == "s":
                            scores(g, n, b, j, k, wait_free=before or j > 0)
                        if kind == "m" and more:
                            max_scores(g + b, 1 - b, n + 1, j, k)
                        if kind == "o" and before:
                            if more:
                                pe.wait_ge(q_low, 2 * n + 4)
                            else:
                                pe.wait_ge(o_made, n - 1)
                            turn_o(n - 1)
                        if kind == "q" and more:
                            if j == 0:
                                pe.wait_ge(q_low, 2 * n + 3)
                            queries(g + b, 1 - b, 1, j)

            run(pe, body)
            for t in range(ST):
                outputs(2 * groups - 1, 1, t)
            pe.wait_ge(o_made, 2 * groups - 1)
            turn_o(2 * groups - 1)

EPS = 1e-5
HID = 1376
HT = 11
HP = HT * P
RANK = 16
LORA_SCALE = 2.0

NKV = 8
GQ = 4
NCL = 64
THRESHOLD = 0.01
TEMPERATURE = 0.1


def merge_heads_stage(nc, ctx, dram, sb):
    own = ExitStack()
    with own:
        def sem(name):
            return ctx.enter_context(nc.semaphore(name))

        X, ident = sb["X"], sb["ident"]
        x = own.enter_context(nc.sbuf_tensor("x_sb", [P, TT, D], F32))
        wo = own.enter_context(nc.sbuf_tensor("wo0_sb", [P, DC, D], F32))
        oT = own.enter_context(nc.sbuf_tensor("oT0", [P, 2, DC, P], F32))
        turned = [own.enter_context(nc.psum_tensor(f"turned{i}", [P, DC, P], F32)) for i in range(2)]
        made = [own.enter_context(nc.psum_tensor(f"made{i}", [P, D], F32)) for i in range(2)]
        wo_in = sem("wo0_in")
        x_in = [sem(f"x0_in{i}") for i in range(2)]
        o_turned = sem("o0_turned")
        o_taken = sem("o0_taken")
        y_made = sem("y0_made")
        y_taken = sem("y0_taken")
        counted = sem("y0_counted")
        block = own.enter_context(nc.Block())

        @block.sync
        def _(sp):
            sp.dma_start(wo[:, :, :], dram["wo0"].rearrange("(c p) n -> p c n", p=P)).then_inc(wo_in, 16)
            for i in range(2):
                half = slice(i * ST, (i + 1) * ST)
                sp.dma_start(x[:, half, :], dram["x"].rearrange("(t p) n -> p t n", p=P)[:, half, :]).then_inc(x_in[i], 16)

        @block.tensor
        def _(pe):
            def turn(t):
                if t >= 2:
                    pe.wait_ge(o_taken, t - 1)
                for c in range(DC):
                    last = pe.transpose(turned[t % 2][:, c, :], X[:, t, c * P:(c + 1) * P], ident[:, :])
                last.then_inc(o_turned, 1)

            turn(0)
            pe.wait_ge(wo_in, 16)
            for t in range(TT):
                if t + 1 < TT:
                    turn(t + 1)
                pe.wait_ge(o_taken, t + 1)
                if t >= 2:
                    pe.wait_ge(y_taken, t - 1)
                for c in range(DC):
                    last = pe.matmul(made[t % 2][:, :], oT[:, t % 2, c, :], wo[:, c, :], start=c == 0, stop=c == DC - 1)
                last.then_inc(y_made, 1)

        @block.scalar
        def _(act):
            for t in range(TT):
                act.wait_ge(o_turned, t + 1)
                if t >= 2:
                    act.wait_ge(y_made, t - 1)
                act.activation(oT[:, t % 2, :, :], turned[t % 2][:, :, :], ACT.Copy).then_inc(o_taken, 1)

        @block.vector
        def _(dve):
            for t in range(TT):
                if t % ST == 0:
                    dve.wait_ge(x_in[t // ST], 16)
                dve.wait_ge(y_made, t + 1)
                dve.tensor_tensor(X[:, t, :], made[t % 2][:, :], x[:, t, :], ALU.add).then_inc(y_taken, 1)
                dve.wait_ge(y_taken, t + 1)
                dve.bn_stats(sb["stats"][:, t, :], X[:, t, :]).then_inc(counted, 1)
            dve.wait_ge(counted, TT)


def norm_stage(nc, ctx, name, sb, out=None, ahead=None):
    own = ExitStack()
    with own:
        def sem(s):
            return ctx.enter_context(nc.semaphore(name + s))

        X, ident = sb["X"], sb["ident"]
        stats = sb["stats"]
        moments = own.enter_context(nc.sbuf_tensor(name + "moments", [P, TT, 2], F32))
        dev = own.enter_context(nc.sbuf_tensor(name + "dev", [P, TT], F32))
        eps = own.enter_context(nc.sbuf_tensor(name + "eps", [P, 1], F32))
        unused = own.enter_context(nc.sbuf_tensor(name + "unused", [P, 1], F32))
        turned = [own.enter_context(nc.psum_tensor(f"{name}turned{i}", [P, DC, P], F32)) for i in range(4)]
        eps_set = sem("eps_set")
        mean_var = sem("mean_var")
        rooted = sem("rooted")
        inverse = sem("inverse")
        normed = sem("normed")
        if out is None:
            x_turned, high, low = sem("x_turned"), sem("high"), sem("low")
        else:
            stored = sem("stored")
        block = own.enter_context(nc.Block())

        @block.vector
        def _(dve):
            dve.memset(eps[:, :], EPS).then_inc(eps_set, 1)
            for t in range(TT):
                dve.bn_aggr(moments[:, t, :], stats[:, t, :]).then_inc(mean_var, 1)
            dve.wait_ge(rooted, 1)
            dve.reciprocal(dev[:, :], dev[:, :]).then_inc(inverse, 1)
            dve.wait_ge(inverse, 1)
            for t in range(TT):
                dve.tensor_scalar(X[:, t, :], X[:, t, :], moments[:, t, 0:1], dev[:, t:t + 1],
                                  ALU.subtract, ALU.mult).then_inc(normed, 1)
            if out is None:
                for t in range(TT):
                    dve.wait_ge(high, t + 1)
                    dve.tensor_tensor(sb["xl"][:, :, t * P:(t + 1) * P], turned[t % 4][:, :, :],
                                      sb["xh"][:, :, t * P:(t + 1) * P], ALU.subtract).then_inc(low, 1)
                dve.wait_ge(low, TT)

        @block.scalar
        def _(act):
            act.wait_ge(eps_set, 1)
            act.activation(unused[:, :], eps[:, :], ACT.Sqrt)
            act.wait_ge(mean_var, TT)
            act.activation(dev[:, :], moments[:, :, 1], ACT.Sqrt, bias=eps[:, 0:1]).then_inc(rooted, 1)
            if out is None:
                for t in range(TT):
                    act.wait_ge(x_turned, t + 1)
                    act.activation(sb["xh"][:, :, t * P:(t + 1) * P], turned[t % 4][:, :, :], ACT.Copy)\
                       .then_inc(high, 1)

        @block.tensor
        def _(pe):
            if out is None:
                for t in range(TT):
                    pe.wait_ge(normed, t + 1)
                    if t >= 4:
                        pe.wait_ge(low, t - 3)
                    for c in range(DC):
                        last = pe.transpose(turned[t % 4][:, c, :], X[:, t, c * P:(c + 1) * P], ident[:, :])
                    last.then_inc(x_turned, 1)

        @block.sync
        def _(sp):
            if ahead is not None:
                ahead(sp)
            if out is not None:
                rows = out.rearrange("(t p) n -> p t n", p=P)
                for t in range(TT):
                    sp.wait_ge(normed, t + 1)
                    sp.dma_start(rows[:, t, :], X[:, t, :]).then_inc(stored, 16)
                sp.wait_ge(stored, 16 * TT)


RAW = 3
LR = 3 * 32


def swiglu_memory(nc, own, ctx):
    m = {}

    def buf(name, shape, dt=F32):
        m[name] = own.enter_context(nc.sbuf_tensor(name, shape, dt))

    buf("w13_hi", [P, 2, DC, HP], F32R)
    buf("w13_lo", [P, 2, DC, HP], F32R)
    buf("w2_sb", [P, HT, D])
    buf("w13_raw", [P, 2, HP])
    buf("lora_a", [LR, 2, D], F32R)
    buf("lora_b", [LR, 2, HP], F32R)
    buf("lora_a2", [LR, HP], F32R)
    buf("lora_b2", [LR, D], F32R)
    buf("gates", [P, 2, 2, S])
    late = m["w2_sb"][0:LR, :, :].rearrange("p m n -> p (m n)")
    m["raw_a"] = late[:, 0:2 * D].rearrange("p (i d) -> p i d", i=2)
    m["raw_b"] = late[:, 2 * D:2 * D + 2 * HP].rearrange("p (i h) -> p i h", i=2)
    m["raw_a2"] = late[:, 2 * D + 2 * HP:2 * D + 3 * HP]
    early = m["gates"][:, :, :, :].rearrange("p i k s -> p (i k s)")
    m["raw_b2"] = early[0:LR, HP:HP + D]
    m["raw"] = [m["w13_raw"][:, 0, :], m["w13_raw"][:, 1, :], early[:, 0:HP]]
    m["lora_in"] = ctx.enter_context(nc.semaphore("ffn_lora_in"))
    m["raw_in"] = [ctx.enter_context(nc.semaphore(f"ffn_raw_in{i}")) for i in range(RAW)]
    return m


def swiglu_load_step(sp, dram, m, s):
    i, c = s // DC, s % DC
    sp.dma_start(m["raw"][s % RAW], dram["w13"][i, c * P:(c + 1) * P, :]).then_inc(m["raw_in"][s % RAW], 16)


def swiglu_first_loads(sp, dram, m):
    sp.dma_start(m["raw_a"], dram["lora_a13"].rearrange("i r d -> r i d")).then_inc(m["lora_in"], 16)
    sp.dma_start(m["raw_b"], dram["lora_b13"].rearrange("i r h -> r i h")).then_inc(m["lora_in"], 16)
    sp.dma_start(m["raw_a2"], dram["lora_a2"]).then_inc(m["lora_in"], 16)
    sp.dma_start(m["raw_b2"], dram["lora_b2"]).then_inc(m["lora_in"], 16)
    for s in range(RAW):
        swiglu_load_step(sp, dram, m, s)


def swiglu_stage(nc, ctx, dram, sb, mem):
    own = ExitStack()
    with own:
        def sem(name):
            return ctx.enter_context(nc.semaphore("ffn_" + name))

        X, xh, xl = sb["X"], sb["xh"], sb["xl"]
        w_hi, w_lo, w2, raw = mem["w13_hi"], mem["w13_lo"], mem["w2_sb"], mem["raw"]
        lora_a, lora_b, a2, b2 = mem["lora_a"], mem["lora_b"], mem["lora_a2"], mem["lora_b2"]
        gate, g = mem["gates"][:, 0, :, :], mem["gates"][:, 1, :, :]
        lora_in, raw_in = mem["lora_in"], mem["raw_in"]
        w2_in = sem("w2_in")
        banks = [own.enter_context(nc.psum_tensor(f"ffn_ps{i}", [P, S], F32)) for i in range(8)]
        factors = [(mem["raw_a"], lora_a[:, :, :], 2),
                   (mem["raw_b"][:, 0, :], lora_b[:, 0, :], 1), (mem["raw_b"][:, 1, :], lora_b[:, 1, :], 1),
                   (mem["raw_a2"], a2[:, :], 2), (mem["raw_b2"], b2[:, :], 1)]
        factor_high = sem("factor_high")
        factor_low = sem("factor_low")
        delta = sem("delta")
        folded = sem("folded")
        w_high = sem("w_high")
        w_low = [sem(f"w_low{i}") for i in range(RAW)]
        hidden = sem("hidden")
        gated = sem("gated")
        g_made = sem("g_made")
        down = sem("down")
        taken = sem("taken")
        counted = sem("counted")
        CUTS = [(0, 512), (512, 512), (1024, HP - 1024)]
        NC = len(CUTS)
        ONE = 1
        block = own.enter_context(nc.Block())
        steps = [(i, c) for i in range(2) for c in range(DC)]

        @block.sync
        def _(sp):
            for s in range(RAW, len(steps)):
                sp.wait_ge(w_low[s % RAW], s // RAW)
                swiglu_load_step(sp, dram, mem, s)
            sp.wait_ge(factor_low, 5)
            sp.dma_start(w2[:, :, :], dram["w2"].rearrange("(m p) n -> p m n", p=P)).then_inc(w2_in, 16)

        def low_part(engine, s):
            i, c = steps[s]
            engine.wait_ge(w_high, s + 1)
            engine.tensor_tensor(w_lo[:, i, c, :], raw[s % RAW], w_hi[:, i, c, :], ALU.subtract)\
                  .then_inc(w_low[s % RAW], 1)

        @block.gpsimd
        def _(pool):
            for s in range(1, len(steps) - 1, 2):
                low_part(pool, s)

        @block.scalar
        def _(act):
            def factor(k):
                act.activation(factors[k][1], factors[k][0], ACT.Copy).then_inc(factor_high, 1)

            act.wait_ge(lora_in, 64)
            for k in range(3):
                factor(k)
            for s, (i, c) in enumerate(steps):
                if s == 2:
                    factor(3)
                    factor(4)
                act.wait_ge(folded, NC * (s + 1))
                act.activation(w_hi[:, i, c, :], raw[s % RAW], ACT.Copy).then_inc(w_high, 1)
            with act.Fori(0, NB) as half:
                for m in range(HT):
                    act.wait_ge(hidden, half * HT + m + 1)
                    if m >= 2:
                        act.wait_ge(g_made, ONE + half * HT + m - 1)
                    else:
                        act.wait_ge(g_made, ONE + half * HT)
                    act.activation(gate[:, m % 2, :], banks[4 + m % 2][:, :], ACT.Silu).then_inc(gated, 1)

        @block.vector
        def _(dve):
            dve.sem_inc(g_made, ONE)
            dve.sem_inc(taken, ONE)

            def factor(k):
                source, parts, slot = factors[k]
                rows = slice(32 * slot, 32 * (slot + 1))
                dve.wait_ge(factor_high, k + 1)
                dve.tensor_tensor(parts[rows], source[rows], parts[rows], ALU.subtract).then_inc(factor_low, 1)

            factor(0)
            factor(1)
            for s, (i, c) in enumerate(steps):
                if s == 1:
                    factor(2)
                if s == 3:
                    factor(3)
                    factor(4)
                dve.wait_ge(raw_in[s % RAW], 16 * (s // RAW + 1))
                for k, (at, n) in enumerate(CUTS):
                    j = NC * s + k
                    dve.wait_ge(delta, j + 1)
                    dve.scalar_tensor_tensor(out=raw[s % RAW][:, at:at + n], in0=banks[j % 8][:, 0:n], scalar=LORA_SCALE,
                                             in1=raw[s % RAW][:, at:at + n], op0=ALU.mult, op1=ALU.add)\
                       .then_inc(folded, 1)
                if s % 2:
                    low_part(dve, s - 1)
            low_part(dve, len(steps) - 1)
            dve.wait_ge(w2_in, 16)
            for m in range(HT):
                j = NC * len(steps) + m
                dve.wait_ge(delta, j + 1)
                dve.scalar_tensor_tensor(out=w2[:, m, :], in0=banks[m % 4][:, :], scalar=LORA_SCALE,
                                         in1=w2[:, m, :], op0=ALU.mult, op1=ALU.add).then_inc(folded, 1)
            with dve.Fori(0, NB) as half:
                for m in range(HT):
                    dve.wait_ge(gated, half * HT + m + 1)
                    if m >= 2:
                        dve.wait_ge(down, ONE + half * HT + m - 1)
                    else:
                        dve.wait_ge(down, ONE + half * HT)
                    dve.tensor_tensor(g[:, m % 2, :], banks[6 + m % 2][:, :], gate[:, m % 2, :], ALU.mult)\
                       .then_inc(g_made, 1)
                dve.wait_ge(down, ONE + (half + 1) * HT)
                for t in range(ST):
                    row = X[:, bass.ds(half * ST + t, 1), :].rearrange("p a n -> p (a n)")
                    dve.tensor_tensor(row, banks[t][:, :], row, ALU.add).then_inc(taken, 1)
                for t in range(ST):
                    dve.wait_ge(taken, ONE + half * ST + t + 1)
                    row = X[:, bass.ds(half * ST + t, 1), :].rearrange("p a n -> p (a n)")
                    dve.bn_stats(sb["stats"][:, bass.ds(half * ST + t, 1), :].rearrange("p a n -> p (a n)"), row)\
                       .then_inc(counted, 1)
            dve.wait_ge(counted, TT)

        @block.tensor
        def _(pe):
            pe.sem_inc(down, ONE)
            j = 0
            for i, c in steps:
                if c == 0:
                    pe.wait_ge(factor_low, i + 2)
                for at, n in CUTS:
                    if j >= 8:
                        pe.wait_ge(folded, j - 7)
                    pe.matmul(banks[j % 8][:, 0:n], lora_a[:, i, c * P:(c + 1) * P], lora_b[:, i, at:at + n],
                              start=True, stop=True).then_inc(delta, 1)
                    j += 1
            pe.wait_ge(factor_low, 5)
            for m in range(HT):
                pe.wait_ge(folded, NC * len(steps) if m < 4 else j - 3)
                pe.matmul(banks[m % 4][:, :], a2[:, m * P:(m + 1) * P], b2[:, :], start=True, stop=True)\
                  .then_inc(delta, 1)
                j += 1
            for k in range(RAW):
                pe.wait_ge(w_low[k], len(steps[k::RAW]))

            def project(half, m):
                if m >= 2:
                    pe.wait_ge(g_made, ONE + half * HT + m - 1)
                else:
                    pe.wait_ge(g_made, ONE + half * HT)
                for i in range(2):
                    k = 0
                    for w, x in ((w_hi, xh), (w_lo, xh), (w_hi, xl)):
                        for c in range(DC):
                            last = pe.matmul(banks[4 + 2 * i + m % 2][:, :], w[:, i, c, m * P:(m + 1) * P],
                                             x[:, c, bass.ds(half * S, S)], start=k == 0, stop=k == 3 * DC - 1)
                            k += 1
                last.then_inc(hidden, 1)

            with pe.Fori(0, NB) as half:
                project(half, 0)
                pe.wait_ge(taken, ONE + half * ST)
                for m in range(HT):
                    if m + 1 < HT:
                        project(half, m + 1)
                    pe.wait_ge(g_made, ONE + half * HT + m + 1)
                    if m == 0:
                        pe.wait_ge(folded, NC * len(steps) + HT)
                    for t in range(ST):
                        last = pe.matmul(banks[t][:, :], g[:, m % 2, t * P:(t + 1) * P], w2[:, m, :],
                                         start=m == 0, stop=m == HT - 1)
                    last.then_inc(down, 1)


def gqa_memory(nc, own, ctx):
    m = {}
    for name, shape in (("wq_raw", [P, GQ, DC, P]), ("wkv_raw", [P, 2, DC, P]),
                        ("wo_raw", [P, GQ, D]),
                        ("tables", [P, 4, S])):
        m[name] = own.enter_context(nc.sbuf_tensor(name, shape, F32))
    for name in ("tables_in", "wqkv_in", "wo_in"):
        m[name] = ctx.enter_context(nc.semaphore("gqa_" + name))
    return m


def gqa_load_qkv(sp, dram, m, kv):
    sp.dma_start(m["wkv_raw"][:, :, :, :], dram["wkv1"][bass.ds(kv, 1), :, :, :, :].rearrange(
        "a p i c n -> (a p) i c n")).then_inc(m["wqkv_in"], 16)
    sp.dma_start(m["wq_raw"][:, :, :, :], dram["wq1"][bass.ds(kv, 1), :, :, :, :].rearrange(
        "a p h c n -> (a p) h c n")).then_inc(m["wqkv_in"], 16)


def gqa_load_wo(sp, dram, m, kv):
    sp.dma_start(m["wo_raw"][:, :, :], dram["wo1"][bass.ds(kv, 1), :, :, :].rearrange(
        "a p h n -> (a p) h n")).then_inc(m["wo_in"], 16)


def gqa_first_loads(sp, dram, m):
    gqa_load_qkv(sp, dram, m, 0)
    sp.dma_start(m["tables"][:, :, :], dram["tables"].rearrange("i p s -> p i s")).then_inc(m["tables_in"], 16)
    gqa_load_wo(sp, dram, m, 0)


def gqa_stage(nc, ctx, dram, sb, mem):
    own = ExitStack()
    with own:
        def buf(name, shape, dt=F32):
            return own.enter_context(nc.sbuf_tensor(name, shape, dt))

        def psum(name, shape):
            return own.enter_context(nc.psum_tensor(name, shape, F32))

        def sem(name):
            return ctx.enter_context(nc.semaphore("gqa_" + name))

        X, xh, xl, ident = sb["X"], sb["xh"], sb["xl"], sb["ident"]
        NU = GQ * NB
        wq_raw, wkv_raw, wo_raw, tables = (mem[name] for name in ("wq_raw", "wkv_raw", "wo_raw", "tables"))
        wq = [buf(f"wq_{k}", [P, GQ, DC, P], F32R) for k in ("hi", "lo")]
        wkv = [buf(f"wkv_{k}", [P, 2, DC, P], F32R) for k in ("hi", "lo")]
        wo = [buf(f"wo_{k}", [P, GQ, D], F32R) for k in ("hi", "lo")]
        K = [buf(f"k_{k}", [P, NB, S], F32R) for k in ("hi", "lo")]
        Q = [buf(f"q_{k}", [P, 2, S], F32R) for k in ("hi", "lo")]
        V = buf("v1", [P, NB, ST, P])
        by_sin = buf("by_sin", [P, S])
        roped = buf("roped", [P, 2, S])
        probs = buf("probs1", [P, 2, ST, S])
        probsT = buf("probsT", [P, 3, S])
        O = [buf(f"o_{k}", [P, NB, GQ, S], F32R) for k in ("hi", "lo")]
        minus_max = buf("minus_max", [P, ST])
        sums = buf("sums", [P, 2, ST])
        inverse = buf("inverse", [P, ST])
        mask = buf("mask_sb", [P, 2, P], F32R)
        mask_raw = buf("mask_raw", [P, 2, P])
        ps_s = [psum(f"ps_s{i}", [P, S]) for i in range(3)]
        place = {3: (0, 0), 2: (1, 0), 0: (1, 3 * P), 1: (2, 0)}
        ps_t = [psum(f"ps_t{i}", [P, S]) for i in range(2)]
        ps_r = [psum(f"ps_r{i}", [P, S]) for i in range(2)]
        ps_o = psum("ps_o1", [P, S])
        pieces = [[(0, 0)], [(1, 0), (3, 3 * P)], [(2, 0)]]

        tables_in = mem["tables_in"]
        mask_set = sem("mask_set")
        wqkv_in = mem["wqkv_in"]
        wo_in = mem["wo_in"]
        step = sem("step")
        wkv_split = sem("wkv_split")
        wq_split = sem("wq_split")
        wo_split = sem("wo_split")
        made = sem("made")
        taken = sem("taken")
        v_taken = sem("v_taken")
        v_turned = sem("v_turned")
        v_ready = sem("v_ready")
        summed = sem("summed")
        r_high = sem("r_high")
        r_low = sem("r_low")
        scored = sem("scored")
        maxed = sem("maxed")
        exped = sem("exped")
        inverted = sem("inverted")
        normed = sem("normed")
        turned = sem("turned")
        t_taken = sem("t_taken")
        pv_made = sem("pv_made")
        o_high = sem("o_high")
        o_low = sem("o_low")
        counted = sem("counted")
        gate_sp, gate_pool = sem("gate_sp"), sem("gate_pool")
        first_splits = [([w[:, i] for w in parts], raw[:, i], count)
                        for i in range(2) for parts, raw, count in ((wkv, wkv_raw, wkv_split), (wq, wq_raw, wq_split))]
        FIRST = len(first_splits)
        START, PER, TAKEN = 4, 3 * NU - 4, 3 * NU - 6

        def ring_query(u): return u
        def ring_next(k): return NU + k
        def ring_out(last, j): return (NU if last else NU + 4) + j
        def take_query(u): return u - 2
        def take_next(k): return NU - 2 + k
        def take_out(last, j): return (NU - 2 if last else NU + 2) + j
        ONE = 1
        RP = NU + 2

        block = own.enter_context(nc.Block())

        def run(engine, body):
            with engine.Fori(0, NKV - 1) as kv:
                body(kv, False)
            body(NKV - 1, True)

        @block.sync
        def _(sp):
            def body(kv, last):
                if not last:
                    sp.wait_ge(wkv_split, 2 * (kv + 1))
                    sp.sem_inc(gate_sp, 1)
                    sp.wait_ge(wq_split, GQ * (kv + 1))
                    sp.sem_inc(gate_sp, 1)
                    gqa_load_qkv(sp, dram, mem, kv + 1)
                    sp.wait_ge(wo_split, GQ * (kv + 1))
                    sp.sem_inc(gate_sp, 1)
                    gqa_load_wo(sp, dram, mem, kv + 1)

            run(sp, body)

        @block.gpsimd
        def _(pool):
            pool.memset(mask_raw[:, :, :], 0.0).then_inc(mask_set, 1)
            pool.wait_ge(mask_set, 1)
            pool.affine_select(out=mask_raw[:, 0, :], in_=mask_raw[:, 0, :], compare_op=ALU.not_equal, fill=1.0,
                               base=0, pattern=[[-1, P]], channel_multiplier=1).then_inc(mask_set, 1)
            pool.affine_select(out=mask_raw[:, 1, :], in_=mask_raw[:, 1, :], compare_op=ALU.is_ge, fill=-1e30,
                               base=0, pattern=[[-1, P]], channel_multiplier=1).then_inc(mask_set, 1)
            pool.wait_ge(mask_set, 3)
            pool.tensor_copy(mask[:, :, :], mask_raw[:, :, :]).then_inc(mask_set, 1)

            def split(parts, raw, count, at_step):
                pool.sem_inc(gate_pool, 1)
                hi, lo = parts
                pool.tensor_copy(hi, raw).then_inc(step, 1)
                pool.wait_ge(step, at_step)
                pool.tensor_tensor(lo, raw, hi, ALU.subtract).then_inc(count, 1)

            EACH = 2 + 2 * GQ

            def split_kv(i, at_step):
                split([w[:, i, :, :] for w in wkv], wkv_raw[:, i, :, :], wkv_split, at_step)

            def split_q(h, at_step):
                split([w[:, h, :, :] for w in wq], wq_raw[:, h, :, :], wq_split, at_step)

            def split_o(h, at_step):
                split([w[:, h, :] for w in wo], wo_raw[:, h, :], wo_split, at_step)

            def rope(n, at, parts):
                pool.wait_ge(summed, n + 1)
                pool.sem_inc(gate_pool, 1)
                pool.tensor_copy(parts[0], roped[:, at, :]).then_inc(r_high, 1)
                pool.wait_ge(r_high, n + 1)
                pool.tensor_tensor(parts[1], roped[:, at, :], parts[0], ALU.subtract).then_inc(r_low, 1)

            def rope_key(n, b):
                rope(n, 0, [k[:, b, :] for k in K])

            def rope_query(n, u, at):
                rope(n, at, [q[:, u % 2, :] for q in Q])

            for b in range(NB):
                rope_key(2 * b, b)
                rope_query(2 * b + 1, b, 1)
            pool.wait_ge(wq_split, 2)
            for h in range(2, GQ):
                split_q(h, FIRST + h - 1)

            def body(kv, last):
                r = START + RP * kv
                s = FIRST + GQ - 2 + EACH * kv
                n = 0
                after = {2: ("o", 0), 3: ("kv", 0), 4: ("q", 0), 5: ("o", 1), 6: ("o", 2), 7: ("o", 3)}
                for u in range(2, NU):
                    pool.wait_ge(scored, NU * kv + u - 1)
                    rope_query(r + u - 2, u, u % 2)
                    if u == 2:
                        pool.wait_ge(wo_in, 16 * (kv + 1))
                        pool.sem_inc(gate_pool, 1)
                        pool.wait_ge(made, START + PER * kv)
                    if u == 3 and not last:
                        pool.wait_ge(wqkv_in, 32 * (kv + 2))
                    kind, h = after[u]
                    if kind == "o" or not last:
                        n += 1
                        {"o": split_o, "kv": split_kv, "q": split_q}[kind](h, s + n)
                if not last:
                    for b in range(NB):
                        pool.wait_ge(scored, NU * kv + NU - 1 + b)
                        rope_key(r + NU - 2 + 2 * b, b)
                        rope_query(r + NU - 1 + 2 * b, b, 1)
                        if b == 0:
                            split_kv(1, s + n + 1)
                    for h in range(1, GQ):
                        split_q(h, s + n + 1 + h)

            run(pool, body)

        @block.scalar
        def _(act):
            def values(kv, b):
                act.wait_ge(made, START + PER * kv + b + 1)
                act.activation(probsT[:, b, :], ps_r[(START + b) % 2][:, :], ACT.Copy).then_inc(v_taken, 1)

            def turned_values(kv, b):
                act.wait_ge(v_turned, NB * kv + b + 1)
                act.activation(V[:, b, :, :], ps_t[b][:, :].rearrange("p (t n) -> p t n", t=ST), ACT.Copy)\
                   .then_inc(v_ready, 1)

            def softmax(i, u):
                for k, t in enumerate((3, 2, 0, 1)):
                    act.wait_ge(maxed, ST * i + (3 if k == 1 else k + 1))
                    bank, at = place[t]
                    n = (t + 1) * P
                    act.activation(probs[:, u % 2, t, 0:n], ps_s[bank][:, at:at + n], ACT.Exp,
                                   bias=minus_max[:, t:t + 1], accum_out=sums[:, u % 2, t:t + 1]).then_inc(exped, 1)

            def take_turned(kv, u, k):
                act.wait_ge(turned, 3 * (NU * kv + u) + k + 1)
                n = S if k < 2 else 2 * P
                act.activation(probsT[:, k, 0:n], ps_t[(u + k) % 2][:, 0:n], ACT.Copy).then_inc(t_taken, 1)

            def take_outputs(kv, u):
                i = NU * kv + u
                act.wait_ge(pv_made, i + 1)
                act.activation(O[0][:, u % 2, u // 2, :], ps_o[:, :], ACT.Copy).then_inc(o_high, 1)

            act.sem_inc(exped, ONE)
            act.wait_ge(wqkv_in, 32)
            for parts, raw, _ in first_splits:
                act.activation(parts[0], raw, ACT.Copy).then_inc(step, 1)
            def body(kv, last):
                i = NU * kv
                softmax(i, 0)
                values(kv, 0)
                values(kv, 1)
                turned_values(kv, 0)
                turned_values(kv, 1)
                for u in range(1, NU):
                    take_turned(kv, u - 1, 0)
                    take_turned(kv, u - 1, 1)
                    softmax(i + u, u)
                    take_turned(kv, u - 1, 2)
                    take_outputs(kv, u - 1)
                for k in range(3):
                    take_turned(kv, NU - 1, k)
                take_outputs(kv, NU - 1)

            run(act, body)

        @block.vector
        def _(dve):
            def rope(n, ring, bank, keys, take, at, first=False, second=False):
                dve.wait_ge(made, ring + 1)
                if not first:
                    dve.wait_ge(summed, n)
                if not first and not second:
                    dve.wait_ge(r_low, n - 1)
                cos, sin = tables[:, 2 * keys, :], 2 * keys + 1
                ps = ps_r[bank]
                h = P // 2
                dve.tensor_tensor(by_sin[0:h, :], ps[h:P, :], tables[0:h, sin, :], ALU.mult)
                dve.tensor_tensor(by_sin[h:P, :], ps[0:h, :], tables[h:P, sin, :], ALU.mult)
                dve.tensor_tensor(roped[:, at, :], ps[:, :], cos, ALU.mult).then_inc(taken, 1)
                dve.wait_ge(taken, take + 1)
                dve.tensor_tensor(roped[:, at, :], roped[:, at, :], by_sin[:, :], ALU.add).then_inc(summed, 1)

            def maxima(i):
                for k, t in enumerate((3, 2, 0, 1)):
                    if k == 0:
                        dve.wait_ge(scored, i + 1)
                    bank, at = place[t]
                    dve.tensor_reduce(minus_max[:, t:t + 1], ps_s[bank][:, at:at + (t + 1) * P], axis=AXX, op=ALU.max,
                                      negate=True).then_inc(maxed, 1)

            def normalise(i, u):
                dve.wait_ge(exped, ONE + ST * (i + 1))
                dve.reciprocal(inverse[:, :], sums[:, u % 2, :]).then_inc(inverted, 1)
                dve.wait_ge(inverted, i + 1)
                for t in range(ST):
                    n = (t + 1) * P
                    ins = dve.tensor_scalar(probs[:, u % 2, t, 0:n], probs[:, u % 2, t, 0:n], inverse[:, t:t + 1],
                                            None, ALU.mult)
                ins.then_inc(normed, 1)

            def low_o(i, u):
                dve.wait_ge(o_high, i + 1)
                dve.tensor_tensor(O[1][:, u % 2, u // 2, :], ps_o[:, :], O[0][:, u % 2, u // 2, :], ALU.subtract)\
                   .then_inc(o_low, 1)

            dve.sem_inc(o_low, ONE)
            for k, ((hi, lo), raw, count) in enumerate(first_splits):
                dve.wait_ge(step, k + 1)
                dve.tensor_tensor(lo, raw, hi, ALU.subtract).then_inc(count, 1)
            dve.wait_ge(tables_in, 16)
            for n in range(START):
                rope(n, n, n % 2, 1 - n % 2, n, n % 2, n == 0, n == 1)

            def body(kv, last):
                r = START + RP * kv
                ring = START + PER * kv
                tk = START + TAKEN * kv
                i = NU * kv

                def add_out(j):
                    at = ring_out(last, j)
                    dve.wait_ge(made, ring + at + 1)
                    dve.tensor_tensor(X[:, j, :], ps_r[(START + at) % 2][:, :], X[:, j, :], ALU.add).then_inc(taken, 1)
                    if last:
                        dve.wait_ge(taken, tk + take_out(last, j) + 1)
                        dve.bn_stats(sb["stats"][:, j, :], X[:, j, :]).then_inc(counted, 1)

                maxima(i)
                normalise(i, 0)
                rope(r, ring + ring_query(2), (START + ring_query(2)) % 2, 0, tk, 0)
                for u in range(1, NU):
                    maxima(i + u)
                    normalise(i + u, u)
                    if u < NU - 2:
                        rope(r + u, ring + ring_query(u + 2), (START + ring_query(u + 2)) % 2, 0, tk + u, u % 2)
                        low_o(i + u - 1, u - 1)
                    else:
                        for k in range(2) if not last else ():
                            at = 2 * (u % 2) + k
                            rope(r + NU - 2 + at, ring + ring_next(at), (START + ring_next(at)) % 2, 1 - k, tk + take_next(at), k)
                        low_o(i + u - 1, u - 1)
                add_out(0)
                add_out(1)
                low_o(i + NU - 1, NU - 1)
                for j in range(2, TT):
                    add_out(j)

            run(dve, body)
            dve.wait_ge(counted, TT)

        @block.tensor
        def _(pe):
            TERMS = ((0, 0), (1, 0), (0, 1))
            x = (xh, xl)

            def project(w, sl, b, bank):
                k = 0
                for i, j in TERMS:
                    for c in range(DC):
                        last = pe.matmul(ps_r[bank][:, :], w[i][:, sl, c, :], x[j][:, c, b * S:(b + 1) * S],
                                         start=k == 0, stop=k == 3 * DC - 1)
                        k += 1
                last.then_inc(made, 1)

            def turn_values(kv, b):
                pe.wait_ge(v_taken, NB * kv + b + 1)
                for t in range(ST):
                    last = pe.transpose(ps_t[b][:, t * P:(t + 1) * P], probsT[:, b, t * P:(t + 1) * P], ident[:, :])
                last.then_inc(v_turned, 1)

            def scores(i, u, rope):
                b = u % 2
                pe.wait_ge(r_low, rope + 1)
                pe.wait_ge(exped, ONE + ST * i)
                for t in (3, 2, 0, 1):
                    bank, at = place[t]
                    n = (t + 1) * P
                    out = ps_s[bank][:, at:at + n]
                    for k, (q, kk) in enumerate(TERMS):
                        pe.matmul(out, Q[q][:, b, t * P:(t + 1) * P], K[kk][:, b, 0:n], start=k == 0, stop=False)
                    last = pe.matmul(ps_s[bank][:, at + n - P:at + n], mask[:, 0, :], mask[:, 1, :],
                                     start=False, stop=True)
                last.then_inc(scored, 1)

            def turn(i, u, k):
                if k == 0:
                    pe.wait_ge(normed, i + 1)
                if k == 2:
                    pe.wait_ge(t_taken, 3 * i + 1)
                for tile, at in pieces[k]:
                    for t in range(tile, ST):
                        last = pe.transpose(ps_t[(u + k) % 2][:, at + (t - tile) * P:at + (t - tile + 1) * P],
                                            probs[:, u % 2, t, tile * P:(tile + 1) * P], ident[:, :])
                last.then_inc(turned, 1)

            def outputs(i, u):
                b = u % 2
                pe.wait_ge(o_low, ONE + i)
                for k, piece in enumerate(pieces):
                    pe.wait_ge(t_taken, 3 * i + k + 1)
                    for tile, at in piece:
                        last = pe.matmul(ps_o[:, tile * P:S], V[:, b, tile, :], probsT[:, k, at:at + S - tile * P],
                                         start=tile == 0, stop=k == 2)
                last.then_inc(pv_made, 1)

            def merge(last, tk, j):
                at = ring_out(last, j)
                pe.wait_ge(taken, tk + take_out(last, j) - 1)
                k = 0
                for o, w in TERMS:
                    for h in range(GQ):
                        ins = pe.matmul(ps_r[(START + at) % 2][:, :],
                                        O[o][:, j // ST, h, (j % ST) * P:(j % ST + 1) * P], wo[w][:, h, :],
                                        start=k == 0, stop=k == 3 * GQ - 1)
                        k += 1
                ins.then_inc(made, 1)

            pe.wait_ge(wkv_split, 1)
            project(wkv, 0, 0, 0)
            pe.wait_ge(wq_split, 1)
            project(wq, 0, 0, 1)
            pe.wait_ge(taken, 1)
            project(wkv, 0, 1, 0)
            pe.wait_ge(taken, 2)
            project(wq, 0, 1, 1)
            pe.wait_ge(mask_set, 4)

            def body(kv, last):
                tk = START + TAKEN * kv
                r = START + RP * kv
                i = NU * kv

                def query(u):
                    pe.wait_ge(wq_split, GQ * kv + u // 2 + 1)
                    if u < 4:
                        pe.wait_ge(v_taken, 2 * kv + u - 1)
                    else:
                        pe.wait_ge(taken, tk + take_query(u) - 1)
                    project(wq, u // 2, u % 2, (START + ring_query(u)) % 2)

                scores(i, 0, r - 3)
                pe.wait_ge(wkv_split, 2 * kv + 2)
                for b in range(NB):
                    pe.wait_ge(taken, tk + b - 1)
                    project(wkv, 1, b, (START + b) % 2)
                query(2)
                for b in range(NB):
                    turn_values(kv, b)
                for u in range(1, NU):
                    scores(i + u, u, r + u - 2)
                    if u == 1:
                        pe.wait_ge(v_ready, NB * (kv + 1))
                    turn(i + u - 1, u - 1, 0)
                    turn(i + u - 1, u - 1, 1)
                    if u < NU - 2:
                        query(u + 2)
                    elif not last:
                        b = u % 2
                        pe.wait_ge(wkv_split, 2 * kv + 3)
                        pe.wait_ge(taken, tk + take_next(2 * b) - 1)
                        project(wkv, 0, b, (START + ring_next(2 * b)) % 2)
                        pe.wait_ge(wq_split, GQ * (kv + 1) + 1)
                        pe.wait_ge(taken, tk + take_next(2 * b + 1) - 1)
                        project(wq, 0, b, (START + ring_next(2 * b + 1)) % 2)
                    turn(i + u - 1, u - 1, 2)
                    outputs(i + u - 1, u - 1)
                for k in range(3):
                    turn(i + NU - 1, NU - 1, k)
                pe.wait_ge(wo_split, GQ * (kv + 1))
                pe.wait_ge(o_low, ONE + i + NU - 1)
                merge(last, tk, 0)
                merge(last, tk, 1)
                outputs(i + NU - 1, NU - 1)
                merge(last, tk, 2)
                merge(last, tk, 3)
                pe.wait_ge(o_low, ONE + i + NU)
                for j in range(ST, TT):
                    merge(last, tk, j)

            run(pe, body)


def cluster_memory(nc, own, ctx):
    m = {}
    for name, shape, dt in (("w_dense", [P, DC, D], F32), ("cent", [P, DC, NCL], F32), ("bias_sb", [1, D], F32),
                            ("assign_i", [NCL, D], mybir.dt.int32)):
        m[name] = own.enter_context(nc.sbuf_tensor(name, shape, dt))
    for name in ("cent_in", "w_in", "small_in"):
        m[name] = ctx.enter_context(nc.semaphore("cl_" + name))
    return m


def cluster_loads(sp, dram, m):
    sp.dma_start(m["cent"][:, :, :], dram["centroids"].rearrange("(c p) n -> p c n", p=P)).then_inc(m["cent_in"], 16)
    sp.dma_start(m["w_dense"][:, :, :], dram["w_dense"].rearrange("(c p) n -> p c n", p=P)).then_inc(m["w_in"], 16)
    sp.dma_start(m["assign_i"][:, :], dram["assignments"].partition_broadcast(NCL)).then_inc(m["small_in"], 16)
    sp.dma_start(m["bias_sb"][:, :], dram["bias"].rearrange("(a n) -> a n", a=1)).then_inc(m["small_in"], 16)


def cluster_stage(nc, ctx, sb, mem):
    own = ExitStack()
    with own:
        def buf(name, shape, dt=F32):
            return own.enter_context(nc.sbuf_tensor(name, shape, dt))

        def sem(name):
            return ctx.enter_context(nc.semaphore("cl_" + name))

        X, xh, xl, ident = sb["X"], sb["xh"], sb["xl"], sb["ident"]
        w, cent, bias, assign_i = (mem[name] for name in ("w_dense", "cent", "bias_sb", "assign_i"))
        wh = buf("w_dense_hi", [P, DC, D], F32R)
        wl = buf("w_dense_lo", [P, DC, D], F32R)
        ch = buf("cent_hi", [P, DC, NCL], F32R)
        cl = buf("cent_lo", [P, DC, NCL], F32R)
        ones = buf("ones_sb", [P, P])
        assign = buf("assign", [NCL, D])
        which = buf("which", [NCL, 1])
        onehot = buf("onehot", [NCL, D])
        chosen = buf("chosen", [NCL, 1])
        logits_T = buf("logits_T", [NCL, NB, S])
        bias_h = buf("bias_hi", [1, D], F32R)
        bias_l = buf("bias_lo", [1, D], F32R)
        ones_r = buf("ones_r", [1, P], F32R)
        soft = buf("soft", [P, TT, NCL])
        top = buf("top", [P, TT, 1])
        total = buf("total", [P, TT, 1])
        query = buf("query", [P, TT])
        any_hit = buf("any_hit", [P, NCL])
        column = buf("column", [P, D])
        dense = buf("dense", [P, 2, D])
        ps_l = own.enter_context(nc.psum_tensor("ps_l", [P, TT, NCL], F32))
        ps_c = own.enter_context(nc.psum_tensor("ps_c", [P, D], F32))
        ps_h = own.enter_context(nc.psum_tensor("ps_h", [P, D], F32))
        ps_d = [own.enter_context(nc.psum_tensor(f"ps_d{i}", [P, D], F32)) for i in range(4)]
        cent_in, w_in, small_in = mem["cent_in"], mem["w_in"], mem["small_in"]
        ones_set = sem("ones_set")
        which_set = sem("which_set")
        step = sem("step")
        turnable = sem("turnable")
        turn_taken = sem("turn_taken")
        bias_done = sem("bias_done")
        logits = sem("logits")
        shifted = sem("shifted")
        exped = sem("exped")
        hits_done = sem("hits_done")
        cent_done = sem("cent_done")
        w_done = sem("w_done")
        counted = sem("counted")
        onehot_done = sem("onehot_done")
        column_made = sem("column_made")
        made = sem("made")
        taken = sem("taken")
        added = sem("added")
        stats_made = sem("stats_made")
        block = own.enter_context(nc.Block())

        @block.gpsimd
        def _(pool):
            pool.memset(ones[:, :], 1.0).then_inc(ones_set, 1)
            pool.iota(which[:, :], pattern=[[0, 1]], base=0, channel_multiplier=1,
                      allow_small_or_imprecise_dtypes=True).then_inc(which_set, 1)

        @block.scalar
        def _(act):
            act.wait_ge(w_in, 16)
            act.activation(wh[:, :, :], w[:, :, :], ACT.Copy).then_inc(w_done, 1)
            for b in range(NB):
                act.wait_ge(turnable, b + 1)
                act.activation(logits_T[:, b, :], (ps_c, ps_h)[b][0:NCL, :], ACT.Copy).then_inc(turn_taken, 1)
            act.wait_ge(shifted, 1)
            act.activation(soft[:, :, :], soft[:, :, :], ACT.Exp, scale=1.0 / TEMPERATURE).then_inc(exped, 1)

        @block.vector
        def _(dve):
            n = [0]

            def after(ins):
                n[0] += 1
                ins.then_inc(step, 1)
                dve.wait_ge(step, n[0])

            dve.wait_ge(cent_in, 16)
            after(dve.tensor_copy(ch[:, :, :], cent[:, :, :]))
            dve.tensor_tensor(cl[:, :, :], cent[:, :, :], ch[:, :, :], ALU.subtract).then_inc(cent_done, 1)
            dve.wait_ge(w_done, 1)
            dve.tensor_tensor(wl[:, :, :], w[:, :, :], wh[:, :, :], ALU.subtract).then_inc(w_done, 1)
            dve.wait_ge(small_in, 32)
            after(dve.tensor_copy(assign[:, :], assign_i[:, :]))
            after(dve.tensor_copy(bias_h[:, :], bias[:, :]))
            dve.tensor_tensor(bias_l[:, :], bias[:, :], bias_h[:, :], ALU.subtract).then_inc(bias_done, 1)
            dve.wait_ge(ones_set, 1)
            dve.tensor_copy(ones_r[:, :], ones[0:1, :]).then_inc(bias_done, 1)
            dve.wait_ge(logits, 1)
            after(dve.tensor_reduce(top[:, :, 0], ps_l[:, :, :], axis=AXX, op=ALU.max))
            dve.tensor_tensor(soft[:, :, :], ps_l[:, :, :], top[:, :, :].broadcast_to([P, TT, NCL]),
                              ALU.subtract).then_inc(shifted, 1)
            dve.wait_ge(exped, 1)
            after(dve.tensor_reduce(total[:, :, 0], soft[:, :, :], axis=AXX, op=ALU.add))
            after(dve.reciprocal(total[:, :, 0], total[:, :, 0]))
            after(dve.tensor_tensor(soft[:, :, :], soft[:, :, :], total[:, :, :].broadcast_to([P, TT, NCL]), ALU.mult))
            after(dve.tensor_scalar(soft[:, :, :], soft[:, :, :], THRESHOLD, None, ALU.is_gt))
            dve.tensor_reduce(query[:, :], soft[:, :, :], axis=AXX, op=ALU.max)
            dve.tensor_reduce(any_hit[:, :], soft[:, :, :].rearrange("p t n -> p n t"), axis=AXX, op=ALU.max)\
               .then_inc(hits_done, 1)
            dve.wait_ge(counted, 1)
            after(dve.tensor_scalar(chosen[:, :], ps_c[0:NCL, 0:1], 0.5, None, ALU.is_gt))
            dve.wait_ge(which_set, 1)
            dve.tensor_scalar(onehot[:, :], assign[:, :], which[:, 0:1], chosen[:, 0:1], ALU.is_equal, ALU.mult)\
               .then_inc(onehot_done, 1)
            dve.wait_ge(column_made, 1)
            after(dve.tensor_copy(column[:, :], ps_h[:, :]))
            for t in range(TT):
                dve.wait_ge(made, t + 1)
                dve.scalar_tensor_tensor(out=dense[:, t % 2, :], in0=ps_d[t % 4][:, :], scalar=query[:, t:t + 1],
                                         in1=column[:, :], op0=ALU.mult, op1=ALU.mult).then_inc(taken, 1)
                dve.wait_ge(taken, t + 1)
                dve.tensor_tensor(X[:, t, :], X[:, t, :], dense[:, t % 2, :], ALU.add).then_inc(added, 1)
                dve.wait_ge(added, t + 1)
                dve.bn_stats(sb["stats"][:, t, :], X[:, t, :]).then_inc(stats_made, 1)
            dve.wait_ge(stats_made, TT)

        @block.tensor
        def _(pe):
            TERMS = ((0, 0), (1, 0), (0, 1))
            x = (xh, xl)

            pe.wait_ge(cent_done, 1)
            for b in range(NB):
                k = 0
                for i, j in TERMS:
                    for c in range(DC):
                        last = pe.matmul((ps_c, ps_h)[b][0:NCL, :], (ch, cl)[j][:, c, :], x[i][:, c, b * S:(b + 1) * S],
                                         start=k == 0, stop=k == 3 * DC - 1)
                        k += 1
                last.then_inc(turnable, 1)
            for b in range(NB):
                pe.wait_ge(turn_taken, b + 1)
                for t in range(ST):
                    last = pe.transpose(ps_l[:, b * ST + t, :], logits_T[:, b, t * P:(t + 1) * P],
                                        ident[0:NCL, 0:NCL])
            last.then_inc(logits, 1)
            pe.wait_ge(w_done, 2)
            pe.wait_ge(bias_done, 2)

            def dense_tile(t):
                if t >= 4:
                    pe.wait_ge(taken, t - 3)
                for k, part in enumerate((bias_h, bias_l)):
                    pe.matmul(ps_d[t % 4][:, :], ones_r[:, :], part[:, :], start=k == 0, stop=False)
                k = 0
                for i, j in TERMS:
                    for c in range(DC):
                        last = pe.matmul(ps_d[t % 4][:, :], x[i][:, c, t * P:(t + 1) * P], (wh, wl)[j][:, c, :],
                                         start=False, stop=k == 3 * DC - 1)
                        k += 1
                last.then_inc(made, 1)

            for t in range(2):
                dense_tile(t)
            pe.wait_ge(hits_done, 1)
            pe.matmul(ps_c[0:NCL, 0:1], any_hit[:, :], ones[:, 0:1], start=True, stop=True).then_inc(counted, 1)
            dense_tile(2)
            pe.wait_ge(onehot_done, 1)
            pe.matmul(ps_h[:, :], ones[0:NCL, :], onehot[:, :], start=True, stop=True).then_inc(column_made, 1)
            for t in range(3, TT):
                dense_tile(t)


def program(nc, dram, out):
    for name in ("content_q", "content_k"):
        dram[name] = nc.dram_tensor(name, (NH0, PARTS * HD0, T), F32, kind="Internal").ap()
    with ExitStack() as ctx:
        def keep(stack, name, shape, dt=F32):
            sb[name] = stack.enter_context(nc.sbuf_tensor(name, shape, dt))

        sb = {}
        keep(ctx, "ident", [P, P])
        keep(ctx, "X", [P, TT, D])
        keep(ctx, "xh", [P, DC, T], F32R)
        keep(ctx, "xl", [P, DC, T], F32R)
        keep(ctx, "stats", [P, TT, 6])
        with ExitStack() as layer:
            for name in ("Q1", "Q2", "K2", "KX"):
                keep(layer, name, [P, NB, GH, S], F32R)
            keep(layer, "K1", [P, NB, S], F32R)
            keep(layer, "V", [P, TT, D])
            keep(layer, "V_slot", [P, NB, ST, GH, 32])
            keep(layer, "mrow", [GH, S], F32R)
            latent_stage(nc, ctx, dram, sb)
            mla_stage(nc, ctx, dram, sb)
        merge_heads_stage(nc, ctx, dram, sb)
        with ExitStack() as own:
            mem = swiglu_memory(nc, own, ctx)
            norm_stage(nc, ctx, "n1_", sb, ahead=lambda sp: swiglu_first_loads(sp, dram, mem))
            swiglu_stage(nc, ctx, dram, sb, mem)
        with ExitStack() as own:
            mem = gqa_memory(nc, own, ctx)
            norm_stage(nc, ctx, "n2_", sb, ahead=lambda sp: gqa_first_loads(sp, dram, mem))
            gqa_stage(nc, ctx, dram, sb, mem)
        with ExitStack() as own:
            mem = cluster_memory(nc, own, ctx)
            norm_stage(nc, ctx, "n3_", sb, ahead=lambda sp: cluster_loads(sp, dram, mem))
            cluster_stage(nc, ctx, sb, mem)
        norm_stage(nc, ctx, "n4_", sb, out)


def layouts(i):
    import numpy as np

    def cat(names, axis):
        return np.concatenate([i[n] for n in names], axis)

    def pad(a, axis):
        width = [(0, 0)] * a.ndim
        width[axis] = (0, HP - HID)
        return np.pad(a, width)

    def slots(a, axis):
        width = [(0, 0)] * a.ndim
        width[axis] = (0, 32 - a.shape[axis])
        return np.concatenate([np.pad(a, width)] * 3, axis)

    def by_key_head(w, heads):
        return w.reshape(DC, P, NKV, heads, P).transpose(2, 1, 3, 0, 4)

    x = i["L0_attn_x"].reshape(T, D)
    inv_freq = (1.0 / 10000.0 ** (np.arange(0, P, 2, dtype=np.float32) / np.float32(P))).astype(np.float32)
    angle = np.outer(inv_freq, np.arange(S, dtype=np.float32)).astype(np.float32)
    cos = np.concatenate([np.cos(angle)] * 2, 0).astype(np.float32)
    sin = np.concatenate([-np.sin(angle), np.sin(angle)], 0).astype(np.float32)
    scale = np.float32(P) ** np.float32(-0.5)
    return {
        "x": x,
        "xT": x.T,
        "w_down": cat(["L0_attn_Wq_down", "L0_attn_Wkv_down"], 1),
        "w_krope": cat(["L0_attn_Wk_rope", "L0_attn_Wk_rope"], 1),
        "w_qup": i["L0_attn_Wq_up"],
        "w_kvup": cat(["L0_attn_Wk_up", "L0_attn_Wv_up"], 1),
        "w_qrope": i["L0_attn_Wq_rope"],
        "wo0": i["L0_attn_Wo"],
        "w13": pad(np.stack([i["L0_ffn_w1"].T, i["L0_ffn_w3"].T]), 2),
        "w2": pad(i["L0_ffn_w2"].T, 0),
        "lora_a13": slots(np.stack([i["L0_ffn_lora_A1"], i["L0_ffn_lora_A3"]]), 1),
        "lora_b13": slots(pad(np.stack([i["L0_ffn_lora_B1"].T, i["L0_ffn_lora_B3"].T]), 2), 1),
        "lora_a2": slots(pad(i["L0_ffn_lora_A2"], 1), 0),
        "lora_b2": slots(i["L0_ffn_lora_B2"].T, 0),
        "wq1": by_key_head(i["L1_attn_Wq"], GQ),
        "wkv1": np.concatenate([by_key_head(i["L1_attn_Wk"], 1), by_key_head(i["L1_attn_Wv"], 1)], 2),
        "wo1": i["L1_attn_Wo"].reshape(NKV, GQ, P, D).transpose(0, 2, 1, 3),
        "tables": np.stack([cos * scale, sin * scale, cos, sin]).astype(np.float32),
        "w_dense": i["L1_ffn_weight"].T,
        "bias": i["L1_ffn_bias"],
        "centroids": i["L1_ffn_centroids"].T,
        "assignments": i["L1_ffn_assignments"],
    }


def kernel(**inputs):
    import numpy as np
    import concourse.bacc as bacc
    from concourse.bass_utils import run_bass_kernel_spmd

    arrays = {"in_" + n: np.ascontiguousarray(a) for n, a in layouts({n: np.asarray(a) for n, a in inputs.items()}).items()}
    nc = bacc.Bacc("TRN2", target_bir_lowering=False, num_devices=1)
    dram = {n[3:]: nc.dram_tensor(n, a.shape, mybir.dt.from_np(a.dtype), kind="ExternalInput").ap()
            for n, a in arrays.items()}
    out = nc.dram_tensor("out", (T, D), F32, kind="ExternalOutput").ap()
    program(nc, dram, out)
    r = run_bass_kernel_spmd(nc, [arrays], core_ids=[0])
    return r.results[0]["out"].reshape(NB, S, D)
```
